# Optimizing a Trainium2 kernel written in Bass

```python
import numpy as np
import jax
import jax.numpy as jnp

def _softmax(x, axis=-1):
    return jax.nn.softmax(x, axis=axis)

def _gelu(x):
    return jax.nn.gelu(x, approximate=True)

def _silu(x):
    return jax.nn.silu(x)

def _sigmoid(x):
    return jax.nn.sigmoid(x)

def _layernorm(x, axis=-1, eps=1e-05):
    m = jnp.mean(x, axis=axis, keepdims=True)
    v = jnp.var(x, axis=axis, keepdims=True)
    return (x - m) / jnp.sqrt(v + eps)

def _scatter_add(tgt, idx, src, axis=0):
    return tgt.at[idx].add(src)

def _segment_sum(src, seg, n):
    return jax.ops.segment_sum(src, seg, n)
kernel_name = 'mk_xattn_ffn_d2_seqx_r4_652967'

def setup_inputs(seed: int=0):
    np.random.seed(seed)
    _w = jnp.asarray

    def _rec_inputs():
        import jax
        import jax.numpy as jnp
        _rk = jax.random.key(seed)
        x = -0.0002928 + 1 * jax.random.normal(jax.random.fold_in(_rk, 1), (2, 1024, 256), jnp.float32)
        _lenS = 1024 - jax.random.randint(jax.random.fold_in(_rk, 7), (2,), 0, max(1, 1024 // 4) + 1, jnp.int32)
        _lenS2 = 154 - jax.random.randint(jax.random.fold_in(_rk, 8), (2,), 0, max(1, 154 // 4) + 1, jnp.int32)
        _ctx_1024P = jax.random.normal(jax.random.fold_in(_rk, 11), (2, 16, 256), jnp.float32)
        _ctx_1024c = jax.random.dirichlet(jax.random.fold_in(_rk, 511), 0.3 * jnp.ones((16,), jnp.float32), (2, 154))
        _ctx_1024t = jnp.einsum('bsk,bkd->bsd', _ctx_1024c, _ctx_1024P)
        _ctx_1024t = _ctx_1024t * jax.lax.rsqrt(jnp.mean(jnp.square(_ctx_1024t)) + 1e-12) * 0.953939
        ctx_1024 = -0.000191848 + 0.999787 * (_ctx_1024t + 0.3 * jax.random.normal(jax.random.fold_in(_rk, 611), (2, 154, 256), jnp.float32))
        return (x, ctx_1024)
    x, ctx_1024 = _rec_inputs()

    def _L0_xattn_setup():
        import jax, jax.numpy as jnp
        import numpy as np
        D_MODEL = 256
        NUM_HEADS = 16
        DEPTH = D_MODEL // NUM_HEADS
        key = jax.random.key(seed)
        ks = jax.random.split(key, 10)
        B, T, C = (2, 512, 768)
        s = 1.0 / np.sqrt(D_MODEL)
        inp = {'x': jax.random.normal(ks[0], (B, T, D_MODEL), dtype=jnp.float32), 'context': jax.random.normal(ks[1], (B, C, D_MODEL), dtype=jnp.float32), 'Wq': jax.random.normal(ks[2], (D_MODEL, D_MODEL), dtype=jnp.float32) * s, 'bq': jnp.zeros((D_MODEL,), dtype=jnp.float32), 'Wk': jax.random.normal(ks[3], (D_MODEL, D_MODEL), dtype=jnp.float32) * s, 'bk': jnp.zeros((D_MODEL,), dtype=jnp.float32), 'Wv': jax.random.normal(ks[4], (D_MODEL, D_MODEL), dtype=jnp.float32) * s, 'bv': jnp.zeros((D_MODEL,), dtype=jnp.float32), 'Wo': jax.random.normal(ks[5], (D_MODEL, D_MODEL), dtype=jnp.float32) * s, 'bo': jnp.zeros((D_MODEL,), dtype=jnp.float32)}
        return inp
    _L0_xattn_all = _L0_xattn_setup()
    _L0_xattn_in = {k: v for k, v in _L0_xattn_all.items() if k in ('Wq', 'bq', 'Wk', 'bk', 'Wv', 'bv', 'Wo', 'bo')}
    del _L0_xattn_all

    def _L0_ffn_setup():
        import jax, jax.numpy as jnp
        import numpy as np
        TOP_K = 2
        ROUTE_SCALE = 1.0
        EPS = 1e-20
        key = jax.random.key(seed)
        ks = jax.random.split(key, 8)
        dim, hid, E, X = (256, 704, 8, 1)
        std = 0.02
        x = jax.random.normal(ks[0], (2, 512, dim), dtype=jnp.float32)
        w1 = jax.random.normal(ks[1], (E, hid, dim), dtype=jnp.float32) * std
        w2 = jax.random.normal(ks[2], (E, dim, hid), dtype=jnp.float32) * std
        w3 = jax.random.normal(ks[3], (E, hid, dim), dtype=jnp.float32) * std
        new_w1 = jax.random.normal(ks[4], (X, hid, dim), dtype=jnp.float32) * std
        new_w2 = jnp.zeros((X, dim, hid), dtype=jnp.float32)
        new_w3 = jax.random.normal(ks[5], (X, hid, dim), dtype=jnp.float32) * std
        gate_weight = jax.random.normal(ks[6], (E, dim), dtype=jnp.float32) * std
        new_gate_weight = jax.random.normal(ks[7], (X, dim), dtype=jnp.float32) * std
        gate_bias = jnp.zeros((X,), dtype=jnp.float32)
        return dict(x=x, w1=w1, w2=w2, w3=w3, new_w1=new_w1, new_w2=new_w2, new_w3=new_w3, gate_weight=gate_weight, new_gate_weight=new_gate_weight, gate_bias=gate_bias)
    _L0_ffn_all = _L0_ffn_setup()
    _L0_ffn_in = {k: v for k, v in _L0_ffn_all.items() if k in ('w1', 'w2', 'w3', 'new_w1', 'new_w2', 'new_w3', 'gate_weight', 'new_gate_weight', 'gate_bias')}
    del _L0_ffn_all

    def _L1_xattn_setup():
        import jax, jax.numpy as jnp
        import numpy as np
        import math
        D_MODEL = 256
        N_HEADS = 16
        key = jax.random.key(seed)
        ks = jax.random.split(key, 11)
        N, L, S = (2, 512, 512)
        d = D_MODEL
        s = 1.0 / math.sqrt(d)
        return {'queries': jax.random.normal(ks[0], (N, L, d), dtype=jnp.float32), 'keys': jax.random.normal(ks[1], (N, S, d), dtype=jnp.float32), 'values': jax.random.normal(ks[2], (N, S, d), dtype=jnp.float32), 'Wq': jax.random.normal(ks[3], (d, d), dtype=jnp.float32) * s, 'bq': jax.random.normal(ks[4], (d,), dtype=jnp.float32) * s, 'Wk': jax.random.normal(ks[5], (d, d), dtype=jnp.float32) * s, 'bk': jax.random.normal(ks[6], (d,), dtype=jnp.float32) * s, 'Wv': jax.random.normal(ks[7], (d, d), dtype=jnp.float32) * s, 'bv': jax.random.normal(ks[8], (d,), dtype=jnp.float32) * s, 'Wo': jax.random.normal(ks[9], (d, d), dtype=jnp.float32) * s, 'bo': jax.random.normal(ks[10], (d,), dtype=jnp.float32) * s}
    _L1_xattn_all = _L1_xattn_setup()
    _L1_xattn_in = {k: v for k, v in _L1_xattn_all.items() if k in ('Wq', 'bq', 'Wk', 'bk', 'Wv', 'bv', 'Wo', 'bo')}
    del _L1_xattn_all

    def _L1_ffn_setup():
        import jax, jax.numpy as jnp
        import numpy as np
        SL, BS, HS, FF, E, TOPK = (512, 2, 256, 1024, 8, 2)
        key = jax.random.key(seed)
        ks = jax.random.split(key, 6)
        T = SL * BS
        x = jax.random.normal(ks[0], (SL, BS, HS), jnp.float32)
        scores = jax.random.uniform(ks[1], (T, E), jnp.float32)
        expert_weights = jax.random.uniform(ks[2], (T, TOPK), jnp.float32)
        expert_indices = jax.random.randint(ks[3], (T, TOPK), 0, E, jnp.int32)
        w1 = jax.random.normal(ks[4], (E, HS, FF), jnp.float32) * (1.0 / np.sqrt(HS))
        w2 = jax.random.normal(ks[5], (E, FF, HS), jnp.float32) * (1.0 / np.sqrt(FF))
        bias = jnp.zeros((HS,), jnp.float32)
        return dict(x=x, scores=scores, expert_weights=expert_weights, expert_indices=expert_indices, w1=w1, w2=w2, bias=bias)
    _L1_ffn_all = _L1_ffn_setup()
    _L1_ffn_in = {k: v for k, v in _L1_ffn_all.items() if k in ('scores', 'expert_weights', 'expert_indices', 'w1', 'w2', 'bias')}
    del _L1_ffn_all
    return {'x': x, 'ctx_1024': ctx_1024, 'L0_xattn_Wq': _L0_xattn_in['Wq'], 'L0_xattn_bq': _L0_xattn_in['bq'], 'L0_xattn_Wk': _L0_xattn_in['Wk'], 'L0_xattn_bk': _L0_xattn_in['bk'], 'L0_xattn_Wv': _L0_xattn_in['Wv'], 'L0_xattn_bv': _L0_xattn_in['bv'], 'L0_xattn_Wo': _L0_xattn_in['Wo'], 'L0_xattn_bo': _L0_xattn_in['bo'], 'L0_ffn_w1': _L0_ffn_in['w1'], 'L0_ffn_w2': _L0_ffn_in['w2'], 'L0_ffn_w3': _L0_ffn_in['w3'], 'L0_ffn_new_w1': _L0_ffn_in['new_w1'], 'L0_ffn_new_w2': _L0_ffn_in['new_w2'], 'L0_ffn_new_w3': _L0_ffn_in['new_w3'], 'L0_ffn_gate_weight': _L0_ffn_in['gate_weight'], 'L0_ffn_new_gate_weight': _L0_ffn_in['new_gate_weight'], 'L0_ffn_gate_bias': _L0_ffn_in['gate_bias'], 'L1_xattn_Wq': _L1_xattn_in['Wq'], 'L1_xattn_bq': _L1_xattn_in['bq'], 'L1_xattn_Wk': _L1_xattn_in['Wk'], 'L1_xattn_bk': _L1_xattn_in['bk'], 'L1_xattn_Wv': _L1_xattn_in['Wv'], 'L1_xattn_bv': _L1_xattn_in['bv'], 'L1_xattn_Wo': _L1_xattn_in['Wo'], 'L1_xattn_bo': _L1_xattn_in['bo'], 'L1_ffn_scores': _L1_ffn_in['scores'], 'L1_ffn_expert_weights': _L1_ffn_in['expert_weights'], 'L1_ffn_expert_indices': _L1_ffn_in['expert_indices'], 'L1_ffn_w1': _L1_ffn_in['w1'], 'L1_ffn_w2': _L1_ffn_in['w2'], 'L1_ffn_bias': _L1_ffn_in['bias']}

def reference(x, ctx_1024, L0_xattn_Wq, L0_xattn_bq, L0_xattn_Wk, L0_xattn_bk, L0_xattn_Wv, L0_xattn_bv, L0_xattn_Wo, L0_xattn_bo, L0_ffn_w1, L0_ffn_w2, L0_ffn_w3, L0_ffn_new_w1, L0_ffn_new_w2, L0_ffn_new_w3, L0_ffn_gate_weight, L0_ffn_new_gate_weight, L0_ffn_gate_bias, L1_xattn_Wq, L1_xattn_bq, L1_xattn_Wk, L1_xattn_bk, L1_xattn_Wv, L1_xattn_bv, L1_xattn_Wo, L1_xattn_bo, L1_ffn_scores, L1_ffn_expert_weights, L1_ffn_expert_indices, L1_ffn_w1, L1_ffn_w2, L1_ffn_bias):
    import jax
    import jax.numpy as jnp

    def _L0_xattn_ref(x, context, Wq, bq, Wk, bk, Wv, bv, Wo, bo):
        import jax, jax.numpy as jnp
        import numpy as np
        D_MODEL = 256
        NUM_HEADS = 16
        DEPTH = D_MODEL // NUM_HEADS
        B, T, D = x.shape
        C = context.shape[1]
        H, d = (NUM_HEADS, DEPTH)
        q = x @ Wq.T + bq
        k = context @ Wk.T + bk
        v = context @ Wv.T + bv
        q = q.reshape(B, T, H, d).transpose(0, 2, 1, 3)
        k = k.reshape(B, C, H, d).transpose(0, 2, 1, 3)
        v = v.reshape(B, C, H, d).transpose(0, 2, 1, 3)
        scores = jnp.einsum('bhtd,bhcd->bhtc', q, k) / jnp.sqrt(jnp.asarray(d, x.dtype))
        attn = jax.nn.softmax(scores, axis=-1)
        out = jnp.einsum('bhtc,bhcd->bhtd', attn, v)
        out = out.transpose(0, 2, 1, 3).reshape(B, T, D)
        return out @ Wo.T + bo

    def _L0_ffn_ref(x, w1, w2, w3, new_w1, new_w2, new_w3, gate_weight, new_gate_weight, gate_bias):
        import jax, jax.numpy as jnp
        import numpy as np
        TOP_K = 2
        ROUTE_SCALE = 1.0
        EPS = 1e-20
        bs, slen, dim = x.shape
        x_flat = x.reshape(-1, dim)
        ew1 = jnp.concatenate([w1, new_w1], axis=0)
        ew2 = jnp.concatenate([w2, new_w2], axis=0)
        ew3 = jnp.concatenate([w3, new_w3], axis=0)
        gate = jnp.concatenate([gate_weight, new_gate_weight], axis=0)
        e_orig = w1.shape[0]
        e_tot = gate.shape[0]
        bias = jnp.concatenate([jnp.zeros((e_orig,), x.dtype), gate_bias])
        scores = jax.nn.sigmoid((x_flat @ gate.T + bias).astype(jnp.float32))
        top_scores, selected = jax.lax.top_k(scores, TOP_K)
        top_scores = top_scores / (jnp.sum(top_scores, axis=-1, keepdims=True) + EPS)
        top_scores = top_scores * ROUTE_SCALE
        onehot = jax.nn.one_hot(selected, e_tot, dtype=jnp.float32)
        cw = jnp.einsum('tk,tke->te', top_scores, onehot)
        out = jnp.zeros_like(x_flat)
        for e in range(e_tot):
            h = jax.nn.silu(x_flat @ ew1[e].T) * (x_flat @ ew3[e].T)
            out = out + cw[:, e:e + 1] * (h @ ew2[e].T)
        return out.reshape(bs, slen, dim)

    def _L1_xattn_ref(queries, keys, values, Wq, bq, Wk, bk, Wv, bv, Wo, bo):
        import jax, jax.numpy as jnp
        import numpy as np
        import math
        D_MODEL = 256
        N_HEADS = 16
        N, L, _ = queries.shape
        S = keys.shape[1]
        H = N_HEADS
        q = (queries @ Wq.T + bq).reshape(N, L, H, -1)
        k = (keys @ Wk.T + bk).reshape(N, S, H, -1)
        v = (values @ Wv.T + bv).reshape(N, S, H, -1)
        D = k.shape[-1]
        sm = jnp.einsum('nlhd,nshd->nlhs', q, k) / math.sqrt(D)
        causal_mask = jnp.triu(jnp.ones((L, S), dtype=bool), k=1)
        sm = jnp.where(causal_mask[None, :, None, :], -jnp.inf, sm)
        sm = jax.nn.softmax(sm, axis=-1)
        attn = jnp.einsum('nlhs,nshd->nlhd', sm, v)
        new_values = attn.reshape(N, L, H * D)
        return new_values @ Wo.T + bo

    def _L1_ffn_ref(x, scores, expert_weights, expert_indices, w1, w2, bias):
        import jax, jax.numpy as jnp
        import numpy as np
        SL, BS, HS, FF, E, TOPK = (512, 2, 256, 1024, 8, 2)
        sl, bs, hs = x.shape
        n_exp = w1.shape[0]
        top_k = expert_indices.shape[-1]
        xf = x.reshape(-1, hs)
        flat_idx = expert_indices.reshape(-1)
        flat_w = expert_weights.reshape(-1)
        order = jnp.argsort(flat_idx)
        tok = order // top_k
        tokens_per_expert = jnp.bincount(flat_idx, length=n_exp).astype(jnp.int32)
        xs = xf[tok]
        h = jax.nn.gelu(jax.lax.ragged_dot(xs, w1, tokens_per_expert), approximate=False)
        ys = jax.lax.ragged_dot(h, w2, tokens_per_expert)
        ys = ys * flat_w[order][:, None]
        out = jnp.zeros_like(xf).at[tok].add(ys)
        return out.reshape(sl, bs, hs) + bias
    x = x + _L0_xattn_ref(_layernorm(x, axis=-1), ctx_1024, L0_xattn_Wq, L0_xattn_bq, L0_xattn_Wk, L0_xattn_bk, L0_xattn_Wv, L0_xattn_bv, L0_xattn_Wo, L0_xattn_bo)
    x = x + _L0_ffn_ref(_layernorm(x, axis=-1), L0_ffn_w1, L0_ffn_w2, L0_ffn_w3, L0_ffn_new_w1, L0_ffn_new_w2, L0_ffn_new_w3, L0_ffn_gate_weight, L0_ffn_new_gate_weight, L0_ffn_gate_bias)
    x = x + _L1_xattn_ref(_layernorm(x, axis=-1), ctx_1024, ctx_1024, L1_xattn_Wq, L1_xattn_bq, L1_xattn_Wk, L1_xattn_bk, L1_xattn_Wv, L1_xattn_bv, L1_xattn_Wo, L1_xattn_bo)
    x = x + _L1_ffn_ref(_layernorm(x, axis=-1), L1_ffn_scores, L1_ffn_expert_weights, L1_ffn_expert_indices, L1_ffn_w1, L1_ffn_w2, L1_ffn_bias)
    return x

_drawn_inputs = setup_inputs


def setup_inputs(seed=0):
    import zlib

    import numpy as np

    out = dict(_drawn_inputs(seed))
    spreads = {'L0_xattn_bq': (0.0, 0.365),
     'L0_xattn_bk': (0.0, 2.0),
     'L0_xattn_bv': (0.0, 0.1),
     'L0_xattn_bo': (0.0, 0.1),
     'L0_ffn_new_w2': (0.0, 0.325),
     'L1_ffn_bias': (0.0, 0.1)}
    factors = {'L0_ffn_w1': 3.968,
     'L0_ffn_w2': 3.807,
     'L0_ffn_w3': 3.791,
     'L1_xattn_bq': 4.994,
     'L1_xattn_bk': 64.0}
    for name, (base, spread) in spreads.items():
        noise = np.random.default_rng([zlib.crc32(name.encode()), seed]).standard_normal(out[name].shape)
        drawn = base * np.exp(spread * noise) if base else spread * noise
        out[name] = jnp.asarray(drawn.astype(out[name].dtype))
    for name, factor in factors.items():
        out[name] = (out[name] * factor).astype(out[name].dtype)
    return out
```

```python
from contextlib import ExitStack

import concourse.bass as bass
from concourse import mybir

F32 = mybir.dt.float32
I32 = mybir.dt.int32
U32 = mybir.dt.uint32
ALU = mybir.AluOpType
ACT = mybir.ActivationFunctionType
AX = mybir.AxisListType

P = 128
D = 256
KC = D // P
NB = 2
SEQ = 1024
NT = NB * SEQ // P
TB = SEQ // P
H = 16
DH = D // H
C = 154
CL = C - P
HL = 4
NQ = H // HL
SCALE = DH ** -0.5
EPS = 1e-5
NEG = -1.0e30
STEPS = [(0, 3), (3, 3), (6, 2), (8, 3), (11, 3), (14, 2)]
NS = len(STEPS)
SB = 3
HH = H // 2

E0, F0 = 9, 704
E1, F1 = 8, 1024
K0 = (F0 + P - 1) // P
K1 = F1 // P
HALF0 = F0 // 2
T1 = 1024 // P
PAIRS = [2 * NT * P, 2 * T1 * P]


def even(n):
    return n + n % 2


MT = [even((PAIRS[0] + E0 * (P - 1)) // P), even((PAIRS[1] + E1 * (P - 1)) // P)]
EXP = [E0, E1]
REG = 2048 + P

W13 = 2 * KC * F0
W2 = K0 * D
U1 = KC * F1
U2 = K1 * D
ARENA = E0 * (W13 + W2)
KBLK = NB * 2 * HH * C
VM = NB * H * (DH + 1)
ATT = ARENA - (KBLK + H * C + (H + HL) * P + 7 * D + VM + KC * NB * (C + HL * CL) + H * CL)
EARLY1 = (ATT - E1 * U1) // U2
PACK = 4 * KC * D + 2 * KC + 2 * D


def program(nc, x, ctxt, pack0, pack1, w13, w2, gate, gbias, u1, u2, eidx, ewts, fbias, out):
    with ExitStack() as ctx:
        def sb(name, shape, dt=F32):
            return ctx.enter_context(nc.sbuf_tensor(name, shape, dt))

        def sem(name):
            return ctx.enter_context(nc.semaphore(name))

        xs = [nc.dram_tensor(f"rows{L}", (EXP[L] * REG, D), F32).ap() for L in (0, 1)]
        ys = [nc.dram_tensor(f"ffn{L}", (MT[L] * P, D), F32).ap() for L in (0, 1)]

        arena = sb("arena", [P, ARENA])
        o = ATT
        kblk = arena[:, o:o + KBLK].rearrange("p (b s h c) -> p b s h c", b=NB, s=2, h=HH)
        o += KBLK
        probs = arena[:, o:o + H * C].rearrange("p (h c) -> p h c", h=H)
        o += H * C
        probsT = arena[:, o:o + (H + HL) * P].rearrange("p (g n) -> p g n", n=HL * P)
        o += (H + HL) * P
        xn, xnT, qT, on, oT, x2T, vtmp = (arena[:, o + n * D:o + (n + 1) * D] for n in range(7))
        xnT, qT, oT, x2T = (t.rearrange("p (k n) -> p k n", k=KC) for t in (xnT, qT, oT, x2T))
        o += 7 * D
        vm = arena[:, o:o + VM].rearrange("p (b h d) -> p b h d", b=NB, h=H)
        o += VM
        cT = arena[:, o:o + KC * NB * C].rearrange("p (k n) -> p k n", k=KC)
        o += KC * NB * C
        cTrep = arena[:, o:o + KC * NB * HL * CL].rearrange("p (k b h c) -> p k b h c", k=KC, b=NB, h=HL)
        o += KC * NB * HL * CL
        last = arena[:, o:o + H * CL].rearrange("p (h c) -> p h c", h=H)
        X = sb("X", [P, NT, D])
        pack = sb("pack", [P, PACK])
        wq, wk, wv, wo = (pack[:, n * KC * D:(n + 1) * KC * D].rearrange("p (k n) -> p k n", k=KC) for n in range(4))
        bq = pack[:, 4 * KC * D:4 * KC * D + KC]
        bk = pack[:, 4 * KC * D + KC:4 * KC * D + 2 * KC]
        bv = pack[:, PACK - 2 * D:PACK - D]
        bo = pack[:, PACK - D:PACK]
        vl = sb("vl", [P, NB, NQ, HL, DH + 1])
        m16 = sb("m16", [P, HH])
        m26 = sb("m26", [P, HL])
        ident = sb("ident", [P, P])
        ustrict = sb("ustrict", [P, P])
        ones = sb("ones", [P, P])
        iota = sb("iota", [P, 64])
        causal = sb("causal", [P, 2 * P + C])
        mhalf = sb("mhalf", [P, 1])
        stats = sb("stats", [P, 6])
        mv = sb("mv", [P, 2])
        ve = sb("ve", [P, 1])
        rstd = sb("rstd", [P, 1])
        stats2 = sb("stats2", [P, 6])
        mv2 = sb("mv2", [P, 2])
        ve2 = sb("ve2", [P, 1])
        rstd2 = sb("rstd2", [P, 1])
        hmax = sb("hmax", [P, H])
        rden = sb("rden", [P, H])
        xn2 = sb("xn2", [P, D])
        gw = sb("gw", [P, KC, E0])
        gb = sb("gb", [P, E0])
        fb = sb("fb", [P, D])
        z = sb("z", [P, E0])
        mx = sb("mx", [P, 8])
        ix = sb("ix", [P, 8], U32)
        mxs = sb("mxs", [P, NT, 2])
        ixf = sb("ixf", [P, 2])
        oh = [sb("oh0", [P, NT, 2, E0]), sb("oh1", [P, T1, 2, E1])]
        both = sb("both", [P, E0])
        both1 = sb("both1", [P, T1, E1])
        cum = sb("cum", [P, E0])
        cum1 = sb("cum1", [P, T1 + 1, E1])
        sel = sb("sel", [P, 2, E0])
        rank = [sb("rank0", [P, NT, 2]), sb("rank1", [P, T1, 2])]
        posf = sb("posf", [P, 2])
        idx = sb("idx", [P, 2], I32)
        pos1f = sb("pos1f", [P, T1, 2])
        pos1 = sb("pos1", [P, T1, 2], I32)
        ypf = sb("ypf", [P, NT, 2])
        yp = [sb("yp0", [P, NT, 2], I32), sb("yp1", [P, T1, 2], I32)]
        gidx = sb("gidx", [P, 2], I32)
        wts = [sb("wts0", [P, NT, 2]), sb("wts1", [P, T1, 2])]
        wsum = sb("wsum", [P, NT])
        ei = sb("ei", [P, T1, 2], I32)
        eif = sb("eif", [P, T1, 2])
        pref = sb("pref", [P, T1, E1])
        cnti = sb("cnti", [P, E0], I32)
        ntf = sb("ntf", [P, E0])
        incl = sb("incl", [P, E0])
        excl = sb("excl", [P, E0])
        padf = sb("padf", [1, E0])
        padi = sb("padi", [1, E0], I32)
        tab = [sb(f"tab{L}", [1, 2, 40], I32) for L in (0, 1)]
        zero = sb("zero", [P, D])
        xt = sb("xt", [P, 2, D])
        xtT = sb("xtT", [P, 2, KC, P])
        hid = sb("hid", [P, F1])
        hidT = sb("hidT", [P, F1])
        yt = sb("yt", [P, 2, D])
        yg = yt
        ge = xt[0:1].rearrange("p a d -> p (a d)")[:, 0:40 * E0].rearrange("p (i e) -> p i e", e=E0)
        tv = yt[0:1].rearrange("p a d -> p (a d)")[:, NT * 2 * E0:NT * 2 * E0 + 160].rearrange("p (n i) -> p n i", n=4)
        selA = yt[:].rearrange("p a d -> p (a d)")

        bank = [ctx.enter_context(nc.psum_tensor(f"bank{i}", [P, 512], F32)) for i in range(8)]
        bA, bB, bO, bT = bank[0], bank[1], bank[2], bank[3:5]
        bS = bank[5:8]
        oacc = bO[:, 0:H * (DH + 1)].rearrange("p (h d) -> p h d", h=H)
        mX, mG, mT, mY = bank[0], bank[1:5], bank[5:7], bank[7]

        names = """consts passed packed ctx_in x_in gate_in route_in pad_done w13_in w2_in u1_in u2_in
            kt_mm kt_done v_mm v_tmp v_done rep_done vl_mm
            stat1 var1 veps1 rstd1 xn1 bo_added xnT_mm xnT_cp qT_mm qT_cp score_mm masked hmaxed shifted
            exped probsT_mm probsT_cp pv_mm rdened on_cp oT_mm oT_cp y_mm resid
            stat2 var2 veps2 rstd2s xn2s x2T_mm x2T_cp z_mm z_cp top_v top_i ixf_cp onehot both_cp
            prefix_mm selected ranked posf_cp idx_cp cummed scattered fb_added
            cnt_mm rt yp_cp tabled padidx exps wsteps
            r1 r1_mm r1_done
            xt_in0 xt_in1 xtT_mm xtT_cp g1_mm acted hided hidT_mm hidT_cp y2_mm yt_cp yt_out0 yt_out1
            gidx_cp gathered combined0 combined stored""".split()
        s = {n: sem(n) for n in names}
        block = ctx.enter_context(nc.Block())

        def wait_apart(eng, name, value):
            eng.wait_ge(s[name], value)
            eng.sem_inc(s["passed"], 1)

        def tile(i):
            return X[:, bass.ds(i, 1), :].rearrange("p a d -> p (a d)")

        def col(t, i):
            return t[:, bass.ds(i, 1), :].rearrange("p a d -> p (a d)")

        def phases(eng, L, body, tail):
            body(0, True, False, 0)
            with eng.Fori(1, TB) as i:
                body(i, True, True, 0)
            body(TB, True, True, 1, first=True)
            with eng.Fori(TB + 1, NT - 1) as i:
                body(i, True, True, 1)
            body(NT - 1, False, True, 1)
            tail()

        def tiles_loop(eng, L, step):
            n = MT[L]
            step(0, 0, False, True)
            step(1, 1, True, True)
            with eng.Fori(2, n - 2, 2) as i:
                step(i, 0, True, True)
                step(i + 1, 1, True, True)
            step(n - 2, 0, True, True)
            step(n - 1, 1, True, False)

        def nth(L, i, per=1, j=0):
            return (i + L * NT) * per + j + 1

        def nth2(L, i):
            return i + L * NT + 1

        def dma_th(L, i, u):
            return (i - u + L * MT[0]) * 8 + 16

        def results_out(eng, L):
            for u in range(2):
                eng.wait_ge(s[f"yt_out{u}"], 8 * sum(MT[:L + 1]))

        def mth(L, i, per=1, j=0):
            return (i + L * MT[0]) * per + j + 1

        @block.sync
        def _(sp):
            sp.dma_start(X[:, 0:1, :], x[:, 0:1, :]).then_inc(s["x_in"], 16)
            sp.dma_start(pack[:], pack0).then_inc(s["packed"], 16)
            sp.dma_start(cT, ctxt).then_inc(s["ctx_in"], 16)
            sp.wait_ge(s["x_in"], 16)
            sp.dma_start(X[:, 1:NT, :], x[:, 1:NT, :]).then_inc(s["x_in"], 16)
            sp.dma_start(gw[:], gate).then_inc(s["gate_in"], 16)
            sp.dma_start(gb[:], gbias).then_inc(s["gate_in"], 16)
            sp.dma_start(ei[:], eidx).then_inc(s["route_in"], 16)
            sp.dma_start(wts[1][:], ewts).then_inc(s["route_in"], 16)
            sp.dma_start(fb[:], fbias).then_inc(s["route_in"], 16)
            for e in range(E0):
                sp.dma_start(arena[:, e * W13:(e + 1) * W13], w13[e]).then_inc(s["w13_in"], 16)

            def pads(L):
                sp.wait_ge(s["padidx"], L + 1)
                with sp.Fori(0, EXP[L]) as e:
                    r = sp.value_load(padi[0:1, bass.ds(e, 1)], min_val=0, max_val=(EXP[L] - 1) * REG + 2048)
                    sp.dma_start(xs[L][bass.ds(r, P), :], zero[:]).then_inc(s["pad_done"], 16)

            def ffn(L):
                sp.wait_ge(s["pad_done"], 16 * (E0 + L * E1))
                sp.wait_ge(s["scattered"], 32 * (NT + L * T1))
                sp.wait_ge(s["tabled"], L + 1)

                def load(i, u):
                    sp.wait_ge(s["xtT_mm"], mth(L, i) - 2) if not (isinstance(i, int) and i < 2 and L == 0) else None
                    r = sp.value_load(tab[L][0:1, 1, bass.ds(i, 1)], min_val=0, max_val=EXP[L] * REG - P)
                    sp.dma_start(xt[:, u, :], xs[L][bass.ds(r, P), :]).then_inc(s[f"xt_in{u}"], 16)

                load(0, 0)

                def step(i, u, prev, nxt):
                    if nxt:
                        load(i + 1, 1 - u)

                tiles_loop(sp, L, step)

            pads(0)
            sp.wait_ge(s["cnt_mm"], 1)
            for e in range(E0):
                sp.dma_start(arena[:, E0 * W13 + e * W2:E0 * W13 + (e + 1) * W2], w2[e]).then_inc(s["w2_in"], 16)
            ffn(0)
            sp.wait_ge(s["y2_mm"], MT[0])
            for e in range(E1):
                sp.dma_start(arena[:, e * U1:(e + 1) * U1], u1[e]).then_inc(s["u1_in"], 16)
            for e in range(EARLY1):
                sp.dma_start(arena[:, E1 * U1 + e * U2:E1 * U1 + (e + 1) * U2], u2[e]).then_inc(s["u2_in"], 16)
            sp.dma_start(pack[:], pack1).then_inc(s["packed"], 16)
            sp.dma_start(cT, ctxt).then_inc(s["ctx_in"], 16)
            pads(1)
            sp.wait_ge(s["y_mm"], 2 * NT)
            for e in range(EARLY1, E1):
                sp.dma_start(arena[:, E1 * U1 + e * U2:E1 * U1 + (e + 1) * U2], u2[e]).then_inc(s["u2_in"], 16)
            ffn(1)
            sp.wait_ge(s["fb_added"], NT)
            sp.dma_start(out[:, TB:NT, :], X[:, TB:NT, :]).then_inc(s["stored"], 16)
            for i in range(T1):
                sp.wait_ge(s["combined"], NT + i + 1)
                sp.dma_start(out[:, i:i + 1, :], X[:, i:i + 1, :]).then_inc(s["stored"], 16)
            sp.wait_ge(s["stored"], 16 * (T1 + 1))

        @block.gpsimd
        def _(gp):
            g = nc.gpsimd
            for t, v in ((ident, 0.0), (ustrict, 1.0), (ones, 1.0), (m16, 1.0), (m26, 1.0), (causal, 0.0),
                         (mhalf, -0.5), (zero, 0.0), (cum, 0.0), (cum1, 0.0)):
                g.memset(t[:], v).then_inc(s["consts"], 1)
            g.iota(iota[:], [[1, 64]], base=0, channel_multiplier=0,
                   allow_small_or_imprecise_dtypes=True).then_inc(s["consts"], 1)
            gp.wait_ge(s["consts"], 11)

            def select(t, op, fill, base, pattern, cm):
                g.affine_select(out=t, in_=t, compare_op=op, fill=fill, base=base, pattern=pattern,
                                channel_multiplier=cm).then_inc(s["consts"], 1)

            select(ident[:], ALU.not_equal, 1.0, 0, [[-1, P]], 1)
            select(ustrict[:], ALU.is_gt, 0.0, 0, [[1, P]], -1)
            select(m16[:], ALU.is_ge, 0.0, 0, [[-DH, HH]], 1)
            select(m26[:], ALU.is_ge, 0.0, 0, [[-CL, HL]], 1)
            select(causal[:], ALU.is_ge, NEG, 2 * P, [[-1, 2 * P + C]], 1)
            gp.wait_ge(s["consts"], 16)
            select(m16[:], ALU.is_ge, 0.0, DH - 1, [[DH, HH]], -1)
            select(m26[:], ALU.is_ge, 0.0, CL - 1, [[CL, HL]], -1)

            def attention(L):
                gp.wait_ge(s["packed"], 16 * (L + 1))

                def rsqrt1(i):
                    gp.wait_ge(s["veps1"], nth(L, i))
                    g.tensor_tensor(rstd[:], ve[:], mhalf[:], ALU.pow).then_inc(s["rstd1"], 1)

                def add_bo(i):
                    gp.wait_ge(s["xn1"], nth(L, i))
                    g.tensor_tensor(tile(i), tile(i), bo, ALU.add).then_inc(s["bo_added"], 1)

                def gather(i):
                    wait_apart(gp, "gidx_cp", i + 1)
                    for k in range(2):
                        g.indirect_dma_start(yg[:, k, :], None, ys[0],
                                             bass.IndirectOffsetOnAxis(ap=gidx[:, k:k + 1].bitcast(U32), axis=0)
                                             ).then_inc(s["gathered"], 16)

                def tail_of(i, b):
                    if L == 0 or b == 0:
                        gp.wait_ge(s["veps2"], nth2(L, i))
                        g.tensor_tensor(rstd2[:], ve2[:], mhalf[:], ALU.pow).then_inc(s["rstd2s"], 1)
                        gp.wait_ge(s["xn2s"], nth2(L, i))
                        wait_apart(gp, "idx_cp", nth2(L, i))
                        for k in range(2):
                            g.indirect_dma_start(xs[L], bass.IndirectOffsetOnAxis(ap=idx[:, k:k + 1].bitcast(U32), axis=0),
                                                 xn2[:], None).then_inc(s["scattered"], 16)
                    if L == 1:
                        if b == 1:
                            gp.wait_ge(s["resid"], nth(L, i))
                        g.tensor_tensor(tile(i), tile(i), fb[:], ALU.add).then_inc(s["fb_added"], 1)

                if L == 1:
                    gather(0)
                rsqrt1(0)
                add_bo(0)
                if L == 1:
                    gather(1)

                def body(i, front, back, b, first=False):
                    if front:
                        rsqrt1(i + 1)
                        add_bo(i + 1)
                        if L == 1:
                            if not isinstance(i, int) or i < NT - 2:
                                gather(i + 2)
                    if back:
                        tail_of(i - 1, 0 if first else b)

                if L == 0:
                    phases(gp, L, body, lambda: tail_of(NT - 1, 1))
                else:
                    body(0, True, False, 0)
                    with gp.Fori(1, TB) as i:
                        body(i, True, True, 0)
                    body(TB, True, True, 1, first=True)
                    with gp.Fori(TB + 1, NT - 2) as i:
                        body(i, True, True, 1)
                    body(NT - 2, True, True, 1)
                    body(NT - 1, False, True, 1)
                    tail_of(NT - 1, 1)

            def ffn(L):
                def step(i, u, prev, nxt):
                    wait_apart(gp, "yt_cp", mth(L, i))
                    gp.dma_start(ys[L][bass.ds(i * P, P), :], yt[:, u, :]).then_inc(s[f"yt_out{u}"], 16)

                tiles_loop(gp, L, step)

            gp.wait_ge(s["route_in"], 48)
            attention(0)
            ffn(0)
            results_out(gp, 0)
            attention(1)
            ffn(1)
            results_out(gp, 1)
            for i in range(T1):
                gp.wait_ge(s["gidx_cp"], NT + i + 1)
                for k in range(2):
                    g.indirect_dma_start(yg[:, k, :], None, ys[1],
                                         bass.IndirectOffsetOnAxis(ap=gidx[:, k:k + 1].bitcast(U32), axis=0)
                                         ).then_inc(s["gathered"], 16)

        @block.tensor
        def _(pe):
            t = nc.tensor

            def transpose(dst, src, n=P):
                return t.transpose(dst, src, ident[0:n, 0:n])

            pe.wait_ge(s["consts"], 18)

            def context(L):
                pe.wait_ge(s["packed"], 16 * (L + 1))
                pe.wait_ge(s["ctx_in"], 16 * (L + 1))
                for c in range(2):
                    for k in range(KC):
                        m = t.matmul(bS[c][:, 0:NB * C], wk[:, k, c * P:(c + 1) * P], cT[:, k, :],
                                     start=k == 0, stop=k == KC - 1)
                    m.then_inc(s["kt_mm"], 1)
                pe.wait_ge(s["rep_done"], L + 1)
                for b in range(NB):
                    for part, lhs in ((0, cT[:, :, b * C:b * C + P]), (1, cTrep[:, :, b])):
                        for k in range(KC):
                            l = lhs[:, k] if part == 0 else lhs[:, k].rearrange("p a c -> p (a c)")
                            n = P if part == 0 else HL * CL
                            m = t.matmul((bO, bS[2])[b][0:n, part * D:(part + 1) * D], l, wv[:, k, :],
                                         start=k == 0, stop=k == KC - 1)
                    m.then_inc(s["v_mm"], 1)

            def attention(L):
                def front1(i):
                    pe.wait_ge(s["xn1"], nth(L, i))
                    if not (L == 0 and isinstance(i, int) and i == 0):
                        pe.wait_ge(s["qT_cp"], nth(L, i) - 1)
                    for k in range(KC):
                        m = transpose(bA[:, k * P:(k + 1) * P], xn[:, k * P:(k + 1) * P])
                    m.then_inc(s["xnT_mm"], 1)

                def front2(i):
                    pe.wait_ge(s["xnT_cp"], nth(L, i))
                    for c in range(2):
                        for k in range(KC):
                            m = t.matmul(bA[:, D + c * P:D + (c + 1) * P], wq[:, k, c * P:(c + 1) * P],
                                         xnT[:, k, :], start=k == 0, stop=k == KC - 1)
                    m.then_inc(s["qT_mm"], 1)

                def scores(i, j, b):
                    if j == 0:
                        pe.wait_ge(s["qT_cp"], nth(L, i))
                    if not (L == 0 and isinstance(i, int) and i == 0 and j < SB):
                        pe.wait_ge(s["shifted"], nth(L, i, NS, j) - SB)
                    h, n = STEPS[j]
                    half, lo = h // HH, h % HH
                    t.matmul(bS[j % SB][:, 0:n * C], qT[:, half, :],
                             kblk[:, b, half, lo:lo + n, :].rearrange("p h c -> p (h c)"),
                             start=True, stop=True).then_inc(s["score_mm"], 1)

                def turn(i, g):
                    if g % 2 == 0:
                        pe.wait_ge(s["exped"], nth(L, i, 2, min(g // 2, 1)))
                    if not (L == 0 and isinstance(i, int) and i == 0 and g < 2):
                        pe.wait_ge(s["probsT_cp"], nth(L, i, 5, g) - 2)
                    for a in range(HL):
                        if g < NQ:
                            m = transpose(bT[g % 2][:, a * P:(a + 1) * P], probs[:, HL * g + a, 0:P])
                        else:
                            m = transpose(bT[g % 2][0:HL * CL, a * P:(a + 1) * P], last[:, HL * a:HL * a + HL].rearrange("p h c -> p (h c)"))
                    m.then_inc(s["probsT_mm"], 1)

                def weigh(i, g, b):
                    pe.wait_ge(s["probsT_cp"], nth(L, i, 5, g))
                    if g == 0 and not (L == 0 and isinstance(i, int) and i == 0):
                        pe.wait_ge(s["on_cp"], nth(L, i) - 1)
                    for a in range(HL):
                        pt = probsT[:, g, a * P:(a + 1) * P]
                        if g < NQ:
                            t.matmul(oacc[:, HL * g + a, :], pt, vm[:, b, HL * g + a, :], start=g + a == 0, stop=False,
                                     skip_group_check=True)
                        else:
                            m = t.matmul(oacc[:, HL * a:HL * a + HL, :], pt[0:HL * CL], vl[0:HL * CL, b, a],
                                         start=False, stop=a == HL - 1, skip_group_check=True)
                    if g == NQ:
                        m.then_inc(s["pv_mm"], 1)

                def back1(i):
                    pe.wait_ge(s["on_cp"], nth(L, i))
                    if L == 0:
                        if not (isinstance(i, int) and i == 0):
                            pe.wait_ge(s["selected"], i)
                    else:
                        pe.wait_ge(s["resid"], nth(L, i) - 1)
                    for k in range(KC):
                        m = transpose(bB[:, k * P:(k + 1) * P], on[:, k * P:(k + 1) * P])
                    m.then_inc(s["oT_mm"], 1)

                def back2(i):
                    pe.wait_ge(s["oT_cp"], nth(L, i))
                    for k in range(KC):
                        m = t.matmul(bB[:, D:2 * D], oT[:, k, :], wo[:, k, :], start=k == 0, stop=k == KC - 1)
                    m.then_inc(s["y_mm"], 1)

                def back3(i):
                    pe.wait_ge(s["xn2s"], nth2(L, i))
                    for k in range(KC):
                        m = transpose(bB[:, k * P:(k + 1) * P], xn2[:, k * P:(k + 1) * P])
                    m.then_inc(s["x2T_mm"], 1)

                def back4(i):
                    if isinstance(i, int) and i == 0:
                        pe.wait_ge(s["gate_in"], 32)
                    pe.wait_ge(s["x2T_cp"], i + 1)
                    for k in range(KC):
                        m = t.matmul(bB[:, D:D + E0], x2T[:, k, :], gw[:, k, :], start=k == 0, stop=k == KC - 1)
                    m.then_inc(s["z_mm"], 1)

                def back5(i):
                    pe.wait_ge(s["both_cp"], i + 1)
                    t.matmul(bB[:, 0:E0], ustrict[:], both[:], start=True, stop=False)
                    if not (isinstance(i, int) and i == 0):
                        pe.wait_ge(s["cummed"], i)
                    t.matmul(bB[:, 0:E0], ones[:], cum[:], start=False, stop=True).then_inc(s["prefix_mm"], 1)

                def body(i, front, back, b, first=False):
                    for j in (0, 1, 2):
                        scores(i, j, b)
                    if back:
                        back1(i - 1)
                    scores(i, 3, b)
                    if back:
                        back2(i - 1)
                    scores(i, 4, b)
                    scores(i, 5, b)
                    if front:
                        front1(i + 1)
                    turn(i, 0)
                    turn(i, 1)
                    if front:
                        front2(i + 1)
                    weigh(i, 0, b)
                    weigh(i, 1, b)
                    if back and L == 0:
                        back3(i - 1)
                    turn(i, 2)
                    turn(i, 3)
                    if back and L == 0:
                        back4(i - 1)
                    weigh(i, 2, b)
                    turn(i, 4)
                    weigh(i, 3, b)
                    weigh(i, 4, b)
                    if back and L == 0:
                        back5(i - 1)

                def tail():
                    back1(NT - 1)
                    back2(NT - 1)
                    if L == 0:
                        back3(NT - 1)
                        back4(NT - 1)
                        back5(NT - 1)
                        pe.wait_ge(s["cummed"], NT)
                        pe.wait_ge(s["selected"], NT)
                        t.matmul(bA[:, 0:E0], ones[:], cum[:], start=True, stop=True).then_inc(s["cnt_mm"], 1)

                front1(0)
                front2(0)
                pe.wait_ge(s["v_done"], 4 * (L + 1))
                pe.wait_ge(s["kt_done"], 2 * (L + 1))
                phases(pe, L, body, tail)

            def ffn(L):
                E, width, nk = EXP[L], (F0, F1)[L], (K0, K1)[L]
                ones_in = (E0, E1)[L] * 16
                pe.wait_ge(s["w13_in" if L == 0 else "u1_in"], ones_in)

                def turn_x(i, u):
                    pe.wait_ge(s[f"xt_in{u}"], dma_th(L, i, u))
                    if not (isinstance(i, int) and i == 0 and L == 0):
                        pe.wait_ge(s["xtT_cp"], mth(L, i) - 1)
                    for k in range(KC):
                        m = transpose(mX[:, k * P:(k + 1) * P], xt[:, u, k * P:(k + 1) * P])
                    m.then_inc(s["xtT_mm"], 1)

                def first(i, u, e):
                    pe.wait_ge(s["xtT_cp"], mth(L, i))
                    for half in range(2):
                        if L == 0:
                            if not (isinstance(i, int) and i == 0):
                                pe.wait_ge(s["hided"], 2 * i - 1 + half)
                            for w in range(2):
                                for k in range(KC):
                                    m = t.matmul(mG[2 * half + w][:, 0:HALF0], xtT[:, u, k, :],
                                                 arena[:, bass.ds(e * W13 + (w * KC + k) * F0 + half * HALF0, HALF0)],
                                                 start=k == 0, stop=k == KC - 1)
                        else:
                            if not (isinstance(i, int) and i < 2):
                                pe.wait_ge(s["acted"], 2 * MT[0] + 2 * i - 3 + half)
                            for k in range(KC):
                                m = t.matmul(mG[2 * u + half][:], xtT[:, u, k, :],
                                             arena[:, bass.ds(e * U1 + k * F1 + half * 512, 512)],
                                             start=k == 0, stop=k == KC - 1)
                        m.then_inc(s["g1_mm"], 1)

                def turn_h(i):
                    src = hid
                    pe.wait_ge(s["hided" if L == 0 else "acted"], 2 * i + 2 + (0 if L == 0 else 2 * MT[0]))
                    for g in range(2):
                        if not (isinstance(i, int) and i == 0 and L == 0):
                            pe.wait_ge(s["hidT_cp"], mth(L, i, 2, g) - 2)
                        for c in range(4 * g, min(4 * g + 4, nk)):
                            n = min(P, width - c * P)
                            m = transpose(mT[g][0:n, (c - 4 * g) * P:(c - 4 * g + 1) * P], src[:, c * P:c * P + n])
                        m.then_inc(s["hidT_mm"], 1)

                def second(i, e):
                    if not (isinstance(i, int) and i == 0 and L == 0):
                        pe.wait_ge(s["yt_cp"], mth(L, i) - 1)
                    base, step = (E0 * W13, W2) if L == 0 else (E1 * U1, U2)
                    for c in range(nk):
                        if c % 4 == 0:
                            pe.wait_ge(s["hidT_cp"], mth(L, i, 2, c // 4))
                        n = min(P, width - c * P)
                        m = t.matmul(mY[:, 0:D], hidT[0:n, c * P:(c + 1) * P],
                                     arena[0:n, bass.ds(e * step + base + c * D, D)],
                                     start=c == 0, stop=c == nk - 1)
                    m.then_inc(s["y2_mm"], 1)

                pe.wait_ge(s["tabled"], L + 1)
                turn_x(0, 0)

                def step(i, u, prev, nxt):
                    if nxt:
                        turn_x(i + 1, 1 - u)
                    e = pe.value_load(tab[L][0:1, 0, bass.ds(i, 1)], min_val=0, max_val=E - 1)
                    first(i, u, e)
                    if prev:
                        if isinstance(i, int) and i == 1:
                            pe.wait_ge(s["w2_in" if L == 0 else "u2_in"], ones_in)
                        turn_h(i - 1)
                        e = pe.value_load(tab[L][0:1, 0, bass.ds(i - 1, 1)], min_val=0, max_val=E - 1)
                        second(i - 1, e)

                tiles_loop(pe, L, step)
                turn_h(MT[L] - 1)
                e = pe.value_load(tab[L][0:1, 0, MT[L] - 1:MT[L]], min_val=0, max_val=E - 1)
                second(MT[L] - 1, e)

            context(0)
            pe.wait_ge(s["r1"], 3 + T1)
            flat = both1[:].rearrange("p t e -> p (t e)")
            t.matmul(bB[:, 0:T1 * E1], ustrict[:], flat, start=True, stop=False)
            t.matmul(bB[:, 0:T1 * E1], ones[:], cum1[:, 0:T1, :].rearrange("p t e -> p (t e)"), start=False, stop=True)
            t.matmul(bB[:, 256:256 + E1], ones[:], cum1[:, T1, :], start=True, stop=True).then_inc(s["r1_mm"], 1)
            pe.wait_ge(s["r1_done"], 1)
            attention(0)
            ffn(0)
            pe.wait_ge(s["yt_cp"], MT[0])
            context(1)
            attention(1)
            pe.wait_ge(s["resid"], 2 * NT)
            ffn(1)

        @block.scalar
        def _(ac):
            a = nc.scalar

            def attention(L):
                def xnT_out(i):
                    if not (L == 0 and isinstance(i, int) and i == 0):
                        ac.wait_ge(s["qT_mm"], nth(L, i) - 1)
                    ac.wait_ge(s["xnT_mm"], nth(L, i))
                    a.copy(xnT.rearrange("p k n -> p (k n)"), bA[:, 0:D]).then_inc(s["xnT_cp"], 1)

                def qT_out(i):
                    ac.wait_ge(s["qT_mm"], nth(L, i))
                    if not (L == 0 and isinstance(i, int) and i == 0):
                        ac.wait_ge(s["score_mm"], nth(L, i, NS, 0) - 1)
                    for c in range(2):
                        m = a.activation(qT[:, c, :], bA[:, D + c * P:D + (c + 1) * P], ACT.Identity, bias=bq[:, c:c + 1])
                    m.then_inc(s["qT_cp"], 1)

                def exponent(i, half):
                    ac.wait_ge(s["shifted"], nth(L, i, NS, 3 * half + 2))
                    hs = slice(half * HH, half * HH + HH)
                    if half == 0 and not (L == 0 and isinstance(i, int) and i == 0):
                        ac.wait_ge(s["probsT_mm"], nth(L, i, 5, 0) - 1)
                    a.activation(last[:, hs], probs[:, hs, P:C], ACT.Exp, scale=SCALE)
                    a.activation(probs[:, hs, 0:P], probs[:, hs, 0:P], ACT.Exp, scale=SCALE).then_inc(s["exped"], 1)

                def probs_out(i, g):
                    ac.wait_ge(s["probsT_mm"], nth(L, i, 5, g))
                    if g == 0 and not (L == 0 and isinstance(i, int) and i == 0):
                        ac.wait_ge(s["pv_mm"], nth(L, i) - 1)
                    n = P if g < NQ else HL * CL
                    a.copy(probsT[0:n, g, :], bT[g % 2][0:n, :]).then_inc(s["probsT_cp"], 1)

                def oT_out(i):
                    ac.wait_ge(s["oT_mm"], nth(L, i))
                    if not (L == 0 and isinstance(i, int) and i == 0):
                        ac.wait_ge(s["y_mm"], nth(L, i) - 1)
                    a.copy(oT.rearrange("p k n -> p (k n)"), bB[:, 0:D]).then_inc(s["oT_cp"], 1)

                def x2T_out(i):
                    ac.wait_ge(s["x2T_mm"], nth2(L, i))
                    if not (isinstance(i, int) and i == 0):
                        ac.wait_ge(s["z_mm"], i)
                    a.copy(x2T.rearrange("p k n -> p (k n)"), bB[:, 0:D]).then_inc(s["x2T_cp"], 1)

                def body(i, front, back, b, first=False):
                    if back:
                        oT_out(i - 1)
                    exponent(i, 0)
                    if front:
                        xnT_out(i + 1)
                    exponent(i, 1)
                    probs_out(i, 0)
                    probs_out(i, 1)
                    if front:
                        qT_out(i + 1)
                    if back and L == 0:
                        x2T_out(i - 1)
                    probs_out(i, 2)
                    probs_out(i, 3)
                    probs_out(i, 4)

                def tail():
                    oT_out(NT - 1)
                    if L == 0:
                        x2T_out(NT - 1)
                        ac.wait_ge(s["top_v"], 2 * NT)
                        a.activation(wts[0][:], mxs[:], ACT.Exp, scale=-1.0).then_inc(s["exps"], 1)

                ac.wait_ge(s["packed"], 16 * (L + 1))
                xnT_out(0)
                qT_out(0)
                phases(ac, L, body, tail)

            def ffn(L):
                def turned(i, u):
                    ac.wait_ge(s["xtT_mm"], mth(L, i))
                    if not (isinstance(i, int) and i < 2):
                        ac.wait_ge(s["g1_mm"], mth(L, i, 2, 1) - 4)
                    a.copy(xtT[:, u].rearrange("p k n -> p (k n)"), mX[:, 0:D]).then_inc(s["xtT_cp"], 1)

                def activate(i, u):
                    for half in range(2):
                        ac.wait_ge(s["g1_mm"], mth(L, i, 2, half))
                        if not (isinstance(i, int) and i == 0 and L == 0):
                            ac.wait_ge(s["hidT_mm"], mth(L, i, 2, half) - 2)
                        if L == 0:
                            m = a.activation(hid[:, half * HALF0:(half + 1) * HALF0], mG[2 * half][:, 0:HALF0], ACT.Silu)
                        else:
                            m = a.activation(hid[:, half * 512:(half + 1) * 512], mG[2 * u + half][:], ACT.Gelu)
                        m.then_inc(s["acted"], 1)

                def hidden_out(i):
                    for g in range(2):
                        ac.wait_ge(s["hidT_mm"], mth(L, i, 2, g))
                        if not (isinstance(i, int) and i == 0):
                            ac.wait_ge(s["y2_mm"], mth(L, i) - 1)
                        if L == 0 and g == 1:
                            a.copy(hidT[:, 4 * P:5 * P], mT[1][:, 0:P])
                            n = F0 - (K0 - 1) * P
                            m = a.copy(hidT[0:n, 5 * P:6 * P], mT[1][0:n, P:2 * P])
                        else:
                            m = a.copy(hidT[:, 4 * g * P:(4 * g + 4) * P], mT[g][:])
                        m.then_inc(s["hidT_cp"], 1)

                turned(0, 0)

                def step(i, u, prev, nxt):
                    if nxt:
                        turned(i + 1, 1 - u)
                    activate(i, u)
                    if prev:
                        hidden_out(i - 1)

                def step1(i, u, prev, nxt):
                    if nxt:
                        turned(i + 1, 1 - u)
                    if prev:
                        hidden_out(i - 1)
                    activate(i, u)

                tiles_loop(ac, L, step1)
                hidden_out(MT[L] - 1)

            attention(0)
            ffn(0)
            attention(1)
            ffn(1)

        @block.vector
        def _(dv):
            v = nc.vector

            def inc(ins, name):
                ins.then_inc(s[name], 1)

            def step_on(ins, name, counts):
                counts[name] = counts.get(name, 0) + 1
                ins.then_inc(s[name], 1)
                dv.wait_ge(s[name], counts[name])

            counts = {}

            def context(L):
                dv.wait_ge(s["packed"], 16 * (L + 1))
                dv.wait_ge(s["ctx_in"], 16 * (L + 1))
                for b in range(NB):
                    m = v.tensor_copy(cTrep[:, :, b], cT[:, :, b * C + P:(b + 1) * C].unsqueeze(2)
                                      .broadcast_to((P, KC, HL, CL)))
                m.then_inc(s["rep_done"], 1)
                if L == 0:
                    dv.wait_ge(s["consts"], 18)
                for c in range(2):
                    dv.wait_ge(s["kt_mm"], 2 * L + c + 1)
                    for b in range(NB):
                        m = v.scalar_tensor_tensor(
                            out=kblk[:, b, c], in0=bS[c][:, b * C:(b + 1) * C].unsqueeze(1).broadcast_to((P, HH, C)),
                            scalar=bk[:, c:c + 1], in1=m16[:].unsqueeze(2).broadcast_to((P, HH, C)),
                            op0=ALU.add, op1=ALU.mult)
                    m.then_inc(s["kt_done"], 1)
                for b in range(NB):
                    src = (bO, bS[2])[b]
                    dv.wait_ge(s["v_mm"], 2 * L + b + 1)
                    inc(v.tensor_tensor(vm[:, b, :, 0:DH], src[:, 0:D].rearrange("p (h d) -> p h d", h=H),
                                        bv.rearrange("p (h d) -> p h d", h=H), ALU.add), "v_done")
                    step_on(v.tensor_tensor(vtmp[0:HL * CL, :], src[0:HL * CL, D:2 * D], bv[0:HL * CL], ALU.add),
                            "v_tmp", counts)
                    mask = m26[0:HL * CL].unsqueeze(2).broadcast_to((HL * CL, HL, DH))
                    v.memset(vm[:, b, :, DH:DH + 1], 1.0)
                    if L == 0:
                        for q in range(NQ):
                            v.tensor_copy(vl[0:HL * CL, b, q, :, DH:DH + 1], m26[0:HL * CL].unsqueeze(2))
                    for q in range(NQ):
                        m = v.tensor_tensor(vl[0:HL * CL, b, q, :, 0:DH],
                                            vtmp[0:HL * CL, q * HL * DH:(q + 1) * HL * DH].rearrange("p (h d) -> p h d", h=HL),
                                            mask, ALU.mult)
                    inc(m, "v_done")
                    dv.wait_ge(s["v_done"], 4 * L + 2 * b + 2)

            def route1():
                dv.wait_ge(s["route_in"], 48)
                step_on(v.tensor_copy(eif[:], ei[:]), "r1", counts)
                step_on(v.tensor_tensor(oh[1][:].rearrange("p t k e -> p (t k) e"),
                                        eif[:].rearrange("p t k -> p (t k)").unsqueeze(2).broadcast_to((P, 2 * T1, E1)),
                                        iota[:, 0:E1].unsqueeze(1).broadcast_to((P, 2 * T1, E1)), ALU.is_equal), "r1", counts)
                step_on(v.tensor_tensor(both1[:], oh[1][:, :, 0], oh[1][:, :, 1], ALU.add), "r1", counts)
                for i in range(T1):
                    step_on(v.tensor_tensor(cum1[:, i + 1], cum1[:, i], both1[:, i], ALU.add), "r1", counts)
                dv.wait_ge(s["r1_mm"], 1)
                step_on(v.tensor_copy(pref[:].rearrange("p t e -> p (t e)"), bB[:, 0:T1 * E1]), "r1", counts)
                for k in range(2):
                    tmp = selA[:, 0:T1 * E1].rearrange("p (t e) -> p t e", e=E1)
                    step_on(v.tensor_tensor(tmp, oh[1][:, :, k], pref[:], ALU.mult), "r1", counts)
                    step_on(v.tensor_reduce(rank[1][:, :, k], tmp, AX.X, ALU.add), "r1", counts)
                    if k == 0:
                        step_on(v.tensor_tensor(pref[:], pref[:], oh[1][:, :, 0], ALU.add), "r1", counts)
                step_on(v.scalar_tensor_tensor(out=pos1f[:], in0=eif[:], scalar=float(REG), in1=rank[1][:],
                                               op0=ALU.mult, op1=ALU.add), "r1", counts)
                step_on(v.tensor_copy(pos1[:], pos1f[:]), "r1", counts)
                tables(1, bB[:, 256:256 + E1])
                step_on(v.tensor_copy(posf[:], pos1f[:, 0, :]), "r1_done", counts)

            def tables(L, cnt):
                E, n, w = EXP[L], MT[L], (NT, T1)[L]
                go = lambda m: step_on(m, "rt", counts)
                if L == 0:
                    pass
                go(v.tensor_scalar(ntf[:, 0:E], cnt, float(P - 1), None, ALU.add))
                if L == 0:
                    make_pads(0, cnt)
                else:
                    go(v.tensor_copy(cum1[:, T1, :], cnt))
                go(v.tensor_copy(cnti[:, 0:E], ntf[:, 0:E]))
                go(v.tensor_scalar(cnti[:, 0:E], cnti[:, 0:E], 7, None, ALU.arith_shift_right))
                go(v.tensor_copy(ntf[:, 0:E], cnti[:, 0:E]))
                go(v.tensor_tensor_scan(incl[:, 0:E], ones[:, 0:E], ntf[:, 0:E], 0.0, ALU.mult, ALU.add))
                go(v.tensor_tensor(excl[:, 0:E], incl[:, 0:E], ntf[:, 0:E], ALU.subtract))
                g = ge[0:1, 0:n, 0:E]
                go(v.tensor_tensor(g, iota[0:1, 0:n].unsqueeze(2).broadcast_to((1, n, E)),
                                   incl[0:1, 0:E].unsqueeze(1).broadcast_to((1, n, E)), ALU.is_ge))
                go(v.tensor_reduce(tv[0:1, 0, 0:n], g, AX.X, ALU.add))
                go(v.tensor_tensor(g, g, ntf[0:1, 0:E].unsqueeze(1).broadcast_to((1, n, E)), ALU.mult))
                go(v.tensor_reduce(tv[0:1, 1, 0:n], g, AX.X, ALU.add))
                go(v.tensor_tensor(tv[0:1, 1, 0:n], iota[0:1, 0:n], tv[0:1, 1, 0:n], ALU.subtract))
                go(v.tensor_scalar(tv[0:1, 2, 0:n], tv[0:1, 0, 0:n], float(REG), None, ALU.mult))
                go(v.scalar_tensor_tensor(out=tv[0:1, 1, 0:n], in0=tv[0:1, 1, 0:n], scalar=float(P), in1=tv[0:1, 2, 0:n],
                                          op0=ALU.mult, op1=ALU.add))
                go(v.tensor_scalar(tv[0:1, 3, 0:n], tv[0:1, 0, 0:n], float(E), None, ALU.is_lt))
                go(v.tensor_tensor(tv[0:1, 0:2, 0:n], tv[0:1, 0:2, 0:n],
                                   tv[0:1, 3, 0:n].unsqueeze(1).broadcast_to((1, 2, n)), ALU.mult))
                go(v.tensor_copy(tab[L][0:1, :, 0:n], tv[0:1, 0:2, 0:n]))
                tmp = selA[:, 0:w * 2 * E].rearrange("p (t e) -> p t e", e=E)
                go(v.tensor_tensor(tmp, oh[L][:].rearrange("p t k e -> p (t k) e"),
                                   excl[:, 0:E].unsqueeze(1).broadcast_to((P, 2 * w, E)), ALU.mult))
                flat = ypf[:, 0:w, :].rearrange("p t k -> p (t k)")
                go(v.tensor_reduce(flat, tmp, AX.X, ALU.add))
                go(v.scalar_tensor_tensor(out=ypf[:, 0:w, :], in0=ypf[:, 0:w, :], scalar=float(P), in1=rank[L][:],
                                          op0=ALU.mult, op1=ALU.add))
                go(v.tensor_copy(yp[L][:], ypf[:, 0:w, :]))

            def make_pads(L, cnt):
                E = EXP[L]
                go = lambda m: step_on(m, "rt", counts)
                go(v.scalar_tensor_tensor(out=padf[0:1, 0:E], in0=iota[0:1, 0:E], scalar=float(REG), in1=cnt[0:1, :],
                                          op0=ALU.mult, op1=ALU.add))
                step_on(v.tensor_copy(padi[0:1, 0:E], padf[0:1, 0:E]), "padidx", counts)

            def attention(L):
                def norm1(i):
                    if L == 1:
                        combine(i)
                    inc(v.bn_stats(stats[:], tile(i)), "stat1")
                    wait_apart(dv, "stat1", nth(L, i))
                    inc(v.bn_aggr(mv[:], stats[:]), "var1")
                    dv.wait_ge(s["var1"], nth(L, i))
                    inc(v.tensor_scalar(ve[:], mv[:, 1:2], EPS, None, ALU.add), "veps1")

                def scale1(i):
                    dv.wait_ge(s["rstd1"], nth(L, i))
                    if not (L == 0 and isinstance(i, int) and i == 0):
                        dv.wait_ge(s["xnT_mm"], nth(L, i) - 1)
                    inc(v.tensor_scalar(xn, tile(i), mv[:, 0:1], rstd[:, 0:1], ALU.subtract, ALU.mult), "xn1")

                def combine(i):
                    dv.wait_ge(s["gathered"], nth(0, i, 32, 31))
                    inc(v.scalar_tensor_tensor(out=tile(i), in0=yg[:, 0, :], scalar=wcol(0, i, 0), in1=tile(i),
                                               op0=ALU.mult, op1=ALU.add), "combined0")
                    dv.wait_ge(s["combined0"], i + 1)
                    inc(v.scalar_tensor_tensor(out=tile(i), in0=yg[:, 1, :], scalar=wcol(0, i, 1), in1=tile(i),
                                               op0=ALU.mult, op1=ALU.add), "combined")
                    wait_apart(dv, "combined", i + 1)

                def shift(i, j, b, masked):
                    h, n = STEPS[j]
                    dv.wait_ge(s["score_mm"], nth(L, i, NS, j))
                    src = bS[j % SB][:, 0:n * C].rearrange("p (h c) -> p h c", h=n)
                    dst = probs[:, h:h + n, :]
                    if j == 0 and not (L == 0 and isinstance(i, int) and i == 0):
                        dv.wait_ge(s["probsT_mm"], nth(L, i, 5, 0) - 1)
                    if masked is not None:
                        o = 2 * P - masked * P
                        inc(v.tensor_tensor(dst, src, causal[:, o:o + C].unsqueeze(1).broadcast_to((P, n, C)), ALU.add),
                            "masked")
                        counts["masked"] = counts.get("masked", 0) + 1
                        dv.wait_ge(s["masked"], counts["masked"])
                        src = dst
                    inc(v.tensor_reduce(hmax[:, h:h + n], src, AX.X, ALU.max), "hmaxed")
                    dv.wait_ge(s["hmaxed"], nth(L, i, NS, j))
                    inc(v.tensor_tensor(dst, src, hmax[:, h:h + n].unsqueeze(2).broadcast_to((P, n, C)), ALU.subtract),
                        "shifted")

                def normalise(i):
                    dv.wait_ge(s["pv_mm"], nth(L, i))
                    inc(v.reciprocal(rden[:].unsqueeze(2), oacc[:, :, DH:DH + 1]), "rdened")
                    if not (L == 0 and isinstance(i, int) and i == 0):
                        dv.wait_ge(s["oT_mm"], nth(L, i) - 1)
                    dv.wait_ge(s["rdened"], nth(L, i))
                    inc(v.tensor_tensor(on.rearrange("p (h d) -> p h d", h=H), oacc[:, :, 0:DH],
                                        rden[:].unsqueeze(2).broadcast_to((P, H, DH)), ALU.mult), "on_cp")

                def residual(i, b):
                    dv.wait_ge(s["y_mm"], nth(L, i))
                    dv.wait_ge(s["bo_added"], nth(L, i))
                    inc(v.tensor_tensor(tile(i), tile(i), bB[:, D:2 * D], ALU.add), "resid")
                    if L == 0 or b == 0:
                        wait_apart(dv, "resid", nth(L, i))
                        inc(v.bn_stats(stats2[:], tile(i)), "stat2")
                        wait_apart(dv, "stat2", nth2(L, i))
                        inc(v.bn_aggr(mv2[:], stats2[:]), "var2")
                        dv.wait_ge(s["var2"], nth2(L, i))
                        inc(v.tensor_scalar(ve2[:], mv2[:, 1:2], EPS, None, ALU.add), "veps2")

                def scale2(i, b):
                    if L == 1 and b == 1:
                        return
                    dv.wait_ge(s["rstd2s"], nth2(L, i))
                    if not (L == 0 and isinstance(i, int) and i == 0):
                        dv.wait_ge(s["scattered"], nth2(L, i) * 32 - 32)
                    if L == 0 and not (isinstance(i, int) and i == 0):
                        dv.wait_ge(s["x2T_mm"], i)
                    inc(v.tensor_scalar(xn2[:], tile(i), mv2[:, 0:1], rstd2[:, 0:1], ALU.subtract, ALU.mult), "xn2s")
                    if L == 1:
                        inc(v.tensor_copy(idx[:], col(pos1, i)), "idx_cp")

                def choose(i):
                    dv.wait_ge(s["z_mm"], i + 1)
                    inc(v.tensor_tensor(z[:], bB[:, D:D + E0], gb[:], ALU.add), "z_cp")
                    wait_apart(dv, "z_cp", i + 1)
                    inc(v.max(mx[:], z[:]), "top_v")
                    wait_apart(dv, "top_v", 2 * i + 1)
                    inc(v.max_index(ix[:], mx[:], z[:]), "top_i")
                    inc(v.tensor_copy(col(mxs, i), mx[:, 0:2]), "top_v")
                    dv.wait_ge(s["top_i"], i + 1)
                    inc(v.tensor_copy(ixf[:], ix[:, 0:2]), "ixf_cp")
                    dv.wait_ge(s["ixf_cp"], i + 1)
                    inc(v.tensor_tensor(oh[0][:, bass.ds(i, 1)].rearrange("p a k e -> p (a k) e"),
                                        iota[:, 0:E0].unsqueeze(1).broadcast_to((P, 2, E0)),
                                        ixf[:].unsqueeze(2).broadcast_to((P, 2, E0)), ALU.is_equal), "onehot")
                    dv.wait_ge(s["onehot"], i + 1)
                    if not (isinstance(i, int) and i == 0):
                        dv.wait_ge(s["cummed"], i)
                    o = oh[0][:, bass.ds(i, 1)].rearrange("p a k e -> p (a k) e")
                    inc(v.tensor_tensor(both[:], o[:, 0], o[:, 1], ALU.add), "both_cp")

                def place(i):
                    dv.wait_ge(s["prefix_mm"], i + 1)
                    o = oh[0][:, bass.ds(i, 1)].rearrange("p a k e -> p (a k) e")
                    inc(v.tensor_tensor(sel[:], o, bB[:, 0:E0].unsqueeze(1).broadcast_to((P, 2, E0)), ALU.mult), "selected")
                    inc(v.tensor_tensor(cum[:], cum[:], both[:], ALU.add), "cummed")
                    dv.wait_ge(s["selected"], i + 1)
                    inc(v.tensor_reduce(col(rank[0], i), sel[:], AX.X, ALU.add), "ranked")
                    dv.wait_ge(s["ranked"], i + 1)
                    inc(v.scalar_tensor_tensor(out=posf[:], in0=ixf[:], scalar=float(REG), in1=col(rank[0], i),
                                               op0=ALU.mult, op1=ALU.add), "posf_cp")
                    dv.wait_ge(s["posf_cp"], i + 1)
                    inc(v.tensor_copy(idx[:], posf[:]), "idx_cp")

                def next_gather(i):
                    inc(v.tensor_copy(gidx[:], col(yp[0], i)), "gidx_cp")

                def body(i, front, back, b, first=False):
                    pb = 0 if first else b
                    masked = i - TB * b if L == 1 and isinstance(i, int) and i - TB * b < 2 else None
                    for j in (0, 1, 2):
                        shift(i, j, b, masked)
                    if front:
                        norm1(i + 1)
                        if L == 1 and not (isinstance(i, int) and i == NT - 2):
                            next_gather(i + 2)
                    shift(i, 3, b, masked)
                    if front:
                        scale1(i + 1)
                    if back:
                        residual(i - 1, pb)
                    shift(i, 4, b, masked)
                    if back:
                        scale2(i - 1, pb)
                    shift(i, 5, b, masked)
                    if back and L == 0:
                        choose(i - 1)
                    normalise(i)
                    if back and L == 0:
                        place(i - 1)

                def tail():
                    residual(NT - 1, 1)
                    scale2(NT - 1, 1)
                    if L == 0:
                        choose(NT - 1)
                        place(NT - 1)

                if L == 0:
                    dv.wait_ge(s["x_in"], 16)
                else:
                    results_out(dv, 0)
                    next_gather(0)
                norm1(0)
                if L == 1:
                    next_gather(1)
                scale1(0)
                if L == 0:
                    dv.wait_ge(s["x_in"], 32)
                    phases(dv, L, body, tail)
                else:
                    body(0, True, False, 0)
                    body(1, True, True, 0)
                    with dv.Fori(2, TB) as i:
                        body(i, True, True, 0)
                    body(TB, True, True, 1, first=True)
                    body(TB + 1, True, True, 1)
                    with dv.Fori(TB + 2, NT - 2) as i:
                        body(i, True, True, 1)
                    body(NT - 2, True, True, 1)
                    body(NT - 1, False, True, 1)
                    tail()

            def wcol(L, i, k):
                return wts[L][:, bass.ds(i, 1), k:k + 1].rearrange("p a d -> p (a d)")

            def ffn(L):
                def gate_hidden(i):
                    for half in range(2):
                        dv.wait_ge(s["acted"], 2 * i + half + 1)
                        lo = half * HALF0
                        inc(v.tensor_tensor(hid[:, lo:lo + HALF0], hid[:, lo:lo + HALF0], mG[2 * half + 1][:, 0:HALF0],
                                            ALU.mult), "hided")

                def result(i, u):
                    dv.wait_ge(s["y2_mm"], mth(L, i))
                    if not (isinstance(i, int) and i < 2 and L == 0):
                        dv.wait_ge(s[f"yt_out{u}"], dma_th(L, i, u) - 16)
                    inc(v.tensor_copy(yt[:, u, :], mY[:, 0:D]), "yt_cp")

                def step(i, u, prev, nxt):
                    if L == 0:
                        gate_hidden(i)
                    if prev:
                        result(i - 1, 1 - u)

                def step0(i, u, prev, nxt):
                    if L == 0:
                        gate_hidden(i)
                    if prev:
                        result(i - 1, 1 - u)

                tiles_loop(dv, L, step0)
                result(MT[L] - 1, 1)

            context(0)
            route1()
            attention(0)
            dv.wait_ge(s["cnt_mm"], 1)
            tables(0, bA[:, 0:E0])
            inc(v.tensor_copy(posf[:], ypf[:, 0, :]), "tabled")
            dv.wait_ge(s["exps"], 1)
            go = lambda m: step_on(m, "wsteps", counts)
            w = wts[0]
            go(v.tensor_scalar(w[:], w[:], 1.0, None, ALU.add))
            go(v.reciprocal(w[:], w[:]))
            go(v.tensor_tensor(wsum[:], w[:, :, 0], w[:, :, 1], ALU.add))
            go(v.tensor_scalar(wsum[:], wsum[:], 1e-20, None, ALU.add))
            go(v.reciprocal(wsum[:], wsum[:]))
            go(v.tensor_tensor(w[:], w[:], wsum[:].unsqueeze(2).broadcast_to((P, NT, 2)), ALU.mult))
            ffn(0)
            dv.wait_ge(s["pad_done"], 16 * E0)
            make_pads(1, cum1[:, T1, :])
            context(1)
            attention(1)
            inc(v.tensor_copy(posf[:], ypf[:, 0, :]), "tabled")
            ffn(1)
            for i in range(T1):
                if i:
                    dv.wait_ge(s["gathered"], 32 * (NT + i))
                inc(v.tensor_copy(gidx[:], yp[1][:, i]), "gidx_cp")
                dv.wait_ge(s["gathered"], 32 * (NT + i + 1))
                if i == 0:
                    dv.wait_ge(s["fb_added"], NT)
                inc(v.scalar_tensor_tensor(out=X[:, i], in0=yg[:, 0, :], scalar=wts[1][:, i, 0:1], in1=X[:, i],
                                           op0=ALU.mult, op1=ALU.add), "combined0")
                dv.wait_ge(s["combined0"], NT + i + 1)
                inc(v.scalar_tensor_tensor(out=X[:, i], in0=yg[:, 1, :], scalar=wts[1][:, i, 1:2], in1=X[:, i],
                                           op0=ALU.mult, op1=ALU.add), "combined")


def kernel(**inputs):
    import numpy as np
    import concourse.bacc as bacc
    from concourse.bass_utils import run_bass_kernel_spmd as run

    a = {k: np.ascontiguousarray(v) for k, v in inputs.items()}

    def cols(w):
        k, n = w.shape
        pad = -k % P
        if pad:
            w = np.concatenate([w, np.zeros((pad, n), w.dtype)])
        return w.reshape(-1, P, n).transpose(1, 0, 2).reshape(P, -1)

    def rows(v):
        return np.broadcast_to(v, (P, v.shape[0]))

    def packed(L):
        g = lambda n: a[f"L{L}_xattn_{n}"]
        return np.ascontiguousarray(np.concatenate(
            [cols(g(n).T) for n in ("Wq", "Wk", "Wv", "Wo")]
            + [g(n).reshape(KC, P).T for n in ("bq", "bk")] + [rows(g("bv")), rows(g("bo"))], axis=1))

    def experts(n):
        return np.concatenate([a[f"L0_ffn_{n}"], a[f"L0_ffn_new_{n}"]])

    w1, w2, w3 = (experts(n) for n in ("w1", "w2", "w3"))
    gates = np.concatenate([a["L0_ffn_gate_weight"], a["L0_ffn_new_gate_weight"]])
    gbias = np.concatenate([np.zeros(E0 - 1, np.float32), a["L0_ffn_gate_bias"]])
    data = {
        "x": a["x"].reshape(NT, P, D).transpose(1, 0, 2),
        "ctxt": cols(a["ctx_1024"].reshape(NB * C, D).T).reshape(P, KC, NB * C),
        "pack0": packed(0),
        "pack1": packed(1),
        "w13": np.stack([np.concatenate([cols(w1[e].T), cols(w3[e].T)], axis=1) for e in range(E0)]),
        "w2": np.stack([cols(w2[e].T) for e in range(E0)]),
        "gate": cols(gates.T).reshape(P, KC, E0),
        "gbias": rows(gbias),
        "u1": np.stack([cols(a["L1_ffn_w1"][e]) for e in range(E1)]),
        "u2": np.stack([cols(a["L1_ffn_w2"][e]) for e in range(E1)]),
        "eidx": a["L1_ffn_expert_indices"].reshape(T1, P, 2).transpose(1, 0, 2),
        "ewts": a["L1_ffn_expert_weights"].reshape(T1, P, 2).transpose(1, 0, 2),
        "fbias": rows(a["L1_ffn_bias"]),
    }
    data = {k: np.ascontiguousarray(v) for k, v in data.items()}
    nc = bacc.Bacc("TRN2", target_bir_lowering=False, num_devices=1)
    args = [nc.dram_tensor(f"in_{k}", v.shape, mybir.dt.from_np(v.dtype), kind="ExternalInput").ap()
            for k, v in data.items()]
    out = nc.dram_tensor("out_0", (P, NT, D), F32, kind="ExternalOutput").ap()
    program(nc, *args, out)
    r = run(nc, [{f"in_{k}": v for k, v in data.items()}], core_ids=[0])
    return r.results[0]["out_0"].transpose(1, 0, 2).reshape(NB, SEQ, D)
```

```python
from contextlib import ExitStack

import concourse.bass as bass
from concourse import mybir

F32 = mybir.dt.float32
I32 = mybir.dt.int32
U32 = mybir.dt.uint32
ALU = mybir.AluOpType
ACT = mybir.ActivationFunctionType
AX = mybir.AxisListType

P = 128
D = 256
KC = D // P
NB = 2
SEQ = 1024
NT = NB * SEQ // P
TB = SEQ // P
H = 16
DH = D // H
C = 154
SCALE = DH ** -0.5
EPS = 1e-5
NEG = -1.0e30
STEPS = [(0, 3), (3, 3), (6, 2), (8, 3), (11, 3), (14, 2)]
NS = len(STEPS)
SB = 3
HH = H // 2
HW = (HH * C + P - 1) // P * P
NW = HW // P
NG = 2 * NW // 4

E0, F0 = 9, 704
E1, F1 = 8, 1024
K0 = (F0 + P - 1) // P
K1 = F1 // P
HALF0 = F0 // 2
T1 = 1024 // P
PAIRS = [2 * NT * P, 2 * T1 * P]


def even(n):
    return n + n % 2


MT = [even((PAIRS[0] + E0 * (P - 1)) // P), even((PAIRS[1] + E1 * (P - 1)) // P)]
EXP = [E0, E1]
REG = P + 2048

W13 = 2 * KC * F0
W2 = K0 * D
U1 = KC * F1
U2 = K1 * D
WE = W13 + W2
UE = U1 + U2
ARENA = E0 * WE
KBLK = NB * H * C
VBLK = NB * 2 * NW * P
ATT = ARENA - (KBLK + VBLK + 2 * 2 * HW)
EARLY = [ATT // WE, ATT // UE]
PACK = 4 * KC * D + 3 * KC + D


def program(nc, x, ctxt, pack0, pack1, w13, w2, gate, gbias, u1, u2, eidx, ewts, fbias, out):
    with ExitStack() as ctx:
        def sb(name, shape, dt=F32):
            return ctx.enter_context(nc.sbuf_tensor(name, shape, dt))

        def sem(name):
            return ctx.enter_context(nc.semaphore(name))

        xs = [nc.dram_tensor(f"rows{L}", (EXP[L] * REG, D), F32).ap() for L in (0, 1)]
        ys = [nc.dram_tensor(f"ffn{L}", (MT[L] * P, D), F32).ap() for L in (0, 1)]

        arena = sb("arena", [P, ARENA])
        o = ATT
        kblk = arena[:, o:o + KBLK].rearrange("p (b s h c) -> p b s h c", b=NB, s=2, h=HH)
        o += KBLK
        vblk = arena[:, o:o + VBLK].rearrange("p (b w d) -> p b w d", b=NB, w=2 * NW)
        o += VBLK
        probs = arena[:, o:o + 2 * HW].rearrange("p (s w) -> p s w", s=2)
        o += 2 * HW
        probsT = arena[:, o:o + 2 * HW].rearrange("p (w n) -> p w n", w=2 * NW)
        hid = sb("hid", [P, F1])
        hidT = sb("hidT", [P, F1])
        xn, xnT, qT, oT = (hid[:, n * D:(n + 1) * D] for n in range(4))
        x2T, rsrow, rsT = (hidT[:, n * D:(n + 1) * D] for n in range(3))
        xnT, qT, oT, x2T, rsT = (t.rearrange("p (k n) -> p k n", k=KC) for t in (xnT, qT, oT, x2T, rsT))
        cT = sb("cT", [P, KC, NB * C])
        yfin = arena[:, 0:T1 * 2 * D].rearrange("p (t k d) -> p t k d", t=T1, k=2)
        X = sb("X", [P, NT, D])
        pack = sb("pack", [P, PACK])
        wq, wk, wv, wo = (pack[:, n * KC * D:(n + 1) * KC * D].rearrange("p (k n) -> p k n", k=KC) for n in range(4))
        bq = pack[:, 4 * KC * D:4 * KC * D + KC]
        bk = pack[:, 4 * KC * D + KC:4 * KC * D + 2 * KC]
        bv = pack[:, 4 * KC * D + 2 * KC:4 * KC * D + 3 * KC]
        bo = pack[:, PACK - D:PACK]
        bqs = sb("bqs", [P, KC])
        m16 = sb("m16", [P, HH])
        ident = sb("ident", [P, P])
        ustrict = sb("ustrict", [P, P])
        ones = sb("ones", [P, P])
        iota = sb("iota", [P, 64])
        causal = sb("causal", [P, 2 * P + C])
        mhalf = sb("mhalf", [P, 1])
        stats = sb("stats", [P, 6])
        mv = sb("mv", [P, 2])
        ve = sb("ve", [P, 1])
        rstd = sb("rstd", [P, 1])
        stats2 = sb("stats2", [P, 6])
        mv2 = sb("mv2", [P, 2])
        ve2 = sb("ve2", [P, 1])
        rstd2 = sb("rstd2", [P, 1])
        nmax = sb("nmax", [P, H])
        rsum = sb("rsum", [P, H])
        rrec = sb("rrec", [P, H])
        xn2 = sb("xn2", [P, D])
        gw = sb("gw", [P, KC, E0])
        gb = sb("gb", [P, E0])
        fb = sb("fb", [P, D])
        z = sb("z", [P, E0])
        mx = sb("mx", [P, 8])
        ix = sb("ix", [P, 8], U32)
        mxs = sb("mxs", [P, NT, 2])
        ixf = sb("ixf", [P, 2])
        oh = [sb("oh0", [P, NT, 2, E0]), sb("oh1", [P, T1, 2, E1])]
        both = sb("both", [P, E0])
        both1 = sb("both1", [P, T1, E1])
        cum = sb("cum", [P, E0])
        cum1 = sb("cum1", [P, T1 + 1, E1])
        sel = sb("sel", [P, 2, E0])
        rank = [sb("rank0", [P, NT, 2]), sb("rank1", [P, T1, 2])]
        posf = sb("posf", [P, 2])
        idx = sb("idx", [P, 2], I32)
        pos1f = sb("pos1f", [P, T1, 2])
        pos1 = sb("pos1", [P, T1, 2], I32)
        ypf = sb("ypf", [P, NT, 2])
        yp = [sb("yp0", [P, NT, 2], I32), sb("yp1", [P, T1, 2], I32)]
        gidx = sb("gidx", [P, 2], I32)
        wts = [sb("wts0", [P, NT, 2]), sb("wts1", [P, T1, 2])]
        wsum = sb("wsum", [P, NT])
        ei = sb("ei", [P, T1, 2], I32)
        eif = sb("eif", [P, T1, 2])
        pref = sb("pref", [P, T1, E1])
        cnti = sb("cnti", [P, E0], I32)
        ntf = sb("ntf", [P, E0])
        incl = sb("incl", [P, E0])
        first = sb("first", [P, E0])
        skip = sb("skip", [1, E0])
        tab = [sb(f"tab{L}", [1, 2, 40], I32) for L in (0, 1)]
        zero = sb("zero", [P, D])
        xt = sb("xt", [P, 2, D])
        xtT = sb("xtT", [P, 2, KC, P])
        yt = sb("yt", [P, 2, D])
        yg = yt
        ge = xt[0:1].rearrange("p a d -> p (a d)")[:, 0:40 * E0].rearrange("p (i e) -> p i e", e=E0)
        tv = yt[0:1].rearrange("p a d -> p (a d)")[:, NT * 2 * E0:NT * 2 * E0 + 160].rearrange("p (n i) -> p n i", n=4)
        selA = yt[:].rearrange("p a d -> p (a d)")

        bank = [ctx.enter_context(nc.psum_tensor(f"bank{i}", [P, 512], F32)) for i in range(8)]
        bA, bB, bO, bT = bank[0], bank[1], bank[2], bank[3:5]
        bS = bank[5:8]
        oacc = bO[:, 0:D].rearrange("p (k n) -> p k n", k=KC)
        mX, mG, mT, mY = bank[0], bank[1:5], bank[5:7], bank[7]

        names = """consts passed packed ctx_in x_in gate_in route_in pad_done w_in0 w_in1
            kt_mm kt_done vt_mm vt_done vblkT_mm vblkT_cp bq_scaled
            stat1 var1 veps1 rstd1 xn1 bo_added xnT_mm xnT_cp qT_mm qT_cp score_mm masked maxed
            exped probsT_mm probsT_even probsT_odd pv_mm rsummed rsrowed rsT_mm rsT_cp oT_cp y_mm resid
            stat2 var2 veps2 rstd2s xn2s x2T_mm x2T_cp z_mm z_cp top_v top_i ixf_cp onehot both_cp
            prefix_mm selected ranked posf_cp idx_cp cummed scattered fb_added
            cnt_mm rt yp_cp tabled0 tabled1 exps wsteps
            r1 r1_mm r1_done
            xt_in0 xt_in1 xtT_mm xtT_cp g1_mm acted hided hidT_mm hidT_cp y2_mm yt_cp yt_out0 yt_out1
            gidx_cp gathered combined0 combined stored""".split() + [f"got{i}" for i in range(T1)]
        s = {n: sem(n) for n in names}
        block = ctx.enter_context(nc.Block())

        def wait_apart(eng, name, value):
            eng.wait_ge(s[name], value)
            eng.sem_inc(s["passed"], 1)

        def tile(i):
            return X[:, bass.ds(i, 1), :].rearrange("p a d -> p (a d)")

        def col(t, i):
            return t[:, bass.ds(i, 1), :].rearrange("p a d -> p (a d)")

        def token_tiles(eng, body):
            body(0)
            body(1)
            with eng.Fori(2, TB) as i:
                body(i, 0)
            body(TB)
            body(TB + 1)
            with eng.Fori(TB + 2, NT - 2) as i:
                body(i, 1)
            for i in range(NT - 2, NT + 2):
                body(i)

        def there(i):
            return not isinstance(i, int) or 0 <= i < NT

        def batch(i, b):
            return i // TB if isinstance(i, int) else b

        def later(value):
            return not isinstance(value, int) or value > 0

        def expert_tiles(eng, L, step):
            n = MT[L]
            for i in range(4):
                step(i, i % 2, i > 0, True)
            with eng.Fori(4, n - 2, 2) as i:
                step(i, 0, True, True)
                step(i + 1, 1, True, True)
            step(n - 2, 0, True, True)
            step(n - 1, 1, True, False)

        def masked(L, i):
            return L == 1 and isinstance(i, int) and i % TB < (C + P - 1) // P

        def nth(L, i, per=1, j=0):
            return (i + L * NT) * per + j + 1

        def nth2(L, i):
            return i + L * NT + 1

        def dma_th(L, i, u):
            return (i - u + L * MT[0]) * 8 + 16

        def results_out(eng, L):
            for u in range(2):
                eng.wait_ge(s[f"yt_out{u}"], 8 * sum(MT[:L + 1]))

        def mth(L, i, per=1, j=0):
            return (i + L * MT[0]) * per + j + 1

        @block.sync
        def _(sp):
            sp.dma_start(X[:, 0:1, :], x[:, 0:1, :]).then_inc(s["x_in"], 16)
            sp.dma_start(pack[:], pack0).then_inc(s["packed"], 16)
            sp.dma_start(cT[:], ctxt).then_inc(s["ctx_in"], 16)
            sp.wait_ge(s["x_in"], 16)
            sp.dma_start(X[:, 1:NT, :], x[:, 1:NT, :]).then_inc(s["x_in"], 16)
            sp.dma_start(gw[:], gate).then_inc(s["gate_in"], 16)
            sp.dma_start(gb[:], gbias).then_inc(s["gate_in"], 16)
            sp.wait_ge(s["consts"], 15)
            for L in (0, 1):
                for e in range(EXP[L]):
                    sp.dma_start(xs[L][e * REG:e * REG + P, :], zero[:]).then_inc(s["pad_done"], 16)
            sp.dma_start(ei[:], eidx).then_inc(s["route_in"], 16)
            sp.dma_start(wts[1][:], ewts).then_inc(s["route_in"], 16)
            sp.dma_start(fb[:], fbias).then_inc(s["route_in"], 16)

            def experts(L, lo, hi):
                n, first = (WE, UE)[L], (W13, U1)[L]
                for e in range(lo, hi):
                    sp.dma_start(arena[:, e * n:e * n + first], (w13, u1)[L][e]).then_inc(s[f"w_in{L}"], 16)
                    sp.dma_start(arena[:, e * n + first:(e + 1) * n], (w2, u2)[L][e]).then_inc(s[f"w_in{L}"], 16)

            experts(0, 0, EARLY[0])

            def ffn(L):
                if L == 0:
                    sp.wait_ge(s["pad_done"], 16 * (E0 + E1))
                sp.wait_ge(s["scattered"], 32 * (NT + L * T1))
                sp.wait_ge(s[f"tabled{L}"], 1)

                def load(i, u):
                    sp.wait_ge(s["xtT_mm"], mth(L, i) - 2) if not (isinstance(i, int) and i < 2 and L == 0) else None
                    r = sp.value_load(tab[L][0:1, 1, bass.ds(i, 1)], min_val=0, max_val=EXP[L] * REG - P)
                    sp.dma_start(xt[:, u, :], xs[L][bass.ds(r, P), :]).then_inc(s[f"xt_in{u}"], 16)

                load(0, 0)

                def step(i, u, prev, nxt):
                    if nxt:
                        load(i + 1, 1 - u)
                    if isinstance(i, int) and EARLY[L] + i < EXP[L]:
                        experts(L, EARLY[L] + i, EARLY[L] + i + 1)

                expert_tiles(sp, L, step)

            sp.wait_ge(s["cnt_mm"], 1)
            ffn(0)
            sp.dma_start(pack[:], pack1).then_inc(s["packed"], 16)
            sp.wait_ge(s["y2_mm"], MT[0])
            experts(1, 0, EARLY[1])
            sp.wait_ge(s["y_mm"], 2 * NT)
            ffn(1)
            sp.wait_ge(s["fb_added"], NT)
            sp.dma_start(out[:, TB:NT, :], X[:, TB:NT, :]).then_inc(s["stored"], 16)
            for i in range(T1):
                sp.wait_ge(s["combined"], NT + i + 1)
                sp.dma_start(out[:, i:i + 1, :], X[:, i:i + 1, :]).then_inc(s["stored"], 16)
            sp.wait_ge(s["stored"], 16 * (T1 + 1))

        @block.gpsimd
        def _(gp):
            g = nc.gpsimd
            for t, v in ((ident, 0.0), (ustrict, 1.0), (ones, 1.0), (m16, 1.0), (causal, 0.0),
                         (mhalf, -0.5), (zero, 0.0), (cum, 0.0), (cum1, 0.0)):
                g.memset(t[:], v).then_inc(s["consts"], 1)
            g.iota(iota[:], [[1, 64]], base=0, channel_multiplier=0,
                   allow_small_or_imprecise_dtypes=True).then_inc(s["consts"], 1)
            gp.wait_ge(s["consts"], 10)

            def select(t, op, fill, base, pattern, cm):
                g.affine_select(out=t, in_=t, compare_op=op, fill=fill, base=base, pattern=pattern,
                                channel_multiplier=cm).then_inc(s["consts"], 1)

            select(ident[:], ALU.not_equal, 1.0, 0, [[-1, P]], 1)
            select(ustrict[:], ALU.is_gt, 0.0, 0, [[1, P]], -1)
            select(m16[:], ALU.is_ge, 0.0, 0, [[-DH, HH]], 1)
            select(causal[:], ALU.is_ge, NEG, 2 * P, [[-1, 2 * P + C]], 1)
            gp.wait_ge(s["consts"], 14)
            select(m16[:], ALU.is_ge, 0.0, DH - 1, [[DH, HH]], -1)

            def attention(L):
                gp.wait_ge(s["packed"], 16 * (L + 1))

                def rsqrt1(i):
                    gp.wait_ge(s["veps1"], nth(L, i))
                    g.tensor_tensor(rstd[:], ve[:], mhalf[:], ALU.pow).then_inc(s["rstd1"], 1)

                def add_bo(i):
                    gp.wait_ge(s["xn1"], nth(L, i))
                    g.tensor_tensor(tile(i), tile(i), bo, ALU.add).then_inc(s["bo_added"], 1)

                def gather(i):
                    wait_apart(gp, "gidx_cp", i + 1)
                    for k in range(2):
                        g.indirect_dma_start(yg[:, k, :], None, ys[0],
                                             bass.IndirectOffsetOnAxis(ap=gidx[:, k:k + 1].bitcast(U32), axis=0)
                                             ).then_inc(s["gathered"], 16)

                def spread(i):
                    gp.wait_ge(s["rsummed"], nth(L, i))
                    if later(nth(L, i) - 1):
                        gp.wait_ge(s["rsT_mm"], nth(L, i) - 1)
                    g.tensor_tensor(rsrow.rearrange("p (h d) -> p h d", h=H), rrec[:].unsqueeze(2).broadcast_to((P, H, DH)),
                                    ones[:, 0:DH].unsqueeze(1).broadcast_to((P, H, DH)), ALU.mult
                                    ).then_inc(s["rsrowed"], 1)

                def rsqrt2(i):
                    gp.wait_ge(s["veps2"], nth2(L, i))
                    g.tensor_tensor(rstd2[:], ve2[:], mhalf[:], ALU.pow).then_inc(s["rstd2s"], 1)

                def scatter(i):
                    gp.wait_ge(s["xn2s"], nth2(L, i))
                    wait_apart(gp, "idx_cp", nth2(L, i))
                    for k in range(2):
                        g.indirect_dma_start(xs[L], bass.IndirectOffsetOnAxis(ap=idx[:, k:k + 1].bitcast(U32), axis=0),
                                             xn2[:], None).then_inc(s["scattered"], 16)

                def add_fb(i, b):
                    if batch(i, b) == 1:
                        gp.wait_ge(s["resid"], nth(L, i))
                    g.tensor_tensor(tile(i), tile(i), fb[:], ALU.add).then_inc(s["fb_added"], 1)

                if L == 1:
                    gather(0)
                rsqrt1(0)
                add_bo(0)
                if L == 1:
                    gather(1)

                def body(i, b=None):
                    routed = there(i - 2) and (L == 0 or batch(i - 2, b) == 0)
                    if there(i - 1):
                        spread(i - 1)
                    if there(i + 1):
                        rsqrt1(i + 1)
                    if routed:
                        rsqrt2(i - 2)
                    if there(i + 1):
                        add_bo(i + 1)
                    if L == 1 and there(i + 2):
                        gather(i + 2)
                    if routed:
                        scatter(i - 2)
                    if L == 1 and there(i - 2):
                        add_fb(i - 2, b)

                token_tiles(gp, body)

            def ffn(L):
                def step(i, u, prev, nxt):
                    wait_apart(gp, "yt_cp", mth(L, i))
                    gp.dma_start(ys[L][bass.ds(i * P, P), :], yt[:, u, :]).then_inc(s[f"yt_out{u}"], 16)

                expert_tiles(gp, L, step)

            gp.wait_ge(s["route_in"], 48)
            attention(0)
            ffn(0)
            results_out(gp, 0)
            attention(1)
            ffn(1)
            results_out(gp, 1)
            for i in range(T1):
                for k in range(2):
                    g.indirect_dma_start(yfin[:, i, k, :], None, ys[1],
                                         bass.IndirectOffsetOnAxis(ap=yp[1][:, i, k:k + 1].bitcast(U32), axis=0)
                                         ).then_inc(s[f"got{i}"], 16)

        @block.tensor
        def _(pe):
            t = nc.tensor

            def transpose(dst, src, n=P):
                return t.transpose(dst, src, ident[0:n, 0:n])

            pe.wait_ge(s["consts"], 15)

            def context(L):
                pe.wait_ge(s["packed"], 16 * (L + 1))
                pe.wait_ge(s["ctx_in"], 16)
                for w, banks, done in ((wv, (bO, bS[2]), "vt_mm"), (wk, bS[0:2], "kt_mm")):
                    for c in range(2):
                        for k in range(KC):
                            m = t.matmul(banks[c][:, 0:NB * C], w[:, k, c * P:(c + 1) * P], cT[:, k, :],
                                         start=k == 0, stop=k == KC - 1)
                        m.then_inc(s[done], 1)
                for b in range(NB):
                    pe.wait_ge(s["vt_done"], L * NB + b + 1)
                    for g in range(NG):
                        n = (L * NB + b) * NG + g
                        if n >= 2:
                            pe.wait_ge(s["vblkT_cp"], n - 1)
                        turn(g, bT[n % 2]).then_inc(s["vblkT_mm"], 1)

            def turn(g, bank):
                for a in range(4):
                    w = 4 * g + a
                    m = transpose(bank[:, a * P:(a + 1) * P],
                                  probs[:, w // NW, (w % NW) * P:(w % NW + 1) * P])
                return m

            def route1():
                pe.wait_ge(s["r1"], 3 + T1)
                flat = both1[:].rearrange("p t e -> p (t e)")
                t.matmul(bB[:, 0:T1 * E1], ustrict[:], flat, start=True, stop=False)
                t.matmul(bB[:, 0:T1 * E1], ones[:], cum1[:, 0:T1, :].rearrange("p t e -> p (t e)"), start=False, stop=True)
                t.matmul(bB[:, 256:256 + E1], ones[:], cum1[:, T1, :], start=True, stop=True).then_inc(s["r1_mm"], 1)

            def attention(L):
                def norm_turned(i):
                    pe.wait_ge(s["xn1"], nth(L, i))
                    if later(nth(L, i) - 2):
                        pe.wait_ge(s["rsT_cp"], nth(L, i) - 2)
                    if later(nth(L, i) - 1):
                        pe.wait_ge(s["qT_cp"], nth(L, i) - 1)
                    for k in range(KC):
                        m = transpose(bA[:, k * P:(k + 1) * P], xn[:, k * P:(k + 1) * P])
                    m.then_inc(s["xnT_mm"], 1)

                def queries(i):
                    pe.wait_ge(s["xnT_cp"], nth(L, i))
                    for c in range(2):
                        for k in range(KC):
                            m = t.matmul(bA[:, D + c * P:D + (c + 1) * P], wq[:, k, c * P:(c + 1) * P],
                                         xnT[:, k, :], start=k == 0, stop=k == KC - 1)
                    m.then_inc(s["qT_mm"], 1)

                def scores(i, j, b):
                    if j == 0:
                        pe.wait_ge(s["qT_cp"], nth(L, i))
                    if later(nth(L, i, NS, j) - SB):
                        pe.wait_ge(s["exped"], nth(L, i, NS, j) - SB)
                    h, n = STEPS[j]
                    half, lo = h // HH, h % HH
                    t.matmul(bS[j % SB][:, 0:n * C], qT[:, half, :],
                             kblk[:, b, half, lo:lo + n, :].rearrange("p h c -> p (h c)"),
                             start=True, stop=True).then_inc(s["score_mm"], 1)

                def probs_turned(i, g):
                    pe.wait_ge(s["exped"], nth(L, i, NS, g + 1))
                    turn(g, bT[g % 2]).then_inc(s["probsT_mm"], 1)

                def weigh(i, g, b):
                    if g % 2 == 0:
                        pe.wait_ge(s["probsT_even"], nth(L, i, 3, g // 2))
                    else:
                        pe.wait_ge(s["probsT_odd"], nth(L, i, 2, g // 2))
                    if g == 0 and later(nth(L, i) - 1):
                        pe.wait_ge(s["oT_cp"], nth(L, i) - 1)
                    for w in range(4 * g, 4 * g + 4):
                        m = t.matmul(oacc[:, w // NW, :], vblk[:, b, w, :], probsT[:, w, :],
                                     start=w % NW == 0, stop=w % NW == NW - 1)
                    if g == NG - 1:
                        m.then_inc(s["pv_mm"], 1)

                def sums_turned(i):
                    pe.wait_ge(s["rsrowed"], nth(L, i))
                    if not (isinstance(i, int) and i == NT - 1):
                        pe.wait_ge(s["qT_cp"], nth(L, i) + 1)
                    for k in range(KC):
                        m = transpose(bA[:, k * P:(k + 1) * P], rsrow[:, k * P:(k + 1) * P])
                    m.then_inc(s["rsT_mm"], 1)

                def output(i):
                    pe.wait_ge(s["oT_cp"], nth(L, i))
                    if L == 0 and isinstance(i, int) and i == 0:
                        pe.wait_ge(s["r1_done"], 1)
                    if later(nth(L, i) - 1):
                        if L == 0:
                            pe.wait_ge(s["selected"], i)
                        else:
                            pe.wait_ge(s["resid"], nth(L, i) - 1)
                    for k in range(KC):
                        m = t.matmul(bB[:, D:2 * D], oT[:, k, :], wo[:, k, :], start=k == 0, stop=k == KC - 1)
                    m.then_inc(s["y_mm"], 1)

                def norm2_turned(i):
                    pe.wait_ge(s["xn2s"], nth2(L, i))
                    for k in range(KC):
                        m = transpose(bB[:, k * P:(k + 1) * P], xn2[:, k * P:(k + 1) * P])
                    m.then_inc(s["x2T_mm"], 1)

                def gates(i):
                    if isinstance(i, int) and i == 0:
                        pe.wait_ge(s["gate_in"], 32)
                    pe.wait_ge(s["x2T_cp"], i + 1)
                    for k in range(KC):
                        m = t.matmul(bB[:, D:D + E0], x2T[:, k, :], gw[:, k, :], start=k == 0, stop=k == KC - 1)
                    m.then_inc(s["z_mm"], 1)

                def prefix(i):
                    pe.wait_ge(s["both_cp"], i + 1)
                    t.matmul(bB[:, 0:E0], ustrict[:], both[:], start=True, stop=False)
                    if later(i):
                        pe.wait_ge(s["cummed"], i)
                    t.matmul(bB[:, 0:E0], ones[:], cum[:], start=False, stop=True).then_inc(s["prefix_mm"], 1)

                def body(i, b=None):
                    here, prev, old, ahead = there(i), there(i - 1), there(i - 2), there(i + 1)
                    gated = old and L == 0
                    bs, bp = batch(i, b), batch(i - 1, b)
                    if prev:
                        probs_turned(i - 1, 0)
                    if here:
                        scores(i, 0, bs)
                    if old:
                        output(i - 2)
                    if prev:
                        probs_turned(i - 1, 1)
                    if here:
                        scores(i, 1, bs)
                    if prev:
                        weigh(i - 1, 0, bp)
                        sums_turned(i - 1)
                        probs_turned(i - 1, 2)
                    if here:
                        scores(i, 2, bs)
                    if prev:
                        weigh(i - 1, 1, bp)
                    if ahead:
                        norm_turned(i + 1)
                    if prev:
                        probs_turned(i - 1, 3)
                    if here:
                        scores(i, 3, bs)
                    if gated:
                        norm2_turned(i - 2)
                    if prev:
                        weigh(i - 1, 2, bp)
                        probs_turned(i - 1, 4)
                    if here:
                        scores(i, 4, bs)
                    if gated:
                        gates(i - 2)
                    if prev:
                        weigh(i - 1, 3, bp)
                    if here:
                        scores(i, 5, bs)
                    if ahead:
                        queries(i + 1)
                    if prev:
                        weigh(i - 1, 4, bp)
                    if gated:
                        prefix(i - 2)
                    if L == 0 and isinstance(i, int) and i == 0:
                        route1()

                norm_turned(0)
                queries(0)
                pe.wait_ge(s["vblkT_cp"], NB * NG * (L + 1))
                pe.wait_ge(s["kt_done"], L + 1)
                token_tiles(pe, body)
                if L == 0:
                    pe.wait_ge(s["cummed"], NT)
                    pe.wait_ge(s["rsT_cp"], NT)
                    t.matmul(bA[:, 0:E0], ones[:], cum[:], start=True, stop=True).then_inc(s["cnt_mm"], 1)

            def ffn(L):
                E, width, nk = EXP[L], (F0, F1)[L], (K0, K1)[L]
                base = (WE, UE)[L]
                second_at = (W13, U1)[L]

                def turn_x(i, u):
                    pe.wait_ge(s[f"xt_in{u}"], dma_th(L, i, u))
                    if not (isinstance(i, int) and i == 0 and L == 0):
                        pe.wait_ge(s["xtT_cp"], mth(L, i) - 1)
                    for k in range(KC):
                        m = transpose(mX[:, k * P:(k + 1) * P], xt[:, u, k * P:(k + 1) * P])
                    m.then_inc(s["xtT_mm"], 1)

                def first(i, u, e):
                    pe.wait_ge(s["xtT_cp"], mth(L, i))
                    for half in range(2):
                        if L == 0:
                            if not (isinstance(i, int) and i == 0):
                                pe.wait_ge(s["hided"], 2 * i - 1 + half)
                            for w in range(2):
                                for k in range(KC):
                                    m = t.matmul(mG[2 * half + w][:, 0:HALF0], xtT[:, u, k, :],
                                                 arena[:, bass.ds(e * base + (w * KC + k) * F0 + half * HALF0, HALF0)],
                                                 start=k == 0, stop=k == KC - 1)
                        else:
                            if not (isinstance(i, int) and i < 2):
                                pe.wait_ge(s["acted"], 2 * MT[0] + 2 * i - 3 + half)
                            for k in range(KC):
                                m = t.matmul(mG[2 * u + half][:], xtT[:, u, k, :],
                                             arena[:, bass.ds(e * base + k * F1 + half * 512, 512)],
                                             start=k == 0, stop=k == KC - 1)
                        m.then_inc(s["g1_mm"], 1)

                def turn_h(i):
                    src = hid
                    pe.wait_ge(s["hided" if L == 0 else "acted"], 2 * i + 2 + (0 if L == 0 else 2 * MT[0]))
                    for g in range(2):
                        if not (isinstance(i, int) and i == 0 and L == 0):
                            pe.wait_ge(s["hidT_cp"], mth(L, i, 2, g) - 2)
                        for c in range(4 * g, min(4 * g + 4, nk)):
                            n = min(P, width - c * P)
                            m = transpose(mT[g][0:n, (c - 4 * g) * P:(c - 4 * g + 1) * P], src[:, c * P:c * P + n])
                        m.then_inc(s["hidT_mm"], 1)

                def second(i, e):
                    if not (isinstance(i, int) and i == 0 and L == 0):
                        pe.wait_ge(s["yt_cp"], mth(L, i) - 1)
                    for c in range(nk):
                        if c % 4 == 0:
                            pe.wait_ge(s["hidT_cp"], mth(L, i, 2, c // 4))
                        n = min(P, width - c * P)
                        m = t.matmul(mY[:, 0:D], hidT[0:n, c * P:(c + 1) * P],
                                     arena[0:n, bass.ds(e * base + second_at + c * D, D)],
                                     start=c == 0, stop=c == nk - 1)
                    m.then_inc(s["y2_mm"], 1)

                pe.wait_ge(s[f"tabled{L}"], 1)
                pe.wait_ge(s[f"w_in{L}"], EARLY[L] * 32)
                turn_x(0, 0)

                def step(i, u, prev, nxt):
                    if nxt:
                        turn_x(i + 1, 1 - u)
                    e = pe.value_load(tab[L][0:1, 0, bass.ds(i, 1)], min_val=0, max_val=E - 1)
                    first(i, u, e)
                    if prev:
                        if isinstance(i, int) and i == 3:
                            pe.wait_ge(s[f"w_in{L}"], EXP[L] * 32)
                        turn_h(i - 1)
                        e = pe.value_load(tab[L][0:1, 0, bass.ds(i - 1, 1)], min_val=0, max_val=E - 1)
                        second(i - 1, e)

                expert_tiles(pe, L, step)
                turn_h(MT[L] - 1)
                e = pe.value_load(tab[L][0:1, 0, MT[L] - 1:MT[L]], min_val=0, max_val=E - 1)
                second(MT[L] - 1, e)

            context(0)
            attention(0)
            ffn(0)
            pe.wait_ge(s["yt_cp"], MT[0])
            context(1)
            attention(1)
            pe.wait_ge(s["resid"], 2 * NT)
            ffn(1)

        @block.scalar
        def _(ac):
            a = nc.scalar

            def attention(L):
                def xnT_out(i):
                    ac.wait_ge(s["xnT_mm"], nth(L, i))
                    a.copy(xnT.rearrange("p k n -> p (k n)"), bA[:, 0:D]).then_inc(s["xnT_cp"], 1)

                def qT_out(i):
                    ac.wait_ge(s["qT_mm"], nth(L, i))
                    for c in range(2):
                        m = a.activation(qT[:, c, :], bA[:, D + c * P:D + (c + 1) * P], ACT.Identity,
                                         bias=bqs[:, c:c + 1], scale=SCALE)
                    m.then_inc(s["qT_cp"], 1)

                def exponent(i, j, b):
                    h, n = STEPS[j]
                    ac.wait_ge(s["maxed"], nth(L, i, NS, j))
                    for k in range(n):
                        at = (h % HH + k) * C
                        dst = probs[:, h // HH, at:at + C]
                        src = dst if masked(L, i) else bS[j % SB][:, k * C:(k + 1) * C]
                        m = a.activation(dst, src, ACT.Exp, bias=nmax[:, h + k:h + k + 1],
                                         accum_out=rsum[:, h + k:h + k + 1])
                    m.then_inc(s["exped"], 1)

                def probs_out(i, g):
                    ac.wait_ge(s["probsT_mm"], nth(L, i, NG, g))
                    a.copy(probsT[:, 4 * g:4 * g + 4, :].rearrange("p w n -> p (w n)"), bT[g % 2][:]
                           ).then_inc(s["probsT_even"], 1)

                def rsT_out(i):
                    ac.wait_ge(s["rsT_mm"], nth(L, i))
                    if later(nth(L, i) - 1):
                        ac.wait_ge(s["oT_cp"], nth(L, i) - 1)
                    a.copy(rsT.rearrange("p k n -> p (k n)"), bA[:, 0:D]).then_inc(s["rsT_cp"], 1)

                def x2T_out(i):
                    ac.wait_ge(s["x2T_mm"], nth2(L, i))
                    a.copy(x2T.rearrange("p k n -> p (k n)"), bB[:, 0:D]).then_inc(s["x2T_cp"], 1)

                def body(i, b=None):
                    here, prev, old, ahead = there(i), there(i - 1), there(i - 2), there(i + 1)
                    bs = batch(i, b)
                    if prev:
                        probs_out(i - 1, 0)
                    if here:
                        exponent(i, 0, bs)
                        exponent(i, 1, bs)
                    if prev:
                        rsT_out(i - 1)
                        probs_out(i - 1, 2)
                    if here:
                        exponent(i, 2, bs)
                    if ahead:
                        xnT_out(i + 1)
                    if old and L == 0:
                        x2T_out(i - 2)
                    if here:
                        exponent(i, 3, bs)
                    if prev:
                        probs_out(i - 1, 4)
                    if here:
                        exponent(i, 4, bs)
                    if ahead:
                        qT_out(i + 1)
                    if here:
                        exponent(i, 5, bs)

                for n in range(L * NB * NG, (L + 1) * NB * NG):
                    ac.wait_ge(s["vblkT_mm"], n + 1)
                    g = n % NG
                    a.copy(vblk[:, n // NG % NB, 4 * g:4 * g + 4, :].rearrange("p w d -> p (w d)"), bT[n % 2][:]
                           ).then_inc(s["vblkT_cp"], 1)
                xnT_out(0)
                ac.wait_ge(s["bq_scaled"], L + 1)
                qT_out(0)
                token_tiles(ac, body)
                if L == 0:
                    ac.wait_ge(s["top_v"], 2 * NT)
                    a.activation(wts[0][:], mxs[:], ACT.Exp, scale=-1.0).then_inc(s["exps"], 1)

            def ffn(L):
                def turned(i, u):
                    ac.wait_ge(s["xtT_mm"], mth(L, i))
                    if not (isinstance(i, int) and i < 2):
                        ac.wait_ge(s["g1_mm"], mth(L, i, 2, 1) - 4)
                    a.copy(xtT[:, u].rearrange("p k n -> p (k n)"), mX[:, 0:D]).then_inc(s["xtT_cp"], 1)

                def activate(i, u):
                    for half in range(2):
                        ac.wait_ge(s["g1_mm"], mth(L, i, 2, half))
                        if not (isinstance(i, int) and i == 0 and L == 0):
                            ac.wait_ge(s["hidT_mm"], mth(L, i, 2, half) - 2)
                        if L == 0:
                            m = a.activation(hid[:, half * HALF0:(half + 1) * HALF0], mG[2 * half][:, 0:HALF0], ACT.Silu)
                        else:
                            m = a.activation(hid[:, half * 512:(half + 1) * 512], mG[2 * u + half][:], ACT.Gelu)
                        m.then_inc(s["acted"], 1)

                def hidden_out(i):
                    for g in range(2):
                        ac.wait_ge(s["hidT_mm"], mth(L, i, 2, g))
                        if not (isinstance(i, int) and i == 0):
                            ac.wait_ge(s["y2_mm"], mth(L, i) - 1)
                        if L == 0 and g == 1:
                            a.copy(hidT[:, 4 * P:5 * P], mT[1][:, 0:P])
                            n = F0 - (K0 - 1) * P
                            m = a.copy(hidT[0:n, 5 * P:6 * P], mT[1][0:n, P:2 * P])
                        else:
                            m = a.copy(hidT[:, 4 * g * P:(4 * g + 4) * P], mT[g][:])
                        m.then_inc(s["hidT_cp"], 1)

                turned(0, 0)

                def step(i, u, prev, nxt):
                    if nxt:
                        turned(i + 1, 1 - u)
                    if prev:
                        hidden_out(i - 1)
                    activate(i, u)

                expert_tiles(ac, L, step)
                hidden_out(MT[L] - 1)

            attention(0)
            ffn(0)
            attention(1)
            ffn(1)

        @block.vector
        def _(dv):
            v = nc.vector

            def inc(ins, name):
                ins.then_inc(s[name], 1)

            def step_on(ins, name, counts):
                counts[name] = counts.get(name, 0) + 1
                ins.then_inc(s[name], 1)
                dv.wait_ge(s[name], counts[name])

            counts = {}

            def context(L):
                dv.wait_ge(s["packed"], 16 * (L + 1))
                inc(v.tensor_scalar(bqs[:], bq, SCALE, None, ALU.mult), "bq_scaled")
                v.memset(probs[:, :, HH * C:HW], 0.0)

                def by_head(dst, src, b, bias, c):
                    return v.scalar_tensor_tensor(
                        out=dst, in0=src[:, b * C:(b + 1) * C].unsqueeze(1).broadcast_to((P, HH, C)),
                        scalar=bias[:, c:c + 1], in1=m16[:].unsqueeze(2).broadcast_to((P, HH, C)),
                        op0=ALU.add, op1=ALU.mult)

                for b in range(NB):
                    if b == 0:
                        dv.wait_ge(s["vt_mm"], 2 * (L + 1))
                    else:
                        dv.wait_ge(s["vblkT_mm"], (NB * L + b) * NG)
                    for c in range(2):
                        m = by_head(probs[:, c, 0:HH * C].rearrange("p (h c) -> p h c", h=HH), (bO, bS[2])[c], b, bv, c)
                    inc(m, "vt_done")
                    if b == 0:
                        dv.wait_ge(s["kt_mm"], 2 * (L + 1))
                    for c in range(2):
                        m = by_head(kblk[:, b, c], bS[c], b, bk, c)
                inc(m, "kt_done")

            def route1():
                dv.wait_ge(s["route_in"], 48)
                step_on(v.tensor_copy(eif[:], ei[:]), "r1", counts)
                step_on(v.tensor_tensor(oh[1][:].rearrange("p t k e -> p (t k) e"),
                                        eif[:].rearrange("p t k -> p (t k)").unsqueeze(2).broadcast_to((P, 2 * T1, E1)),
                                        iota[:, 0:E1].unsqueeze(1).broadcast_to((P, 2 * T1, E1)), ALU.is_equal), "r1", counts)
                step_on(v.tensor_tensor(both1[:], oh[1][:, :, 0], oh[1][:, :, 1], ALU.add), "r1", counts)
                for i in range(T1):
                    step_on(v.tensor_tensor(cum1[:, i + 1], cum1[:, i], both1[:, i], ALU.add), "r1", counts)
                dv.wait_ge(s["r1_mm"], 1)
                step_on(v.tensor_copy(pref[:].rearrange("p t e -> p (t e)"), bB[:, 0:T1 * E1]), "r1", counts)
                for k in range(2):
                    tmp = selA[:, 0:T1 * E1].rearrange("p (t e) -> p t e", e=E1)
                    step_on(v.tensor_tensor(tmp, oh[1][:, :, k], pref[:], ALU.mult), "r1", counts)
                    step_on(v.tensor_reduce(rank[1][:, :, k], tmp, AX.X, ALU.add), "r1", counts)
                    if k == 0:
                        step_on(v.tensor_tensor(pref[:], pref[:], oh[1][:, :, 0], ALU.add), "r1", counts)
                step_on(v.scalar_tensor_tensor(out=pos1f[:], in0=eif[:], scalar=float(REG), in1=rank[1][:],
                                               op0=ALU.mult, op1=ALU.add), "r1", counts)
                step_on(v.tensor_scalar(pos1[:], pos1f[:], float(P), None, ALU.add), "r1", counts)
                tables(1, bB[:, 256:256 + E1])
                step_on(v.tensor_copy(posf[:], pos1f[:, 0, :]), "r1_done", counts)

            def tables(L, cnt):
                E, n, w = EXP[L], MT[L], (NT, T1)[L]
                go = lambda m: step_on(m, "rt", counts)
                go(v.tensor_scalar(ntf[:, 0:E], cnt, 1.0, float(P - 1), ALU.max, ALU.add))
                go(v.tensor_copy(cnti[:, 0:E], ntf[:, 0:E]))
                go(v.tensor_scalar(cnti[:, 0:E], cnti[:, 0:E], 7, None, ALU.arith_shift_right))
                go(v.tensor_copy(ntf[:, 0:E], cnti[:, 0:E]))
                go(v.tensor_tensor_scan(incl[:, 0:E], ones[:, 0:E], ntf[:, 0:E], 0.0, ALU.mult, ALU.add))
                go(v.scalar_tensor_tensor(out=first[:, 0:E], in0=incl[:, 0:E], scalar=float(P), in1=cnt,
                                          op0=ALU.mult, op1=ALU.subtract))
                go(v.tensor_tensor(skip[0:1, 0:E - 1], first[0:1, 0:E - 1], first[0:1, 1:E], ALU.subtract))
                go(v.tensor_scalar(skip[0:1, 0:E - 1], skip[0:1, 0:E - 1], float(REG), None, ALU.add))
                g = ge[0:1, 0:n, 0:E]
                go(v.tensor_tensor(g, iota[0:1, 0:n].unsqueeze(2).broadcast_to((1, n, E)),
                                   incl[0:1, 0:E].unsqueeze(1).broadcast_to((1, n, E)), ALU.is_ge))
                go(v.tensor_reduce(tv[0:1, 0, 0:n], g, AX.X, ALU.add))
                g = ge[0:1, 0:n, 0:E - 1]
                go(v.tensor_tensor(g, g, skip[0:1, 0:E - 1].unsqueeze(1).broadcast_to((1, n, E - 1)), ALU.mult))
                go(v.tensor_reduce(tv[0:1, 1, 0:n], g, AX.X, ALU.add))
                go(v.tensor_scalar(tv[0:1, 2, 0:n], iota[0:1, 1:n + 1], float(P), first[0:1, 0:1], ALU.mult, ALU.subtract))
                go(v.tensor_tensor(tv[0:1, 1, 0:n], tv[0:1, 1, 0:n], tv[0:1, 2, 0:n], ALU.add))
                go(v.tensor_scalar(tv[0:1, 3, 0:n], tv[0:1, 0, 0:n], float(E), None, ALU.is_lt))
                go(v.tensor_tensor(tv[0:1, 0:2, 0:n], tv[0:1, 0:2, 0:n],
                                   tv[0:1, 3, 0:n].unsqueeze(1).broadcast_to((1, 2, n)), ALU.mult))
                inc(v.tensor_copy(tab[L][0:1, :, 0:n], tv[0:1, 0:2, 0:n]), f"tabled{L}")
                tmp = selA[:, 0:w * 2 * E].rearrange("p (t e) -> p t e", e=E)
                go(v.tensor_tensor(tmp, oh[L][:].rearrange("p t k e -> p (t k) e"),
                                   first[:, 0:E].unsqueeze(1).broadcast_to((P, 2 * w, E)), ALU.mult))
                go(v.tensor_reduce(ypf[:, 0:w, :].rearrange("p t k -> p (t k)"), tmp, AX.X, ALU.add))
                go(v.tensor_tensor(ypf[:, 0:w, :], ypf[:, 0:w, :], rank[L][:], ALU.add))
                go(v.tensor_copy(yp[L][:], ypf[:, 0:w, :]))

            def attention(L):
                def norm1(i):
                    if L == 1:
                        combine(i)
                    inc(v.bn_stats(stats[:], tile(i)), "stat1")
                    wait_apart(dv, "stat1", nth(L, i))
                    inc(v.bn_aggr(mv[:], stats[:]), "var1")
                    dv.wait_ge(s["var1"], nth(L, i))
                    inc(v.tensor_scalar(ve[:], mv[:, 1:2], EPS, None, ALU.add), "veps1")

                def scale1(i):
                    dv.wait_ge(s["rstd1"], nth(L, i))
                    if not (L == 0 and isinstance(i, int) and i == 0):
                        dv.wait_ge(s["xnT_mm"], nth(L, i) - 1)
                    inc(v.tensor_scalar(xn, tile(i), mv[:, 0:1], rstd[:, 0:1], ALU.subtract, ALU.mult), "xn1")

                def combine(i):
                    dv.wait_ge(s["gathered"], nth(0, i, 32, 31))
                    inc(v.scalar_tensor_tensor(out=tile(i), in0=yg[:, 0, :], scalar=wcol(0, i, 0), in1=tile(i),
                                               op0=ALU.mult, op1=ALU.add), "combined0")
                    dv.wait_ge(s["combined0"], i + 1)
                    inc(v.scalar_tensor_tensor(out=tile(i), in0=yg[:, 1, :], scalar=wcol(0, i, 1), in1=tile(i),
                                               op0=ALU.mult, op1=ALU.add), "combined")
                    wait_apart(dv, "combined", i + 1)

                def peak(i, j):
                    h, n = STEPS[j]
                    dv.wait_ge(s["score_mm"], nth(L, i, NS, j))
                    src = bS[j % SB][:, 0:n * C].rearrange("p (h c) -> p h c", h=n)
                    if masked(L, i):
                        at, o = h % HH * C, 2 * P - i % TB * P
                        dst = probs[:, h // HH, at:at + n * C].rearrange("p (h c) -> p h c", h=n)
                        step_on(v.tensor_tensor(dst, src, causal[:, o:o + C].unsqueeze(1).broadcast_to((P, n, C)),
                                                ALU.add), "masked", counts)
                        src = dst
                    inc(v.tensor_reduce(nmax[:, h:h + n], src, AX.X, ALU.max, negate=True), "maxed")

                def probs_out(i, g):
                    dv.wait_ge(s["probsT_mm"], nth(L, i, NG, g))
                    inc(v.tensor_copy(probsT[:, 4 * g:4 * g + 4, :].rearrange("p w n -> p (w n)"), bT[g % 2][:]),
                        "probsT_odd")

                def reciprocals(i):
                    dv.wait_ge(s["exped"], nth(L, i, NS, NS - 1))
                    if later(nth(L, i) - 1):
                        dv.wait_ge(s["rsrowed"], nth(L, i) - 1)
                    inc(v.reciprocal(rrec[:], rsum[:]), "rsummed")

                def normalise(i):
                    dv.wait_ge(s["rsT_cp"], nth(L, i))
                    dv.wait_ge(s["pv_mm"], nth(L, i))
                    inc(v.tensor_tensor(oT, oacc, rsT, ALU.mult), "oT_cp")

                def residual(i, b):
                    dv.wait_ge(s["y_mm"], nth(L, i))
                    dv.wait_ge(s["bo_added"], nth(L, i))
                    inc(v.tensor_tensor(tile(i), tile(i), bB[:, D:2 * D], ALU.add), "resid")
                    if L == 0 or b == 0:
                        wait_apart(dv, "resid", nth(L, i))
                        inc(v.bn_stats(stats2[:], tile(i)), "stat2")
                        wait_apart(dv, "stat2", nth2(L, i))
                        inc(v.bn_aggr(mv2[:], stats2[:]), "var2")
                        dv.wait_ge(s["var2"], nth2(L, i))
                        inc(v.tensor_scalar(ve2[:], mv2[:, 1:2], EPS, None, ALU.add), "veps2")

                def scale2(i, b):
                    if L == 1 and b == 1:
                        return
                    dv.wait_ge(s["rstd2s"], nth2(L, i))
                    if not (L == 0 and isinstance(i, int) and i == 0):
                        dv.wait_ge(s["scattered"], nth2(L, i) * 32 - 32)
                    if L == 0 and not (isinstance(i, int) and i == 0):
                        dv.wait_ge(s["x2T_mm"], i)
                    inc(v.tensor_scalar(xn2[:], tile(i), mv2[:, 0:1], rstd2[:, 0:1], ALU.subtract, ALU.mult), "xn2s")
                    if L == 1:
                        inc(v.tensor_copy(idx[:], col(pos1, i)), "idx_cp")

                def choose(i):
                    dv.wait_ge(s["z_mm"], i + 1)
                    inc(v.tensor_tensor(z[:], bB[:, D:D + E0], gb[:], ALU.add), "z_cp")
                    wait_apart(dv, "z_cp", i + 1)
                    inc(v.max(mx[:], z[:]), "top_v")
                    wait_apart(dv, "top_v", 2 * i + 1)
                    inc(v.max_index(ix[:], mx[:], z[:]), "top_i")
                    inc(v.tensor_copy(col(mxs, i), mx[:, 0:2]), "top_v")
                    dv.wait_ge(s["top_i"], i + 1)
                    inc(v.tensor_copy(ixf[:], ix[:, 0:2]), "ixf_cp")
                    dv.wait_ge(s["ixf_cp"], i + 1)
                    inc(v.tensor_tensor(oh[0][:, bass.ds(i, 1)].rearrange("p a k e -> p (a k) e"),
                                        iota[:, 0:E0].unsqueeze(1).broadcast_to((P, 2, E0)),
                                        ixf[:].unsqueeze(2).broadcast_to((P, 2, E0)), ALU.is_equal), "onehot")
                    dv.wait_ge(s["onehot"], i + 1)
                    if not (isinstance(i, int) and i == 0):
                        dv.wait_ge(s["cummed"], i)
                    o = oh[0][:, bass.ds(i, 1)].rearrange("p a k e -> p (a k) e")
                    inc(v.tensor_tensor(both[:], o[:, 0], o[:, 1], ALU.add), "both_cp")

                def place(i):
                    dv.wait_ge(s["prefix_mm"], i + 1)
                    o = oh[0][:, bass.ds(i, 1)].rearrange("p a k e -> p (a k) e")
                    inc(v.tensor_tensor(sel[:], o, bB[:, 0:E0].unsqueeze(1).broadcast_to((P, 2, E0)), ALU.mult), "selected")
                    inc(v.tensor_tensor(cum[:], cum[:], both[:], ALU.add), "cummed")
                    dv.wait_ge(s["selected"], i + 1)
                    inc(v.tensor_reduce(col(rank[0], i), sel[:], AX.X, ALU.add), "ranked")
                    dv.wait_ge(s["ranked"], i + 1)
                    inc(v.scalar_tensor_tensor(out=posf[:], in0=ixf[:], scalar=float(REG), in1=col(rank[0], i),
                                               op0=ALU.mult, op1=ALU.add), "posf_cp")
                    dv.wait_ge(s["posf_cp"], i + 1)
                    inc(v.tensor_scalar(idx[:], posf[:], float(P), None, ALU.add), "idx_cp")

                def next_gather(i):
                    inc(v.tensor_copy(gidx[:], col(yp[0], i)), "gidx_cp")

                def body(i, b=None):
                    here, prev, old, ahead = there(i), there(i - 1), there(i - 2), there(i + 1)
                    bo_ = batch(i - 2, b)
                    if prev:
                        reciprocals(i - 1)
                    if here:
                        peak(i, 0)
                    if ahead:
                        norm1(i + 1)
                        if L == 1 and there(i + 2):
                            next_gather(i + 2)
                    if prev:
                        probs_out(i - 1, 1)
                    if here:
                        peak(i, 1)
                    if ahead:
                        scale1(i + 1)
                    if old:
                        residual(i - 2, bo_)
                    if here:
                        peak(i, 2)
                    if old:
                        scale2(i - 2, bo_)
                    if prev:
                        probs_out(i - 1, 3)
                    if here:
                        peak(i, 3)
                        peak(i, 4)
                    if old and L == 0:
                        choose(i - 2)
                    if here:
                        peak(i, 5)
                    if prev:
                        normalise(i - 1)
                    if old and L == 0:
                        place(i - 2)
                    if L == 0 and isinstance(i, int) and i == 0:
                        route1()

                if L == 0:
                    context(0)
                    dv.wait_ge(s["x_in"], 16)
                else:
                    next_gather(0)
                    context(1)
                norm1(0)
                if L == 1:
                    next_gather(1)
                scale1(0)
                if L == 0:
                    dv.wait_ge(s["x_in"], 32)
                token_tiles(dv, body)

            def wcol(L, i, k):
                return wts[L][:, bass.ds(i, 1), k:k + 1].rearrange("p a d -> p (a d)")

            def ffn(L):
                def gate_hidden(i):
                    for half in range(2):
                        dv.wait_ge(s["acted"], 2 * i + half + 1)
                        lo = half * HALF0
                        inc(v.tensor_tensor(hid[:, lo:lo + HALF0], hid[:, lo:lo + HALF0], mG[2 * half + 1][:, 0:HALF0],
                                            ALU.mult), "hided")

                def result(i, u):
                    dv.wait_ge(s["y2_mm"], mth(L, i))
                    if not (isinstance(i, int) and i < 2 and L == 0):
                        dv.wait_ge(s[f"yt_out{u}"], dma_th(L, i, u) - 16)
                    inc(v.tensor_copy(yt[:, u, :], mY[:, 0:D]), "yt_cp")

                def step(i, u, prev, nxt):
                    if L == 0:
                        gate_hidden(i)
                    if prev:
                        result(i - 1, 1 - u)

                expert_tiles(dv, L, step)
                result(MT[L] - 1, 1)

            dv.wait_ge(s["consts"], 15)
            attention(0)
            dv.wait_ge(s["cnt_mm"], 1)
            tables(0, bA[:, 0:E0])
            dv.wait_ge(s["exps"], 1)
            go = lambda m: step_on(m, "wsteps", counts)
            w = wts[0]
            go(v.tensor_scalar(w[:], w[:], 1.0, None, ALU.add))
            go(v.reciprocal(w[:], w[:]))
            go(v.tensor_tensor(wsum[:], w[:, :, 0], w[:, :, 1], ALU.add))
            go(v.tensor_scalar(wsum[:], wsum[:], 1e-20, None, ALU.add))
            go(v.reciprocal(wsum[:], wsum[:]))
            go(v.tensor_tensor(w[:], w[:], wsum[:].unsqueeze(2).broadcast_to((P, NT, 2)), ALU.mult))
            ffn(0)
            attention(1)
            ffn(1)
            dv.wait_ge(s["fb_added"], NT)
            for i in range(T1):
                dv.wait_ge(s[f"got{i}"], 32)
                inc(v.scalar_tensor_tensor(out=X[:, i], in0=yfin[:, i, 0, :], scalar=wts[1][:, i, 0:1], in1=X[:, i],
                                           op0=ALU.mult, op1=ALU.add), "combined0")
                dv.wait_ge(s["combined0"], NT + i + 1)
                inc(v.scalar_tensor_tensor(out=X[:, i], in0=yfin[:, i, 1, :], scalar=wts[1][:, i, 1:2], in1=X[:, i],
                                           op0=ALU.mult, op1=ALU.add), "combined")


def kernel(**inputs):
    import numpy as np
    import concourse.bacc as bacc
    from concourse.bass_utils import run_bass_kernel_spmd as run

    a = {k: np.ascontiguousarray(v) for k, v in inputs.items()}

    def cols(w):
        k, n = w.shape
        pad = -k % P
        if pad:
            w = np.concatenate([w, np.zeros((pad, n), w.dtype)])
        return w.reshape(-1, P, n).transpose(1, 0, 2).reshape(P, -1)

    def rows(v):
        return np.broadcast_to(v, (P, v.shape[0]))

    def packed(L):
        g = lambda n: a[f"L{L}_xattn_{n}"]
        return np.ascontiguousarray(np.concatenate(
            [cols(g(n).T) for n in ("Wq", "Wk", "Wv", "Wo")]
            + [g(n).reshape(KC, P).T for n in ("bq", "bk", "bv")] + [rows(g("bo"))], axis=1))

    def experts(n):
        return np.concatenate([a[f"L0_ffn_{n}"], a[f"L0_ffn_new_{n}"]])

    w1, w2, w3 = (experts(n) for n in ("w1", "w2", "w3"))
    gates = np.concatenate([a["L0_ffn_gate_weight"], a["L0_ffn_new_gate_weight"]])
    gbias = np.concatenate([np.zeros(E0 - 1, np.float32), a["L0_ffn_gate_bias"]])
    data = {
        "x": a["x"].reshape(NT, P, D).transpose(1, 0, 2),
        "ctxt": cols(a["ctx_1024"].reshape(NB * C, D).T).reshape(P, KC, NB * C),
        "pack0": packed(0),
        "pack1": packed(1),
        "w13": np.stack([np.concatenate([cols(w1[e].T), cols(w3[e].T)], axis=1) for e in range(E0)]),
        "w2": np.stack([cols(w2[e].T) for e in range(E0)]),
        "gate": cols(gates.T).reshape(P, KC, E0),
        "gbias": rows(gbias),
        "u1": np.stack([cols(a["L1_ffn_w1"][e]) for e in range(E1)]),
        "u2": np.stack([cols(a["L1_ffn_w2"][e]) for e in range(E1)]),
        "eidx": a["L1_ffn_expert_indices"].reshape(T1, P, 2).transpose(1, 0, 2),
        "ewts": a["L1_ffn_expert_weights"].reshape(T1, P, 2).transpose(1, 0, 2),
        "fbias": rows(a["L1_ffn_bias"]),
    }
    data = {k: np.ascontiguousarray(v) for k, v in data.items()}
    nc = bacc.Bacc("TRN2", target_bir_lowering=False, num_devices=1)
    args = [nc.dram_tensor(f"in_{k}", v.shape, mybir.dt.from_np(v.dtype), kind="ExternalInput").ap()
            for k, v in data.items()]
    out = nc.dram_tensor("out_0", (P, NT, D), F32, kind="ExternalOutput").ap()
    program(nc, *args, out)
    r = run(nc, [{f"in_{k}": v for k, v in data.items()}], core_ids=[0])
    return r.results[0]["out_0"].transpose(1, 0, 2).reshape(NB, SEQ, D)
```

```python
from contextlib import ExitStack

import concourse.bass as bass
from concourse import mybir

F32 = mybir.dt.float32
F32R = mybir.dt.float32r
I32 = mybir.dt.int32
U32 = mybir.dt.uint32
ALU = mybir.AluOpType
ACT = mybir.ActivationFunctionType
AX = mybir.AxisListType

P = 128
D = 256
KC = D // P
NB = 2
SEQ = 1024
NT = NB * SEQ // P
TB = SEQ // P
H = 16
DH = D // H
C = 154
CL = C - P
SCALE = DH ** -0.5
EPS = 1e-5
NEG = -1.0e30
HP = 2
NS = H // HP
PARTS = 3
PK = HP * PARTS * DH
SB = 3
HH = H // 2
HW = (HH * C + P - 1) // P * P
NW = HW // P
NG = 2 * NW // 4


def last_step(g):
    half, col = divmod(4 * P * (g + 1) - 1, HW)
    return (half * HH + min(col, HH * C - 1) // C) // HP


KR = 3
ROUNDS = (NS + KR - 1) // KR


E0, F0 = 9, 704
E1, F1 = 8, 1024
K0 = (F0 + P - 1) // P
K1 = F1 // P
HALF0 = F0 // 2
T1 = 1024 // P
PAIRS = [2 * NT * P, 2 * T1 * P]
EXP = [E0, E1]
MT = [(PAIRS[L] + EXP[L] * (P - 1) + EXP[L] - 1) // P for L in (0, 1)]
REG = P + 2048

W13 = 2 * KC * F0
W2 = K0 * D
U1 = KC * F1
U2 = K1 * D
WE = W13 + W2
UE = U1 + U2
ARENA = E0 * WE
KBLK = NB * H * C
VBLK = NB * 2 * NW * P
QT = NS * P
FAST = KBLK + QT
ATT = ARENA - (FAST + VBLK + 2 * 2 * HW + H * PARTS * DH)
EARLY = [ATT // WE, ATT // UE]
PACK1 = 2 * KC * D + KC + 3 * D
PACK = PACK1 + 2 * KC * D


def program(nc, x, ctxt, pack0, pack1, w13, w2, gate, gbias, u1, u2, eidx, ewts, fbias, out):
    with ExitStack() as ctx:
        def sb(name, shape, dt=F32):
            return ctx.enter_context(nc.sbuf_tensor(name, shape, dt))

        def sem(name):
            return ctx.enter_context(nc.semaphore(name))

        xs = [nc.dram_tensor(f"rows{L}", (EXP[L] * REG, D), F32).ap() for L in (0, 1)]
        ys = [nc.dram_tensor(f"ffn{L}", (MT[L] * P, D), F32).ap() for L in (0, 1)]

        with nc.sbuf_tensor("below", [P, ATT], F32), nc.sbuf_tensor("fast", [P, FAST], F32R) as fast:
            pass
        arena = sb("arena", [P, ARENA])
        o = 0
        kblk = fast[0:PK, o:o + KBLK].rearrange("p (b j h c) -> p b j h c", b=NB, j=NS, h=HP)
        qT = fast[0:PK, KBLK:FAST].rearrange("p (j n) -> p j n", j=NS)
        o = ATT + FAST
        vblk = arena[:, o:o + VBLK].rearrange("p (b w d) -> p b w d", b=NB, w=2 * NW)
        o += VBLK
        probs = arena[:, o:o + 2 * HW].rearrange("p (s w) -> p s w", s=2)
        o += 2 * HW
        probsT = arena[:, o:o + 2 * HW].rearrange("p (w n) -> p w n", w=2 * NW)
        kf = arena[:, o:o + 2 * NB * D].rearrange("p (b t d) -> p b t d", b=NB, t=2)
        khl = arena[:, o + 2 * NB * D:o + 2 * NB * D + 2 * H * PARTS * DH].rearrange(
            "p (t h r d) -> p t h r d", t=2, h=H, r=PARTS)
        o += 2 * HW
        qhl = arena[:, o:o + H * PARTS * DH].rearrange("p (h r d) -> p h r d", h=H, r=PARTS)
        hid = sb("hid", [P, F1])
        hidT = sb("hidT", [P, F1])
        xn, xnT, qf, oT = (hid[:, n * D:(n + 1) * D] for n in range(4))
        x2T, rsrow, rsT, zero = (hidT[:, n * D:(n + 1) * D] for n in range(4))
        xnT, oT, x2T, rsT = (t.rearrange("p (k n) -> p k n", k=KC) for t in (xnT, oT, x2T, rsT))
        vT = hidT[:, 0:2 * NB * C].rearrange("p (s n) -> p s n", s=2)
        cT = sb("cT", [P, KC, NB * C])
        yfin = arena[:, 0:T1 * 2 * D].rearrange("p (t k d) -> p t k d", t=T1, k=2)
        X = sb("X", [P, NT, D])
        pack = sb("pack", [P, PACK])
        wk, wv = (pack[:, n * KC * D:(n + 1) * KC * D].rearrange("p (k n) -> p k n", k=KC) for n in range(2))
        wq, wo = (pack[:, PACK - (n + 1) * KC * D:PACK - n * KC * D].rearrange("p (k n) -> p k n", k=KC) for n in range(2))
        bv = pack[:, 2 * KC * D:2 * KC * D + KC]
        bq, bk, bo = (pack[:, PACK1 - (3 - n) * D:PACK1 - (2 - n) * D] for n in range(3))
        m16 = sb("m16", [P, HH])
        m48 = sb("m48", [P, HP])
        ident = sb("ident", [P, P])
        ustrict = sb("ustrict", [P, P])
        ones = sb("ones", [P, P])
        iota = sb("iota", [P, 64])
        causal = sb("causal", [P, 2 * P + C])
        mhalf = sb("mhalf", [P, 1])
        warm = sb("warm", [P, 1])
        stats = sb("stats", [P, 6])
        mv = sb("mv", [P, 2])
        ve = sb("ve", [P, 1])
        rstd = sb("rstd", [P, 1])
        stats2 = sb("stats2", [P, 6])
        mv2 = sb("mv2", [P, 2])
        ve2 = sb("ve2", [P, 1])
        rstd2 = sb("rstd2", [P, 1])
        nmax = sb("nmax", [P, H])
        rsum = sb("rsum", [P, H])
        rrec = sb("rrec", [P, H])
        xn2 = sb("xn2", [P, D])
        gw = sb("gw", [P, KC, E0])
        gb = sb("gb", [P, E0])
        fb = sb("fb", [P, D])
        z = sb("z", [P, E0])
        mx = sb("mx", [P, 8])
        ix = sb("ix", [P, 8], U32)
        mxs = sb("mxs", [P, NT, 2])
        ixf = sb("ixf", [P, 2])
        oh = [sb("oh0", [P, NT, 2, E0]), sb("oh1", [P, T1, 2, E1])]
        both = sb("both", [P, E0])
        both1 = sb("both1", [P, T1, E1])
        cum = sb("cum", [P, E0])
        cum1 = sb("cum1", [P, T1 + 1, E1])
        sel = sb("sel", [P, 2, E0])
        rank = [sb("rank0", [P, NT, 2]), sb("rank1", [P, T1, 2])]
        posf = sb("posf", [P, 2])
        idx = sb("idx", [P, 2], I32)
        idx_last = sb("idx_last", [P, 2], I32)
        pos1f = sb("pos1f", [P, T1, 2])
        pos1 = sb("pos1", [P, T1, 2], I32)
        ypf = sb("ypf", [P, NT, 2])
        yp = [sb("yp0", [P, NT, 2], I32), sb("yp1", [P, T1, 2], I32)]
        gidx = sb("gidx", [P, 2], I32)
        wts = [sb("wts0", [P, NT, 2]), sb("wts1", [P, T1, 2])]
        wsum = sb("wsum", [P, NT])
        ei = sb("ei", [P, T1, 2], I32)
        eif = sb("eif", [P, T1, 2])
        pref = sb("pref", [P, T1, E1])
        cnti = sb("cnti", [P, E0], I32)
        ntf = sb("ntf", [P, E0])
        incl = sb("incl", [P, E0])
        cnt1 = sb("cnt1", [P, E1])
        first = sb("first", [P, E0])
        skip = sb("skip", [1, E0])
        tab = [sb(f"tab{L}", [1, 2, 40], I32) for L in (0, 1)]
        xt = sb("xt", [P, 2, D])
        xtT = sb("xtT", [P, 2, KC, P])
        yt = sb("yt", [P, 2, D])
        yg = yt
        ge = pack[0:1, 0:40 * E0].rearrange("p (i e) -> p i e", e=E0)
        tv = pack[0:1, 512:512 + 4 * 40].rearrange("p (n i) -> p n i", n=4)
        sel2 = pack[:, 1024:1024 + 2 * NT * E0]

        bank = [ctx.enter_context(nc.psum_tensor(f"bank{i}", [P, 512], F32)) for i in range(8)]
        bA, bB, bO, bT = bank[0], bank[1], bank[2], bank[3:5]
        bS = bank[5:8]
        oacc = bO[:, 0:D].rearrange("p (k n) -> p k n", k=KC)
        mX, mG, mT, mY = bank[0], bank[1:5], bank[5:7], bank[7]

        names = """consts passed packed packed2 ctx_in x_in gate_in eidx_in route_in pad_done w_in0 w_in1
            k_mm kfed k_high k_low kT_mm kblked vt_mm vt_cp vt_even vt_odd vblkT_mm vblkT_cp q_bias_scaled
            stat1 var1 veps1 rstd1 xn1 bo_added xnT_mm xnT_cp q_mm q_biased q_high q_low qT_mm qT_cp score_mm masked maxed
            exped probsT_mm probsT_even probsT_odd pv_mm rsummed rsrowed rsT_mm rsT_cp oT_cp y_mm resid
            stat2 var2 veps2 rstd2s xn2s x2T_mm x2T_cp z_mm z_cp top_v top_i ixf_cp onehot both_cp
            prefix_mm selected ranked posf_cp idx_cp cummed scattered fb_added
            cnt_mm rt pairs_found led0 led1 tabled0 tabled1 exps wsteps
            r1 r1_mm r1_done
            xt_in0 xt_in1 xtT_mm xtT_cp g1_mm acted hided hidT_mm hidT_cp y2_mm yt_cp yt_out0 yt_out1
            gidx_cp gathered combined0 combined stored""".split() + [f"got{i}" for i in range(T1)]
        s = {n: sem(n) for n in names}
        block = ctx.enter_context(nc.Block())

        def wait_apart(eng, name, value):
            eng.wait_ge(s[name], value)
            eng.sem_inc(s["passed"], 1)

        def tile(i):
            return X[:, bass.ds(i, 1), :].rearrange("p a d -> p (a d)")

        def col(t, i):
            return t[:, bass.ds(i, 1), :].rearrange("p a d -> p (a d)")

        def token_tiles(eng, body):
            body(0)
            body(1)
            with eng.Fori(1, TB // 2) as p:
                body(2 * p, 0)
                body(2 * p + 1, 0)
            body(TB)
            body(TB + 1)
            with eng.Fori(TB // 2 + 1, NT // 2 - 1) as p:
                body(2 * p, 1)
                body(2 * p + 1, 1)
            for i in range(NT - 2, NT + 2):
                body(i)

        def there(i):
            return not isinstance(i, int) or 0 <= i < NT

        def batch(i, b):
            return i // TB if isinstance(i, int) else b

        def k_bank(b, n):
            return ((bA, bO)[b], bB)[n % 2]

        def bank2(L, i):
            return bS[0] if L == 0 and isinstance(i, int) and i == NT - 1 else bB

        def rows2(L, i):
            last = L == 0 and isinstance(i, int) and i == NT - 1
            return (xn, idx_last) if last else (xn2[:], idx)

        def later(value):
            return not isinstance(value, int) or value > 0

        def expert_tiles(eng, L, step):
            n = MT[L]
            for i in range(4):
                step(i, i % 2, i > 0, True)
            rest = n - 2 - n % 2
            with eng.Fori(4, rest, 2) as i:
                step(i, 0, True, True)
                step(i + 1, 1, True, True)
            for i in range(rest, n):
                step(i, i % 2, True, i < n - 1)

        def v_by_head(eng, ops, L, b, c):
            eng.wait_ge(s["vt_cp"], 2 * L + c + 1)
            if b == 0:
                if c == 1 and L == 1:
                    eng.wait_ge(s["y2_mm"], MT[0])
            else:
                eng.wait_ge(s["vblkT_mm"], (NB * L + 1) * NG)
            ops.tensor_tensor(probs[:, c, 0:HH * C].rearrange("p (h c) -> p h c", h=HH),
                              vT[:, c, b * C:(b + 1) * C].unsqueeze(1).broadcast_to((P, HH, C)),
                              m16[:].unsqueeze(2).broadcast_to((P, HH, C)), ALU.mult
                              ).then_inc(s[("vt_even", "vt_odd")[c]], 1)

        def masked(L, i):
            return L == 1 and isinstance(i, int) and i % TB < (C + P - 1) // P

        def nth(L, i, per=1, j=0):
            return (i + L * NT) * per + j + 1

        def nth2(L, i):
            return i + L * NT + 1

        def dma_th(L, i, u):
            return (i - u + L * MT[0]) * 8 + 16

        def results_out(eng, L):
            for u in range(2):
                eng.wait_ge(s[f"yt_out{u}"], dma_th(L, MT[L] - 1 - (MT[L] - 1 - u) % 2, u))

        def mth(L, i, per=1, j=0):
            return (i + L * MT[0]) * per + j + 1

        @block.sync
        def _(sp):
            sp.dma_start(ei[:], eidx).then_inc(s["eidx_in"], 16)
            sp.dma_start(cT[:], ctxt).then_inc(s["ctx_in"], 16)
            sp.dma_start(pack[:, 0:PACK1], pack0[:, 0:PACK1]).then_inc(s["packed"], 16)
            sp.dma_start(X[:, 0:1, :], x[:, 0:1, :]).then_inc(s["x_in"], 16)
            sp.dma_start(pack[:, PACK1:PACK], pack0[:, PACK1:PACK]).then_inc(s["packed2"], 16)
            sp.wait_ge(s["x_in"], 16)
            sp.dma_start(X[:, 1:NT, :], x[:, 1:NT, :]).then_inc(s["x_in"], 16)
            sp.dma_start(gw[:], gate).then_inc(s["gate_in"], 16)
            sp.dma_start(gb[:], gbias).then_inc(s["gate_in"], 16)
            sp.wait_ge(s["consts"], 18)
            for L in (0, 1):
                for e in range(EXP[L]):
                    sp.dma_start(xs[L][e * REG:e * REG + P, :], zero).then_inc(s["pad_done"], 16)
            sp.dma_start(wts[1][:], ewts).then_inc(s["route_in"], 16)
            sp.dma_start(fb[:], fbias).then_inc(s["route_in"], 16)

            def experts(L, lo, hi):
                n, first = (WE, UE)[L], (W13, U1)[L]
                for e in range(lo, hi):
                    sp.dma_start(arena[:, e * n:e * n + first], (w13, u1)[L][e]).then_inc(s[f"w_in{L}"], 16)
                    sp.dma_start(arena[:, e * n + first:(e + 1) * n], (w2, u2)[L][e]).then_inc(s[f"w_in{L}"], 16)

            experts(0, 0, EARLY[0])

            def ffn(L):
                if L == 0:
                    sp.wait_ge(s["pad_done"], 16 * (E0 + E1))
                sp.wait_ge(s["scattered"], 32 * (NT + L * T1))
                sp.wait_ge(s[f"led{L}"], 1)

                def load(i, u):
                    if later(mth(L, i) - 2):
                        sp.wait_ge(s["xtT_mm"], mth(L, i) - 2)
                    r = sp.value_load(tab[L][0:1, 1, bass.ds(i, 1)], min_val=0, max_val=EXP[L] * REG - P)
                    sp.dma_start(xt[:, u, :], xs[L][bass.ds(r, P), :]).then_inc(s[f"xt_in{u}"], 16)

                load(0, 0)
                sp.wait_ge(s[f"tabled{L}"], 1)

                def step(i, u, prev, nxt):
                    if nxt:
                        load(i + 1, 1 - u)
                    if isinstance(i, int) and EARLY[L] + i < EXP[L]:
                        experts(L, EARLY[L] + i, EARLY[L] + i + 1)

                expert_tiles(sp, L, step)

            sp.wait_ge(s["cnt_mm"], 1)
            ffn(0)
            sp.wait_ge(s["pairs_found"], 2)
            sp.dma_start(pack[:, 0:PACK1], pack1[:, 0:PACK1]).then_inc(s["packed"], 16)
            sp.dma_start(pack[:, PACK1:PACK], pack1[:, PACK1:PACK]).then_inc(s["packed2"], 16)
            for e in range(EARLY[1]):
                sp.wait_ge(s["gathered"], 32 * (e + 4))
                experts(1, e, e + 1)
            sp.wait_ge(s["y_mm"], 2 * NT)
            ffn(1)
            sp.wait_ge(s["fb_added"], NT)
            sp.dma_start(out[:, TB:NT, :], X[:, TB:NT, :]).then_inc(s["stored"], 16)
            for i in range(T1):
                sp.wait_ge(s["combined"], NT + i + 1)
                sp.dma_start(out[:, i:i + 1, :], X[:, i:i + 1, :]).then_inc(s["stored"], 16)
            sp.wait_ge(s["stored"], 16 * (T1 + 1))

        @block.gpsimd
        def _(gp):
            g = nc.gpsimd
            for t, v in ((ident, 0.0), (ustrict, 1.0), (ones, 1.0), (m16, 1.0), (m48, 1.0), (causal, 0.0),
                         (mhalf, -0.5), (zero, 0.0), (cum, 0.0), (cum1, 0.0)):
                g.memset(t if t is zero else t[:], v).then_inc(s["consts"], 1)
            g.iota(iota[:], [[1, 64]], base=0, channel_multiplier=0,
                   allow_small_or_imprecise_dtypes=True).then_inc(s["consts"], 1)
            gp.wait_ge(s["consts"], 11)

            def select(t, op, fill, base, pattern, cm):
                g.affine_select(out=t, in_=t, compare_op=op, fill=fill, base=base, pattern=pattern,
                                channel_multiplier=cm).then_inc(s["consts"], 1)

            select(ident[:], ALU.not_equal, 1.0, 0, [[-1, P]], 1)
            select(ustrict[:], ALU.is_gt, 0.0, 0, [[1, P]], -1)
            select(m16[:], ALU.is_ge, 0.0, 0, [[-DH, HH]], 1)
            select(causal[:], ALU.is_ge, NEG, 2 * P, [[-1, 2 * P + C]], 1)
            select(m48[:], ALU.is_ge, 0.0, 0, [[-PARTS * DH, HP]], 1)
            gp.wait_ge(s["consts"], 16)
            select(m16[:], ALU.is_ge, 0.0, DH - 1, [[DH, HH]], -1)
            select(m48[:], ALU.is_ge, 0.0, PARTS * DH - 1, [[PARTS * DH, HP]], -1)

            def attention(L):
                gp.wait_ge(s["packed"], 16 * (L + 1))

                def rsqrt1(i):
                    gp.wait_ge(s["veps1"], nth(L, i))
                    g.tensor_tensor(rstd[:], ve[:], mhalf[:], ALU.pow).then_inc(s["rstd1"], 1)

                def add_bo(i):
                    gp.wait_ge(s["xn1"], nth(L, i))
                    g.tensor_tensor(tile(i), tile(i), bo, ALU.add).then_inc(s["bo_added"], 1)

                def gather(i):
                    wait_apart(gp, "gidx_cp", i + 1)
                    for k in range(2):
                        g.indirect_dma_start(yg[:, k, :], None, ys[0],
                                             bass.IndirectOffsetOnAxis(ap=gidx[:, k:k + 1].bitcast(U32), axis=0)
                                             ).then_inc(s["gathered"], 16)

                def spread(i):
                    gp.wait_ge(s["rsummed"], nth(L, i))
                    if later(nth(L, i) - 1):
                        gp.wait_ge(s["rsT_mm"], nth(L, i) - 1)
                    g.tensor_tensor(rsrow.rearrange("p (h d) -> p h d", h=H), rrec[:].unsqueeze(2).broadcast_to((P, H, DH)),
                                    ones[:, 0:DH].unsqueeze(1).broadcast_to((P, H, DH)), ALU.mult
                                    ).then_inc(s["rsrowed"], 1)

                def q_low(i):
                    gp.wait_ge(s["q_high"], nth(L, i))
                    g.tensor_tensor(qhl[:, :, 2, :].bitcast(F32R), qf.rearrange("p (h d) -> p h d", h=H), qhl[:, :, 0, :],
                                    ALU.subtract).then_inc(s["q_low"], 1)

                def rsqrt2(i):
                    gp.wait_ge(s["veps2"], nth2(L, i))
                    g.tensor_tensor(rstd2[:], ve2[:], mhalf[:], ALU.pow).then_inc(s["rstd2s"], 1)

                def scatter(i):
                    gp.wait_ge(s["xn2s"], nth2(L, i))
                    wait_apart(gp, "idx_cp", nth2(L, i))
                    rows, places = rows2(L, i)
                    for k in range(2):
                        g.indirect_dma_start(xs[L], bass.IndirectOffsetOnAxis(ap=places[:, k:k + 1].bitcast(U32), axis=0),
                                             rows, None).then_inc(s["scattered"], 16)

                def add_fb(i, b):
                    if batch(i, b) == 1:
                        gp.wait_ge(s["resid"], nth(L, i))
                    g.tensor_tensor(tile(i), tile(i), fb[:], ALU.add).then_inc(s["fb_added"], 1)

                def k_low(b):
                    gp.wait_ge(s["k_high"], L * NB + b + 1)
                    for part, rows in ((0, P), (1, CL)):
                        m = g.tensor_tensor(khl[0:rows, part, :, 1, :].bitcast(F32R),
                                            kf[0:rows, b, part].rearrange("p (h d) -> p h d", h=H),
                                            khl[0:rows, part, :, 0, :], ALU.subtract)
                    m.then_inc(s["k_low"], 1)

                if L == 1:
                    gather(0)
                k_low(0)
                v_by_head(gp, g, L, 0, 1)
                rsqrt1(0)
                add_bo(0)
                v_by_head(gp, g, L, 1, 1)
                q_low(0)
                k_low(1)
                if L == 1:
                    gather(1)

                def body(i, b=None):
                    routed = there(i - 2) and (L == 0 or batch(i - 2, b) == 0)
                    if there(i + 1):
                        rsqrt1(i + 1)
                    if L == 1 and there(i + 2):
                        gather(i + 2)
                    if there(i + 1):
                        add_bo(i + 1)
                    if routed:
                        rsqrt2(i - 2)
                    if there(i + 1):
                        q_low(i + 1)
                    if there(i):
                        spread(i)
                    if routed:
                        scatter(i - 2)
                    if L == 1 and there(i - 2):
                        add_fb(i - 2, b)

                token_tiles(gp, body)

            def ffn(L):
                def step(i, u, prev, nxt):
                    wait_apart(gp, "yt_cp", mth(L, i))
                    gp.dma_start(ys[L][bass.ds(i * P, P), :], yt[:, u, :]).then_inc(s[f"yt_out{u}"], 16)

                expert_tiles(gp, L, step)

            attention(0)
            ffn(0)
            results_out(gp, 0)
            gp.wait_ge(s["route_in"], 32)
            attention(1)
            ffn(1)
            results_out(gp, 1)
            for i in range(T1):
                for k in range(2):
                    g.indirect_dma_start(yfin[:, i, k, :], None, ys[1],
                                         bass.IndirectOffsetOnAxis(ap=yp[1][:, i, k:k + 1].bitcast(U32), axis=0)
                                         ).then_inc(s[f"got{i}"], 16)

        @block.tensor
        def _(pe):
            t = nc.tensor

            def transpose(dst, src, n=P):
                return t.transpose(dst, src, ident[0:n, 0:n])

            pe.wait_ge(s["consts"], 18)

            def context(L):
                pe.wait_ge(s["packed"], 16 * (L + 1))
                pe.wait_ge(s["ctx_in"], 16)
                k_projected(0)
                for c in range(2):
                    for k in range(KC):
                        m = t.matmul((bO, bS[2])[c][:, 0:NB * C], wv[:, k, c * P:(c + 1) * P], cT[:, k, :],
                                     start=k == 0, stop=k == KC - 1)
                    m.then_inc(s["vt_mm"], 1)
                k_projected(1)

            def k_projected(b):
                for part in range(2):
                    lo, n = b * C + part * P, (P, CL)[part]
                    for k in range(KC):
                        m = t.matmul(bS[b][0:n, part * D:(part + 1) * D], cT[:, k, lo:lo + n], wk[:, k, :],
                                     start=k == 0, stop=k == KC - 1)
                m.then_inc(s["k_mm"], 1)

            def k_turned(L, b):
                pe.wait_ge(s["k_low"], L * NB + b + 1)
                for r in range(0, NS, KR):
                    n = (L * NB + b) * ROUNDS + r // KR
                    if n >= 2:
                        pe.wait_ge(s["kblked"], n - 1)
                    for j in range(r, min(r + KR, NS)):
                        for part, rows in ((0, P), (1, CL)):
                            at = (j - r) * C + part * P
                            m = transpose(k_bank(b, n)[0:PK, at:at + rows],
                                          khl[0:rows, part, HP * j:HP * j + HP].rearrange("p h r d -> p (h r d)"), rows)
                    m.then_inc(s["kT_mm"], 1)

            def v_turned(L, b):
                pe.wait_ge(s["vt_even"], L * NB + b + 1)
                for g in range(NG):
                    n = (L * NB + b) * NG + g
                    if (g + 1) * 4 > NW and g * 4 <= NW:
                        pe.wait_ge(s["vt_odd"], L * NB + b + 1)
                    if n >= 2:
                        pe.wait_ge(s["vblkT_cp"], n - 1)
                    turn(g, bT[n % 2]).then_inc(s["vblkT_mm"], 1)

            def turn(g, bank):
                for a in range(4):
                    w = 4 * g + a
                    m = transpose(bank[:, a * P:(a + 1) * P],
                                  probs[:, w // NW, (w % NW) * P:(w % NW + 1) * P])
                return m

            def route1():
                pe.wait_ge(s["r1"], 3 + T1)
                flat = both1[:].rearrange("p t e -> p (t e)")
                t.matmul(bB[:, 0:T1 * E1], ustrict[:], flat, start=True, stop=False)
                t.matmul(bB[:, 0:T1 * E1], ones[:], cum1[:, 0:T1, :].rearrange("p t e -> p (t e)"), start=False, stop=True)
                t.matmul(bB[:, 256:256 + E1], ones[:], cum1[:, T1, :], start=True, stop=True).then_inc(s["r1_mm"], 1)

            def attention(L):
                def norm_turned(i):
                    pe.wait_ge(s["xn1"], nth(L, i))
                    if later(nth(L, i) - 2):
                        pe.wait_ge(s["rsT_cp"], nth(L, i) - 2)
                    if later(nth(L, i) - 1):
                        pe.wait_ge(s["q_biased"], nth(L, i) - 1)
                    for k in range(KC):
                        m = transpose(bA[:, k * P:(k + 1) * P], xn[:, k * P:(k + 1) * P])
                    m.then_inc(s["xnT_mm"], 1)

                def queries(i):
                    pe.wait_ge(s["xnT_cp"], nth(L, i))
                    for k in range(KC):
                        m = t.matmul(bA[:, D:2 * D], xnT[:, k, :], wq[:, k, :], start=k == 0, stop=k == KC - 1)
                    m.then_inc(s["q_mm"], 1)

                def q_turned(i, half):
                    bank = (bS[2], bT[1])[half]
                    pe.wait_ge(s["q_low"], nth(L, i))
                    if half == 0 and later(nth(L, i, NS, 5) - NS):
                        pe.wait_ge(s["exped"], nth(L, i, NS, 5) - NS)
                    for a in range(4):
                        h = HP * (4 * half + a)
                        m = transpose(bank[0:PK, a * P:(a + 1) * P], qhl[:, h:h + HP].rearrange("p h r d -> p (h r d)"))
                    m.then_inc(s["qT_mm"], 1)

                def scores(i, j, b):
                    if j % 4 == 0:
                        pe.wait_ge(s["qT_cp"], nth(L, i, 2, j // 4))
                    before = nth(L, i, NS, j) - (2 if j < 2 else SB)
                    if j != 2 and later(before):
                        pe.wait_ge(s["exped"], before)
                    t.matmul(bS[j % SB][:, 0:HP * C], qT[:, j, :], kblk[:, b, j].rearrange("p h c -> p (h c)"),
                             start=True, stop=True).then_inc(s["score_mm"], 1)

                def probs_turned(i, g):
                    if g == 1 and there(i + 1):
                        pe.wait_ge(s["qT_cp"], nth(L, i + 1, 2, 1))
                    pe.wait_ge(s["exped"], nth(L, i, NS, last_step(g)))
                    turn(g, bT[g % 2]).then_inc(s["probsT_mm"], 1)

                def weigh(i, g, b):
                    if g % 2 == 0:
                        pe.wait_ge(s["probsT_even"], nth(L, i, 3, g // 2))
                    else:
                        pe.wait_ge(s["probsT_odd"], nth(L, i, 2, g // 2))
                    if g == 0 and later(nth(L, i) - 1):
                        pe.wait_ge(s["oT_cp"], nth(L, i) - 1)
                    for w in range(4 * g, 4 * g + 4):
                        m = t.matmul(oacc[:, w // NW, :], vblk[:, b, w, :], probsT[:, w, :],
                                     start=w % NW == 0, stop=w % NW == NW - 1)
                    if g == NG - 1:
                        m.then_inc(s["pv_mm"], 1)

                def sums_turned(i):
                    pe.wait_ge(s["rsrowed"], nth(L, i))
                    if not (isinstance(i, int) and i == NT - 1):
                        pe.wait_ge(s["q_biased"], nth(L, i) + 1)
                    for k in range(KC):
                        m = transpose(bA[:, k * P:(k + 1) * P], rsrow[:, k * P:(k + 1) * P])
                    m.then_inc(s["rsT_mm"], 1)

                def output(i):
                    pe.wait_ge(s["oT_cp"], nth(L, i))
                    if bank2(L, i) is bB and later(nth(L, i) - 1):
                        if L == 0:
                            pe.wait_ge(s["selected"], i)
                        else:
                            pe.wait_ge(s["resid"], nth(L, i) - 1)
                    for k in range(KC):
                        m = t.matmul(bank2(L, i)[:, D:2 * D], oT[:, k, :], wo[:, k, :], start=k == 0, stop=k == KC - 1)
                    m.then_inc(s["y_mm"], 1)

                def norm2_turned(i):
                    pe.wait_ge(s["xn2s"], nth2(L, i))
                    for k in range(KC):
                        m = transpose(bank2(L, i)[:, k * P:(k + 1) * P], rows2(L, i)[0][:, k * P:(k + 1) * P])
                    m.then_inc(s["x2T_mm"], 1)

                def gates(i):
                    pe.wait_ge(s["x2T_cp"], i + 1)
                    for k in range(KC):
                        m = t.matmul(bank2(L, i)[:, D:D + E0], x2T[:, k, :], gw[:, k, :], start=k == 0, stop=k == KC - 1)
                    m.then_inc(s["z_mm"], 1)

                def prefix(i):
                    pe.wait_ge(s["both_cp"], i + 1)
                    t.matmul(bank2(L, i)[:, 0:E0], ustrict[:], both[:], start=True, stop=False)
                    if later(i):
                        pe.wait_ge(s["cummed"], i)
                    t.matmul(bank2(L, i)[:, 0:E0], ones[:], cum[:], start=False, stop=True).then_inc(s["prefix_mm"], 1)

                def body(i, b=None):
                    here, prev, old, ahead = there(i), there(i - 1), there(i - 2), there(i + 1)
                    gated = old and L == 0
                    bs, bp = batch(i, b), batch(i - 1, b)
                    if isinstance(i, int) and i == 1:
                        pe.wait_ge(s["kblked"], (L + 1) * NB * ROUNDS)
                    if prev:
                        probs_turned(i - 1, 0)
                    if here:
                        scores(i, 0, bs)
                    if old:
                        output(i - 2)
                    if prev:
                        probs_turned(i - 1, 1)
                    if here:
                        scores(i, 1, bs)
                        scores(i, 2, bs)
                    if prev:
                        weigh(i - 1, 0, bp)
                        probs_turned(i - 1, 2)
                    if here:
                        scores(i, 3, bs)
                    if prev:
                        sums_turned(i - 1)
                        weigh(i - 1, 1, bp)
                    if ahead:
                        norm_turned(i + 1)
                    if prev:
                        probs_turned(i - 1, 3)
                    if here:
                        scores(i, 4, bs)
                        scores(i, 5, bs)
                    if ahead:
                        queries(i + 1)
                    if prev:
                        weigh(i - 1, 2, bp)
                    if gated and here:
                        norm2_turned(i - 2)
                    if prev:
                        probs_turned(i - 1, 4)
                    if here:
                        scores(i, 6, bs)
                        scores(i, 7, bs)
                    if gated and here:
                        gates(i - 2)
                    if prev:
                        weigh(i - 1, 3, bp)
                    if ahead:
                        q_turned(i + 1, 0)
                    if prev:
                        weigh(i - 1, 4, bp)
                    if ahead:
                        q_turned(i + 1, 1)
                    if gated:
                        if not here:
                            norm2_turned(i - 2)
                            gates(i - 2)
                        prefix(i - 2)
                    if isinstance(i, int) and i == 0:
                        k_turned(L, 1)

                k_turned(L, 0)
                v_turned(L, 0)
                pe.wait_ge(s["kblked"], (L * NB + 1) * ROUNDS)
                norm_turned(0)
                pe.wait_ge(s["packed2"], 16 * (L + 1))
                queries(0)
                pe.wait_ge(s["vt_cp"], 2 * (L + 1))
                pe.wait_ge(s["vblkT_cp"], (L * NB + 1) * NG)
                q_turned(0, 0)
                q_turned(0, 1)
                pe.wait_ge(s["qT_cp"], nth(L, 0, 2, 1))
                v_turned(L, 1)
                pe.wait_ge(s["vblkT_cp"], (L + 1) * NB * NG)
                if L == 0:
                    pe.wait_ge(s["gate_in"], 32)
                token_tiles(pe, body)
                if L == 0:
                    pe.wait_ge(s["cummed"], NT)
                    pe.wait_ge(s["rsT_cp"], NT)
                    t.matmul(bA[:, 0:E0], ones[:], cum[:], start=True, stop=True).then_inc(s["cnt_mm"], 1)

            def ffn(L):
                E, width, nk = EXP[L], (F0, F1)[L], (K0, K1)[L]
                base = (WE, UE)[L]
                second_at = (W13, U1)[L]

                def turn_x(i, u):
                    pe.wait_ge(s[f"xt_in{u}"], dma_th(L, i, u))
                    if later(mth(L, i) - 1):
                        pe.wait_ge(s["xtT_cp"], mth(L, i) - 1)
                    for k in range(KC):
                        m = transpose(mX[:, k * P:(k + 1) * P], xt[:, u, k * P:(k + 1) * P])
                    m.then_inc(s["xtT_mm"], 1)

                def first(i, u, e, half):
                    if half == 0:
                        pe.wait_ge(s["xtT_cp"], mth(L, i))
                    if L == 0:
                        if later(i):
                            pe.wait_ge(s["hided"], 2 * i - 1 + half)
                        for w in range(2):
                            for k in range(KC):
                                m = t.matmul(mG[2 * half + w][:, 0:HALF0], xtT[:, u, k, :],
                                             arena[:, bass.ds(e * base + (w * KC + k) * F0 + half * HALF0, HALF0)],
                                             start=k == 0, stop=k == KC - 1)
                    else:
                        if not isinstance(i, int) or i >= 2:
                            pe.wait_ge(s["acted"], 2 * MT[0] + 2 * i - 3 + half)
                        for k in range(KC):
                            m = t.matmul(mG[2 * u + half][:], xtT[:, u, k, :],
                                         arena[:, bass.ds(e * base + k * F1 + half * 512, 512)],
                                         start=k == 0, stop=k == KC - 1)
                    m.then_inc(s["g1_mm"], 1)

                def turn_h(i):
                    if L == 0:
                        pe.wait_ge(s["hided"], 2 * i + 2)
                    else:
                        pe.wait_ge(s["acted"], 2 * MT[0] + 2 * i + 2)
                    for g in range(2):
                        if later(mth(L, i, 2, g) - 2):
                            pe.wait_ge(s["hidT_cp"], mth(L, i, 2, g) - 2)
                        for c in range(4 * g, min(4 * g + 4, nk)):
                            n = min(P, width - c * P)
                            m = transpose(mT[g][0:n, (c - 4 * g) * P:(c - 4 * g + 1) * P], hid[:, c * P:c * P + n])
                        m.then_inc(s["hidT_mm"], 1)

                def second(i, e):
                    if later(mth(L, i) - 1):
                        pe.wait_ge(s["yt_cp"], mth(L, i) - 1)
                    for c in range(nk):
                        if c % 4 == 0:
                            pe.wait_ge(s["hidT_cp"], mth(L, i, 2, c // 4))
                        n = min(P, width - c * P)
                        m = t.matmul(mY[:, 0:D], hidT[0:n, c * P:(c + 1) * P],
                                     arena[0:n, bass.ds(e * base + second_at + c * D, D)],
                                     start=c == 0, stop=c == nk - 1)
                    m.then_inc(s["y2_mm"], 1)

                def expert(i):
                    if isinstance(i, int) and i == 0:
                        return 0
                    if isinstance(i, int) and i == 1:
                        pe.wait_ge(s[f"tabled{L}"], 1)
                    return pe.value_load(tab[L][0:1, 0, bass.ds(i, 1)], min_val=0, max_val=E - 1)

                pe.wait_ge(s[f"led{L}"], 1)
                pe.wait_ge(s[f"w_in{L}"], EARLY[L] * 32)
                turn_x(0, 0)

                def step(i, u, prev, nxt):
                    if nxt:
                        turn_x(i + 1, 1 - u)
                    e = expert(i)
                    first(i, u, e, 0)
                    if prev:
                        turn_h(i - 1)
                    first(i, u, e, 1)
                    if prev:
                        if isinstance(i, int) and i == 3:
                            pe.wait_ge(s[f"w_in{L}"], EXP[L] * 32)
                        second(i - 1, expert(i - 1))

                expert_tiles(pe, L, step)
                turn_h(MT[L] - 1)
                second(MT[L] - 1, expert(MT[L] - 1))

            route1()
            context(0)
            pe.wait_ge(s["r1_done"], 1)
            attention(0)
            ffn(0)
            pe.wait_ge(s["yt_cp"], MT[0])
            context(1)
            attention(1)
            pe.wait_ge(s["resid"], 2 * NT)
            ffn(1)

        @block.scalar
        def _(ac):
            a = nc.scalar

            def attention(L):
                def xnT_out(i):
                    ac.wait_ge(s["xnT_mm"], nth(L, i))
                    a.copy(xnT.rearrange("p k n -> p (k n)"), bA[:, 0:D]).then_inc(s["xnT_cp"], 1)

                def q_high(i):
                    ac.wait_ge(s["q_biased"], nth(L, i))
                    if later(nth(L, i, 2) - 1):
                        ac.wait_ge(s["qT_mm"], nth(L, i, 2) - 1)
                    a.copy(qhl[:, :, 0:2, :].bitcast(F32R), qf.rearrange("p (h d) -> p h d", h=H).unsqueeze(2)
                           .broadcast_to((P, H, 2, DH))).then_inc(s["q_high"], 1)

                def qT_out(i, half):
                    ac.wait_ge(s["qT_mm"], nth(L, i, 2, half))
                    if later(nth(L, i, NS) - 1):
                        ac.wait_ge(s["score_mm"], nth(L, i, NS) - 1)
                    a.copy(qT[:, 4 * half:4 * half + 4].rearrange("p j n -> p (j n)"), (bS[2], bT[1])[half][0:PK]
                           ).then_inc(s["qT_cp"], 1)

                def exponent(i, j):
                    ac.wait_ge(s["maxed"], nth(L, i, NS, j))
                    if j == 0 and later(nth(L, i) - 1):
                        ac.wait_ge(s["rsummed"], nth(L, i) - 1)
                    for k in range(HP):
                        h = HP * j + k
                        dst = probs[:, h // HH, h % HH * C:(h % HH + 1) * C]
                        src = dst if masked(L, i) else bS[j % SB][:, k * C:(k + 1) * C]
                        m = a.activation(dst, src, ACT.Exp, bias=nmax[:, h:h + 1], accum_out=rsum[:, h:h + 1])
                    m.then_inc(s["exped"], 1)

                def probs_out(i, g):
                    ac.wait_ge(s["probsT_mm"], nth(L, i, NG, g))
                    a.copy(probsT[:, 4 * g:4 * g + 4, :].rearrange("p w n -> p (w n)"), bT[g % 2][:]
                           ).then_inc(s["probsT_even"], 1)

                def rsT_out(i):
                    ac.wait_ge(s["rsT_mm"], nth(L, i))
                    if later(nth(L, i) - 1):
                        ac.wait_ge(s["oT_cp"], nth(L, i) - 1)
                    a.copy(rsT.rearrange("p k n -> p (k n)"), bA[:, 0:D]).then_inc(s["rsT_cp"], 1)

                def x2T_out(i):
                    ac.wait_ge(s["x2T_mm"], nth2(L, i))
                    a.copy(x2T.rearrange("p k n -> p (k n)"), bank2(L, i)[:, 0:D]).then_inc(s["x2T_cp"], 1)

                def body(i, b=None):
                    here, prev, old, ahead = there(i), there(i - 1), there(i - 2), there(i + 1)
                    if prev:
                        probs_out(i - 1, 0)
                    if here:
                        exponent(i, 0)
                        exponent(i, 1)
                    if prev:
                        probs_out(i - 1, 2)
                        rsT_out(i - 1)
                    if here:
                        exponent(i, 2)
                    if ahead:
                        xnT_out(i + 1)
                    if here:
                        exponent(i, 3)
                        exponent(i, 4)
                    if old and here and L == 0:
                        x2T_out(i - 2)
                    if ahead:
                        q_high(i + 1)
                    if here:
                        exponent(i, 5)
                    if prev:
                        probs_out(i - 1, 4)
                    if here:
                        exponent(i, 6)
                    if ahead:
                        qT_out(i + 1, 0)
                    if here:
                        exponent(i, 7)
                    if ahead:
                        qT_out(i + 1, 1)
                    if old and not here and L == 0:
                        x2T_out(i - 2)

                def k_high(b):
                    ac.wait_ge(s["kfed"], L * NB + b + 1)
                    if b == 1:
                        ac.wait_ge(s["kT_mm"], (L * NB + 1) * ROUNDS)
                    for part, rows in ((0, P), (1, CL)):
                        src = kf[0:rows, b, part].rearrange("p (h d) -> p h d", h=H)
                        for r in (0, 2):
                            m = a.copy(khl[0:rows, part, :, r, :].bitcast(F32R), src)
                    m.then_inc(s["k_high"], 1)

                def v_out(b):
                    for n in range((L * NB + b) * NG, (L * NB + b + 1) * NG):
                        ac.wait_ge(s["vblkT_mm"], n + 1)
                        g = n % NG
                        a.copy(vblk[:, b, 4 * g:4 * g + 4, :].rearrange("p w d -> p (w d)"), bT[n % 2][:]
                               ).then_inc(s["vblkT_cp"], 1)

                a.activation(warm[:], mhalf[:], ACT.Exp)
                ac.wait_ge(s["packed"], 16 * (L + 1))
                k_high(0)
                for c in range(2):
                    ac.wait_ge(s["vt_mm"], 2 * L + c + 1)
                    a.activation(vT[:, c], (bO, bS[2])[c][:, 0:NB * C], ACT.Identity, bias=bv[:, c:c + 1]
                                 ).then_inc(s["vt_cp"], 1)
                v_out(0)
                xnT_out(0)
                k_high(1)
                q_high(0)
                qT_out(0, 0)
                qT_out(0, 1)
                v_out(1)
                token_tiles(ac, body)
                if L == 0:
                    ac.wait_ge(s["top_v"], 2 * NT)
                    a.activation(wts[0][:], mxs[:], ACT.Exp, scale=-1.0).then_inc(s["exps"], 1)

            def ffn(L):
                def turned(i, u):
                    ac.wait_ge(s["xtT_mm"], mth(L, i))
                    if later(mth(L, i, 2, 1) - 4):
                        ac.wait_ge(s["g1_mm"], mth(L, i, 2, 1) - 4)
                    a.copy(xtT[:, u].rearrange("p k n -> p (k n)"), mX[:, 0:D]).then_inc(s["xtT_cp"], 1)

                def activate(i, u):
                    for half in range(2):
                        ac.wait_ge(s["g1_mm"], mth(L, i, 2, half))
                        if later(mth(L, i, 2, half) - 2):
                            ac.wait_ge(s["hidT_mm"], mth(L, i, 2, half) - 2)
                        if L == 0:
                            m = a.activation(hid[:, half * HALF0:(half + 1) * HALF0], mG[2 * half][:, 0:HALF0], ACT.Silu)
                        else:
                            m = a.activation(hid[:, half * 512:(half + 1) * 512], mG[2 * u + half][:], ACT.Gelu)
                        m.then_inc(s["acted"], 1)

                def hidden_out(i):
                    for g in range(2):
                        ac.wait_ge(s["hidT_mm"], mth(L, i, 2, g))
                        if later(mth(L, i) - 1):
                            ac.wait_ge(s["y2_mm"], mth(L, i) - 1)
                        if L == 0 and g == 1:
                            a.copy(hidT[:, 4 * P:5 * P], mT[1][:, 0:P])
                            n = F0 - (K0 - 1) * P
                            m = a.copy(hidT[0:n, 5 * P:6 * P], mT[1][0:n, P:2 * P])
                        else:
                            m = a.copy(hidT[:, 4 * g * P:(4 * g + 4) * P], mT[g][:])
                        m.then_inc(s["hidT_cp"], 1)

                a.activation(warm[:], mhalf[:], (ACT.Silu, ACT.Gelu)[L])
                turned(0, 0)

                def step(i, u, prev, nxt):
                    if nxt:
                        turned(i + 1, 1 - u)
                    if prev:
                        hidden_out(i - 1)
                    activate(i, u)

                expert_tiles(ac, L, step)
                hidden_out(MT[L] - 1)

            ac.wait_ge(s["consts"], 18)
            attention(0)
            ffn(0)
            attention(1)
            ffn(1)

        @block.vector
        def _(dv):
            v = nc.vector

            def inc(ins, name):
                ins.then_inc(s[name], 1)

            def step_on(ins, name, counts):
                counts[name] = counts.get(name, 0) + 1
                ins.then_inc(s[name], 1)
                dv.wait_ge(s[name], counts[name])

            counts = {}

            def context(L):
                dv.wait_ge(s["packed"], 16 * (L + 1))
                step_on(v.tensor_scalar(bq, bq, SCALE, None, ALU.mult), "q_bias_scaled", counts)
                v.memset(probs[:, :, HH * C:HW], 0.0)

            def k_bias(L, b):
                dv.wait_ge(s["k_mm"], NB * L + b + 1)
                for part, rows in ((0, P), (1, CL)):
                    m = v.tensor_tensor(kf[0:rows, b, part], bS[b][0:rows, part * D:(part + 1) * D], bk[0:rows], ALU.add)
                inc(m, "kfed")

            def k_by_pair(L, b):
                for r in range(0, NS, KR):
                    n = (L * NB + b) * ROUNDS + r // KR
                    dv.wait_ge(s["kT_mm"], n + 1)
                    k = min(KR, NS - r)
                    src = k_bank(b, n)[0:PK, 0:k * C].rearrange("p (j c) -> p j c", j=k)
                    inc(v.tensor_tensor(kblk[:, b, r:r + k], src.unsqueeze(2).broadcast_to((PK, k, HP, C)),
                                        m48[0:PK].unsqueeze(1).unsqueeze(3).broadcast_to((PK, k, HP, C)), ALU.mult),
                        "kblked")

            def route1():
                dv.wait_ge(s["eidx_in"], 16)
                step_on(v.tensor_copy(eif[:], ei[:]), "r1", counts)
                step_on(v.tensor_tensor(oh[1][:].rearrange("p t k e -> p (t k) e"),
                                        eif[:].rearrange("p t k -> p (t k)").unsqueeze(2).broadcast_to((P, 2 * T1, E1)),
                                        iota[:, 0:E1].unsqueeze(1).broadcast_to((P, 2 * T1, E1)), ALU.is_equal), "r1", counts)
                step_on(v.tensor_tensor(both1[:], oh[1][:, :, 0], oh[1][:, :, 1], ALU.add), "r1", counts)
                for i in range(T1):
                    step_on(v.tensor_tensor(cum1[:, i + 1], cum1[:, i], both1[:, i], ALU.add), "r1", counts)
                dv.wait_ge(s["r1_mm"], 1)
                v.tensor_copy(cnt1[:], bB[:, 256:256 + E1])
                step_on(v.tensor_copy(pref[:].rearrange("p t e -> p (t e)"), bB[:, 0:T1 * E1]), "r1_done", counts)
                for k in range(2):
                    tmp = xn2[:, 0:T1 * E1].rearrange("p (t e) -> p t e", e=E1)
                    step_on(v.tensor_tensor(tmp, oh[1][:, :, k], pref[:], ALU.mult), "r1", counts)
                    step_on(v.tensor_reduce(rank[1][:, :, k], tmp, AX.X, ALU.add), "r1", counts)
                    if k == 0:
                        step_on(v.tensor_tensor(pref[:], pref[:], oh[1][:, :, 0], ALU.add), "r1", counts)
                step_on(v.scalar_tensor_tensor(out=pos1f[:], in0=eif[:], scalar=float(REG), in1=rank[1][:],
                                               op0=ALU.mult, op1=ALU.add), "r1", counts)
                step_on(v.tensor_scalar(pos1[:], pos1f[:], float(P), None, ALU.add), "r1", counts)

            def tables(L, cnt):
                E, n, w = EXP[L], MT[L], (NT, T1)[L]
                go = lambda m: step_on(m, "rt", counts)
                go(v.tensor_scalar(cnti[:, 0:E], cnt, 1.0, float(P - 1), ALU.max, ALU.add))
                go(v.tensor_scalar(cnti[:, 0:E], cnti[:, 0:E], 7, None, ALU.arith_shift_right))
                go(v.tensor_copy(ntf[:, 0:E], cnti[:, 0:E]))
                go(v.tensor_tensor_scan(incl[:, 0:E], ones[:, 0:E], ntf[:, 0:E], 0.0, ALU.mult, ALU.add))
                go(v.scalar_tensor_tensor(out=first[:, 0:E], in0=incl[:, 0:E], scalar=float(P), in1=cnt,
                                          op0=ALU.mult, op1=ALU.subtract))
                inc(v.tensor_scalar(tab[L][0:1, 1, 0:1], first[0:1, 0:1], -1.0, float(P), ALU.mult, ALU.add), f"led{L}")
                go(v.tensor_tensor(skip[0:1, 0:E - 1], first[0:1, 0:E - 1], first[0:1, 1:E], ALU.subtract))
                go(v.tensor_scalar(skip[0:1, 0:E - 1], skip[0:1, 0:E - 1], float(REG), None, ALU.add))
                g = ge[0:1, 0:n, 0:E]
                go(v.tensor_tensor(g, iota[0:1, 0:n].unsqueeze(2).broadcast_to((1, n, E)),
                                   incl[0:1, 0:E].unsqueeze(1).broadcast_to((1, n, E)), ALU.is_ge))
                go(v.tensor_reduce(tv[0:1, 0, 0:n], g, AX.X, ALU.add))
                g = ge[0:1, 0:n, 0:E - 1]
                go(v.tensor_tensor(g, g, skip[0:1, 0:E - 1].unsqueeze(1).broadcast_to((1, n, E - 1)), ALU.mult))
                go(v.tensor_reduce(tv[0:1, 1, 0:n], g, AX.X, ALU.add))
                go(v.tensor_scalar(tv[0:1, 2, 0:n], iota[0:1, 1:n + 1], float(P), first[0:1, 0:1], ALU.mult, ALU.subtract))
                go(v.tensor_tensor(tv[0:1, 1, 0:n], tv[0:1, 1, 0:n], tv[0:1, 2, 0:n], ALU.add))
                go(v.tensor_scalar(tv[0:1, 3, 0:n], tv[0:1, 0, 0:n], float(E), None, ALU.is_lt))
                go(v.tensor_tensor(tv[0:1, 0:2, 0:n], tv[0:1, 0:2, 0:n],
                                   tv[0:1, 3, 0:n].unsqueeze(1).broadcast_to((1, 2, n)), ALU.mult))
                inc(v.tensor_copy(tab[L][0:1, :, 1:n], tv[0:1, 0:2, 1:n]), f"tabled{L}")
                tmp = sel2[:, 0:w * 2 * E].rearrange("p (t e) -> p t e", e=E)
                go(v.tensor_tensor(tmp, oh[L][:].rearrange("p t k e -> p (t k) e"),
                                   first[:, 0:E].unsqueeze(1).broadcast_to((P, 2 * w, E)), ALU.mult))
                go(v.tensor_reduce(ypf[:, 0:w, :].rearrange("p t k -> p (t k)"), tmp, AX.X, ALU.add))
                go(v.tensor_tensor(ypf[:, 0:w, :], ypf[:, 0:w, :], rank[L][:], ALU.add))
                step_on(v.tensor_copy(yp[L][:], ypf[:, 0:w, :]), "pairs_found", counts)

            def attention(L):
                def norm1a(i):
                    if L == 1:
                        wait_apart(dv, "combined", i + 1)
                    inc(v.bn_stats(stats[:], tile(i)), "stat1")

                def norm1b(i):
                    wait_apart(dv, "stat1", nth(L, i))
                    inc(v.bn_aggr(mv[:], stats[:]), "var1")

                def norm1c(i):
                    dv.wait_ge(s["var1"], nth(L, i))
                    inc(v.tensor_scalar(ve[:], mv[:, 1:2], EPS, None, ALU.add), "veps1")

                def scale1(i):
                    dv.wait_ge(s["rstd1"], nth(L, i))
                    if later(nth(L, i) - 1):
                        dv.wait_ge(s["xnT_mm"], nth(L, i) - 1)
                    inc(v.tensor_scalar(xn, tile(i), mv[:, 0:1], rstd[:, 0:1], ALU.subtract, ALU.mult), "xn1")

                def combine(i):
                    dv.wait_ge(s["gathered"], nth(0, i, 32, 31))
                    inc(v.scalar_tensor_tensor(out=tile(i), in0=yg[:, 0, :], scalar=wcol(0, i, 0), in1=tile(i),
                                               op0=ALU.mult, op1=ALU.add), "combined0")
                    dv.wait_ge(s["combined0"], i + 1)
                    inc(v.scalar_tensor_tensor(out=tile(i), in0=yg[:, 1, :], scalar=wcol(0, i, 1), in1=tile(i),
                                               op0=ALU.mult, op1=ALU.add), "combined")

                def q_bias(i):
                    dv.wait_ge(s["q_mm"], nth(L, i))
                    if later(nth(L, i) - 1):
                        dv.wait_ge(s["q_low"], nth(L, i) - 1)
                    inc(v.scalar_tensor_tensor(out=qf, in0=bA[:, D:2 * D], scalar=SCALE, in1=bq, op0=ALU.mult, op1=ALU.add),
                        "q_biased")

                def peak(i, j):
                    h = HP * j
                    dv.wait_ge(s["score_mm"], nth(L, i, NS, j))
                    src = bS[j % SB][:, 0:HP * C].rearrange("p (h c) -> p h c", h=HP)
                    if masked(L, i):
                        at, o = h % HH * C, 2 * P - i % TB * P
                        dst = probs[:, h // HH, at:at + HP * C].rearrange("p (h c) -> p h c", h=HP)
                        step_on(v.tensor_tensor(dst, src, causal[:, o:o + C].unsqueeze(1).broadcast_to((P, HP, C)),
                                                ALU.add), "masked", counts)
                        src = dst
                    inc(v.tensor_reduce(nmax[:, h:h + HP], src, AX.X, ALU.max, negate=True), "maxed")

                def probs_out(i, g):
                    dv.wait_ge(s["probsT_mm"], nth(L, i, NG, g))
                    inc(v.tensor_copy(probsT[:, 4 * g:4 * g + 4, :].rearrange("p w n -> p (w n)"), bT[g % 2][:]),
                        "probsT_odd")

                def reciprocals(i):
                    dv.wait_ge(s["exped"], nth(L, i, NS, NS - 1))
                    if later(nth(L, i) - 1):
                        dv.wait_ge(s["rsrowed"], nth(L, i) - 1)
                    inc(v.reciprocal(rrec[:], rsum[:]), "rsummed")

                def normalise(i):
                    dv.wait_ge(s["rsT_cp"], nth(L, i))
                    dv.wait_ge(s["pv_mm"], nth(L, i))
                    inc(v.tensor_tensor(oT, oacc, rsT, ALU.mult), "oT_cp")

                def residual(i):
                    dv.wait_ge(s["y_mm"], nth(L, i))
                    dv.wait_ge(s["bo_added"], nth(L, i))
                    inc(v.tensor_tensor(tile(i), tile(i), bank2(L, i)[:, D:2 * D], ALU.add), "resid")

                def norm2a(i):
                    wait_apart(dv, "resid", nth(L, i))
                    inc(v.bn_stats(stats2[:], tile(i)), "stat2")

                def norm2b(i):
                    wait_apart(dv, "stat2", nth2(L, i))
                    inc(v.bn_aggr(mv2[:], stats2[:]), "var2")

                def norm2c(i):
                    dv.wait_ge(s["var2"], nth2(L, i))
                    inc(v.tensor_scalar(ve2[:], mv2[:, 1:2], EPS, None, ALU.add), "veps2")

                def scale2(i):
                    dv.wait_ge(s["rstd2s"], nth2(L, i))
                    if bank2(L, i) is bB and later(nth2(L, i) - 1):
                        dv.wait_ge(s["scattered"], nth2(L, i) * 32 - 32)
                    if L == 0 and later(i):
                        dv.wait_ge(s["x2T_mm"], i)
                    inc(v.tensor_scalar(rows2(L, i)[0], tile(i), mv2[:, 0:1], rstd2[:, 0:1], ALU.subtract, ALU.mult), "xn2s")
                    if L == 1:
                        inc(v.tensor_copy(idx[:], col(pos1, i)), "idx_cp")

                def gate(i):
                    dv.wait_ge(s["z_mm"], i + 1)
                    if later(i):
                        dv.wait_ge(s["top_i"], i)
                    inc(v.tensor_tensor(z[:], bank2(L, i)[:, D:D + E0], gb[:], ALU.add), "z_cp")

                def best(i):
                    wait_apart(dv, "z_cp", i + 1)
                    inc(v.max(mx[:], z[:]), "top_v")
                    wait_apart(dv, "top_v", 2 * i + 1)
                    inc(v.max_index(ix[:], mx[:], z[:]), "top_i")
                    inc(v.tensor_copy(col(mxs, i), mx[:, 0:2]), "top_v")

                def choose(i):
                    dv.wait_ge(s["top_i"], i + 1)
                    inc(v.tensor_copy(ixf[:], ix[:, 0:2]), "ixf_cp")
                    dv.wait_ge(s["ixf_cp"], i + 1)
                    inc(v.tensor_tensor(oh[0][:, bass.ds(i, 1)].rearrange("p a k e -> p (a k) e"),
                                        iota[:, 0:E0].unsqueeze(1).broadcast_to((P, 2, E0)),
                                        ixf[:].unsqueeze(2).broadcast_to((P, 2, E0)), ALU.is_equal), "onehot")
                    dv.wait_ge(s["onehot"], i + 1)
                    if later(i):
                        dv.wait_ge(s["cummed"], i)
                    o = oh[0][:, bass.ds(i, 1)].rearrange("p a k e -> p (a k) e")
                    inc(v.tensor_tensor(both[:], o[:, 0], o[:, 1], ALU.add), "both_cp")

                def place(i):
                    dv.wait_ge(s["prefix_mm"], i + 1)
                    o = oh[0][:, bass.ds(i, 1)].rearrange("p a k e -> p (a k) e")
                    inc(v.tensor_tensor(sel[:], o, bank2(L, i)[:, 0:E0].unsqueeze(1).broadcast_to((P, 2, E0)), ALU.mult), "selected")
                    inc(v.tensor_tensor(cum[:], cum[:], both[:], ALU.add), "cummed")
                    dv.wait_ge(s["selected"], i + 1)
                    inc(v.tensor_reduce(col(rank[0], i), sel[:], AX.X, ALU.add), "ranked")
                    dv.wait_ge(s["ranked"], i + 1)
                    inc(v.scalar_tensor_tensor(out=posf[:], in0=ixf[:], scalar=float(REG), in1=col(rank[0], i),
                                               op0=ALU.mult, op1=ALU.add), "posf_cp")
                    dv.wait_ge(s["posf_cp"], i + 1)
                    inc(v.tensor_scalar(rows2(L, i)[1][:], posf[:], float(P), None, ALU.add), "idx_cp")

                def next_gather(i):
                    inc(v.tensor_copy(gidx[:], col(yp[0], i)), "gidx_cp")

                def body(i, b=None):
                    here, prev, old, ahead = there(i), there(i - 1), there(i - 2), there(i + 1)
                    gated = old and L == 0
                    routed = gated or old and batch(i - 2, b) == 0
                    if ahead:
                        norm1a(i + 1)
                    if L == 1 and there(i + 2):
                        next_gather(i + 2)
                    if here:
                        peak(i, 0)
                    if ahead:
                        norm1b(i + 1)
                    if here:
                        peak(i, 1)
                    if prev:
                        probs_out(i - 1, 1)
                    if ahead:
                        norm1c(i + 1)
                    if here:
                        peak(i, 2)
                    if old:
                        residual(i - 2)
                    if ahead:
                        scale1(i + 1)
                    if routed:
                        norm2a(i - 2)
                    if here:
                        peak(i, 3)
                    if routed:
                        norm2b(i - 2)
                        norm2c(i - 2)
                    if gated:
                        scale2(i - 2)
                    if here:
                        peak(i, 4)
                    if prev:
                        probs_out(i - 1, 3)
                    if ahead:
                        q_bias(i + 1)
                    if here:
                        peak(i, 5)
                    if prev and not here:
                        normalise(i - 1)
                    if here:
                        peak(i, 6)
                    if gated:
                        gate(i - 2)
                    if here:
                        peak(i, 7)
                    if gated:
                        best(i - 2)
                        choose(i - 2)
                    if L == 1 and routed:
                        scale2(i - 2)
                    if L == 1 and there(i + 2):
                        combine(i + 2)
                    if prev and here:
                        normalise(i - 1)
                    if here:
                        reciprocals(i)
                    if gated:
                        place(i - 2)
                    if here and isinstance(i, int) and i == 0:
                        k_by_pair(L, 1)

                if L == 1:
                    next_gather(0)
                context(L)
                k_bias(L, 0)
                v_by_head(dv, v, L, 0, 0)
                k_bias(L, 1)
                k_by_pair(L, 0)
                if L == 0:
                    dv.wait_ge(s["x_in"], 16)
                if L == 1:
                    combine(0)
                    next_gather(1)
                norm1a(0)
                norm1b(0)
                norm1c(0)
                scale1(0)
                v_by_head(dv, v, L, 1, 0)
                q_bias(0)
                if L == 1:
                    combine(1)
                if L == 0:
                    dv.wait_ge(s["x_in"], 32)
                token_tiles(dv, body)

            def wcol(L, i, k):
                return wts[L][:, bass.ds(i, 1), k:k + 1].rearrange("p a d -> p (a d)")

            def ffn(L):
                def gate_hidden(i):
                    for half in range(2):
                        dv.wait_ge(s["acted"], 2 * i + half + 1)
                        lo = half * HALF0
                        inc(v.tensor_tensor(hid[:, lo:lo + HALF0], hid[:, lo:lo + HALF0], mG[2 * half + 1][:, 0:HALF0],
                                            ALU.mult), "hided")

                def result(i, u):
                    dv.wait_ge(s["y2_mm"], mth(L, i))
                    if later(dma_th(L, i, u) - 16):
                        dv.wait_ge(s[f"yt_out{u}"], dma_th(L, i, u) - 16)
                    inc(v.tensor_copy(yt[:, u, :], mY[:, 0:D]), "yt_cp")

                def step(i, u, prev, nxt):
                    if L == 0:
                        gate_hidden(i)
                    if prev:
                        result(i - 1, 1 - u)
                    if L == 0 and isinstance(i, int) and i == 1:
                        tables(1, cnt1[:])

                expert_tiles(dv, L, step)
                result(MT[L] - 1, (MT[L] - 1) % 2)

            dv.wait_ge(s["consts"], 18)
            route1()
            attention(0)
            dv.wait_ge(s["cnt_mm"], 1)
            tables(0, bA[:, 0:E0])
            dv.wait_ge(s["exps"], 1)
            go = lambda m: step_on(m, "wsteps", counts)
            w = wts[0]
            go(v.tensor_scalar(w[:], w[:], 1.0, None, ALU.add))
            go(v.reciprocal(w[:], w[:]))
            go(v.tensor_tensor(wsum[:], w[:, :, 0], w[:, :, 1], ALU.add))
            go(v.tensor_scalar(wsum[:], wsum[:], 1e-20, None, ALU.add))
            go(v.reciprocal(wsum[:], wsum[:]))
            go(v.tensor_tensor(w[:], w[:], wsum[:].unsqueeze(2).broadcast_to((P, NT, 2)), ALU.mult))
            ffn(0)
            attention(1)
            ffn(1)
            dv.wait_ge(s["fb_added"], NT)
            for i in range(T1):
                dv.wait_ge(s[f"got{i}"], 32)
                inc(v.scalar_tensor_tensor(out=X[:, i], in0=yfin[:, i, 0, :], scalar=wts[1][:, i, 0:1], in1=X[:, i],
                                           op0=ALU.mult, op1=ALU.add), "combined0")
                dv.wait_ge(s["combined0"], NT + i + 1)
                inc(v.scalar_tensor_tensor(out=X[:, i], in0=yfin[:, i, 1, :], scalar=wts[1][:, i, 1:2], in1=X[:, i],
                                           op0=ALU.mult, op1=ALU.add), "combined")


def kernel(**inputs):
    import numpy as np
    import concourse.bacc as bacc
    from concourse.bass_utils import run_bass_kernel_spmd as run

    a = {k: np.ascontiguousarray(v) for k, v in inputs.items()}

    def cols(w):
        k, n = w.shape
        pad = -k % P
        if pad:
            w = np.concatenate([w, np.zeros((pad, n), w.dtype)])
        return w.reshape(-1, P, n).transpose(1, 0, 2).reshape(P, -1)

    def rows(v):
        return np.broadcast_to(v, (P, v.shape[0]))

    def packed(L):
        g = lambda n: a[f"L{L}_xattn_{n}"]
        return np.ascontiguousarray(np.concatenate(
            [cols(g(n).T) for n in ("Wk", "Wv")] + [g("bv").reshape(KC, P).T] + [rows(g(n)) for n in ("bq", "bk", "bo")]
            + [cols(g(n).T) for n in ("Wo", "Wq")], axis=1))

    def experts(n):
        return np.concatenate([a[f"L0_ffn_{n}"], a[f"L0_ffn_new_{n}"]])

    w1, w2, w3 = (experts(n) for n in ("w1", "w2", "w3"))
    gates = np.concatenate([a["L0_ffn_gate_weight"], a["L0_ffn_new_gate_weight"]])
    gbias = np.concatenate([np.zeros(E0 - 1, np.float32), a["L0_ffn_gate_bias"]])
    data = {
        "x": a["x"].reshape(NT, P, D).transpose(1, 0, 2),
        "ctxt": cols(a["ctx_1024"].reshape(NB * C, D).T).reshape(P, KC, NB * C),
        "pack0": packed(0),
        "pack1": packed(1),
        "w13": np.stack([np.concatenate([cols(w1[e].T), cols(w3[e].T)], axis=1) for e in range(E0)]),
        "w2": np.stack([cols(w2[e].T) for e in range(E0)]),
        "gate": cols(gates.T).reshape(P, KC, E0),
        "gbias": rows(gbias),
        "u1": np.stack([cols(a["L1_ffn_w1"][e]) for e in range(E1)]),
        "u2": np.stack([cols(a["L1_ffn_w2"][e]) for e in range(E1)]),
        "eidx": a["L1_ffn_expert_indices"].reshape(T1, P, 2).transpose(1, 0, 2),
        "ewts": a["L1_ffn_expert_weights"].reshape(T1, P, 2).transpose(1, 0, 2),
        "fbias": rows(a["L1_ffn_bias"]),
    }
    data = {k: np.ascontiguousarray(v) for k, v in data.items()}
    nc = bacc.Bacc("TRN2", target_bir_lowering=False, num_devices=1)
    args = [nc.dram_tensor(f"in_{k}", v.shape, mybir.dt.from_np(v.dtype), kind="ExternalInput").ap()
            for k, v in data.items()]
    out = nc.dram_tensor("out_0", (P, NT, D), F32, kind="ExternalOutput").ap()
    program(nc, *args, out)
    r = run(nc, [{f"in_{k}": v for k, v in data.items()}], core_ids=[0])
    return r.results[0]["out_0"].transpose(1, 0, 2).reshape(NB, SEQ, D)
```
